# Optimizing a Trainium2 kernel written in Bass

```python
import numpy as np
import jax
import jax.numpy as jnp

def _softmax(x, axis=-1):
    return jax.nn.softmax(x, axis=axis)

def _gelu(x):
    return jax.nn.gelu(x, approximate=True)

def _silu(x):
    return jax.nn.silu(x)

def _sigmoid(x):
    return jax.nn.sigmoid(x)

def _layernorm(x, axis=-1, eps=1e-05):
    m = jnp.mean(x, axis=axis, keepdims=True)
    v = jnp.var(x, axis=axis, keepdims=True)
    return (x - m) / jnp.sqrt(v + eps)

def _scatter_add(tgt, idx, src, axis=0):
    return tgt.at[idx].add(src)

def _segment_sum(src, seg, n):
    return jax.ops.segment_sum(src, seg, n)
kernel_name = 'mk_adaln_ffn_d1_seqx_r4_f9f5dc'

def setup_inputs(seed: int=0):
    np.random.seed(seed)
    _w = jnp.asarray

    def _rec_inputs():
        import jax
        import jax.numpy as jnp
        _rk = jax.random.key(seed)
        x = -0.0003929 + 0.9999 * jax.random.normal(jax.random.fold_in(_rk, 1), (64, 64, 1024), jnp.float32)
        _lenS = 64 - jax.random.randint(jax.random.fold_in(_rk, 7), (64,), 0, max(1, 64 // 4) + 1, jnp.int32)
        _lenS2 = 64 - jax.random.randint(jax.random.fold_in(_rk, 8), (64,), 0, max(1, 64 // 4) + 1, jnp.int32)
        itok_B_8_3872 = jax.random.randint(jax.random.fold_in(_rk, 11), (64,), 8, 3873, jnp.int32)
        return (x, itok_B_8_3872)
    x, itok_B_8_3872 = _rec_inputs()

    def _L0_cond_setup():
        import math
        import jax, jax.numpy as jnp
        import numpy as np
        H, N, B, L = (64, 64, 16, 1024)
        DT_MIN, DT_MAX = (0.001, 0.1)

        def _get_kernel(log_dt, C, log_A_real, A_imag, length):
            Cc = C[..., 0] + 1j * C[..., 1]
            dt = jnp.exp(log_dt)
            A = -jnp.exp(log_A_real) + 1j * A_imag
            dtA = A * dt[:, None]
            P = dtA[:, :, None] * jnp.arange(length, dtype=jnp.float32)
            Cs = Cc * (jnp.exp(dtA) - 1.0) / A
            K = 2.0 * jnp.einsum('hn,hnl->hl', Cs, jnp.exp(P)).real
            return K
        key = jax.random.key(seed)
        ks = jax.random.split(key, 6)
        u = jax.random.normal(ks[0], (B, H, L), dtype=jnp.float32)
        length = jax.random.randint(ks[1], (B,), 0, L)
        log_dt = jax.random.uniform(ks[2], (H,), dtype=jnp.float32) * (math.log(DT_MAX) - math.log(DT_MIN)) + math.log(DT_MIN)
        C = jax.random.normal(ks[3], (H, N, 2), dtype=jnp.float32)
        log_A_real = jnp.log(0.5 * jnp.ones((H, N), dtype=jnp.float32))
        A_imag = math.pi * jnp.broadcast_to(jnp.arange(N, dtype=jnp.float32), (H, N))
        D = jax.random.normal(ks[4], (H,), dtype=jnp.float32)
        return {'u': u, 'length': length, 'log_dt': log_dt, 'C': C, 'log_A_real': log_A_real, 'A_imag': A_imag, 'D': D}
    _L0_cond_all = _L0_cond_setup()
    _L0_cond_in = {k: v for k, v in _L0_cond_all.items() if k in ('log_dt', 'C', 'log_A_real', 'A_imag', 'D')}
    del _L0_cond_all

    def _L0_ffn_setup():
        import jax, jax.numpy as jnp
        import numpy as np
        HID, INT, LAT, NE, K = (1024, 2048, 512, 8, 2)
        LN_EPS = 1e-05

        def _layernorm(x, gamma, beta):
            mu = jnp.mean(x, axis=-1, keepdims=True)
            var = jnp.var(x, axis=-1, keepdims=True)
            return (x - mu) * jax.lax.rsqrt(var + LN_EPS) * gamma + beta
        key = jax.random.key(seed)
        ks = jax.random.split(key, 8)
        s = lambda d: 1.0 / np.sqrt(d)
        return {'hidden_states': jax.random.normal(ks[0], (4, 512, HID), jnp.float32), 'gate_w': jax.random.normal(ks[1], (HID, NE), jnp.float32) * s(HID), 'up_w': jax.random.normal(ks[2], (HID, INT), jnp.float32) * s(HID), 'down_w': jax.random.normal(ks[3], (INT, HID), jnp.float32) * s(INT), 'fc1_w': jax.random.normal(ks[4], (HID, LAT), jnp.float32) * s(HID), 'fc2_w': jax.random.normal(ks[5], (LAT, HID), jnp.float32) * s(LAT), 'expert_w': jax.random.normal(ks[6], (LAT, LAT), jnp.float32), 'ln_gamma': jnp.ones((HID,), jnp.float32), 'ln_beta': jnp.zeros((HID,), jnp.float32)}
    _L0_ffn_all = _L0_ffn_setup()
    _L0_ffn_in = {k: v for k, v in _L0_ffn_all.items() if k in ('gate_w', 'up_w', 'down_w', 'fc1_w', 'fc2_w', 'expert_w', 'ln_gamma', 'ln_beta')}
    del _L0_ffn_all
    return {'x': x, 'itok_B_8_3872': itok_B_8_3872, 'L0_cond_log_dt': _L0_cond_in['log_dt'], 'L0_cond_C': _L0_cond_in['C'], 'L0_cond_log_A_real': _L0_cond_in['log_A_real'], 'L0_cond_A_imag': _L0_cond_in['A_imag'], 'L0_cond_D': _L0_cond_in['D'], 'L0_ffn_gate_w': _L0_ffn_in['gate_w'], 'L0_ffn_up_w': _L0_ffn_in['up_w'], 'L0_ffn_down_w': _L0_ffn_in['down_w'], 'L0_ffn_fc1_w': _L0_ffn_in['fc1_w'], 'L0_ffn_fc2_w': _L0_ffn_in['fc2_w'], 'L0_ffn_expert_w': _L0_ffn_in['expert_w'], 'L0_ffn_ln_gamma': _L0_ffn_in['ln_gamma'], 'L0_ffn_ln_beta': _L0_ffn_in['ln_beta']}

def reference(x, itok_B_8_3872, L0_cond_log_dt, L0_cond_C, L0_cond_log_A_real, L0_cond_A_imag, L0_cond_D, L0_ffn_gate_w, L0_ffn_up_w, L0_ffn_down_w, L0_ffn_fc1_w, L0_ffn_fc2_w, L0_ffn_expert_w, L0_ffn_ln_gamma, L0_ffn_ln_beta):
    import jax
    import jax.numpy as jnp

    def _L0_cond_ref(u, length, log_dt, C, log_A_real, A_imag, D):
        import math
        import jax, jax.numpy as jnp
        import numpy as np
        H, N, B, L = (64, 64, 16, 1024)
        DT_MIN, DT_MAX = (0.001, 0.1)

        def _get_kernel(log_dt, C, log_A_real, A_imag, length):
            Cc = C[..., 0] + 1j * C[..., 1]
            dt = jnp.exp(log_dt)
            A = -jnp.exp(log_A_real) + 1j * A_imag
            dtA = A * dt[:, None]
            P = dtA[:, :, None] * jnp.arange(length, dtype=jnp.float32)
            Cs = Cc * (jnp.exp(dtA) - 1.0) / A
            K = 2.0 * jnp.einsum('hn,hnl->hl', Cs, jnp.exp(P)).real
            return K
        Bq, Hq, Lq = u.shape
        mask = (jnp.arange(Lq) < length[:, None]).astype(u.dtype)
        u_m = u * mask[:, None, :]
        kernel = _get_kernel(log_dt, C, log_A_real, A_imag, Lq)
        n = 2 * Lq
        k_f = jnp.fft.rfft(kernel, n=n)
        u_f = jnp.fft.rfft(u_m, n=n)
        y = jnp.fft.irfft(u_f * k_f, n=n)[..., :Lq]
        y = y + u_m * D[:, None]
        return y * mask[:, None, :]

    def _L0_ffn_ref(hidden_states, gate_w, up_w, down_w, fc1_w, fc2_w, expert_w, ln_gamma, ln_beta):
        import jax, jax.numpy as jnp
        import numpy as np
        HID, INT, LAT, NE, K = (1024, 2048, 512, 8, 2)
        LN_EPS = 1e-05

        def _layernorm(x, gamma, beta):
            mu = jnp.mean(x, axis=-1, keepdims=True)
            var = jnp.var(x, axis=-1, keepdims=True)
            return (x - mu) * jax.lax.rsqrt(var + LN_EPS) * gamma + beta
        logits = jnp.einsum('bsh,he->bse', hidden_states, gate_w)
        routing_weights, selected_experts = jax.lax.top_k(logits, K)
        h = jax.nn.relu(jnp.einsum('bsh,hi->bsi', hidden_states, up_w)) ** 2
        shared_out = jnp.einsum('bsi,ih->bsh', h, down_w)
        x_latent = jnp.einsum('bsh,hl->bsl', hidden_states, fc1_w)
        expert_out = jnp.einsum('bsl,lm->bsm', x_latent, expert_w)
        moe_out = expert_out * jnp.sum(routing_weights, axis=-1, keepdims=True)
        routed_out = jnp.einsum('bsl,lh->bsh', moe_out, fc2_w)
        return _layernorm(shared_out + routed_out, ln_gamma, ln_beta)
    x = x + _L0_ffn_ref(_L0_cond_ref(x, itok_B_8_3872, L0_cond_log_dt, L0_cond_C, L0_cond_log_A_real, L0_cond_A_imag, L0_cond_D), L0_ffn_gate_w, L0_ffn_up_w, L0_ffn_down_w, L0_ffn_fc1_w, L0_ffn_fc2_w, L0_ffn_expert_w, L0_ffn_ln_gamma, L0_ffn_ln_beta)
    return x

_drawn_inputs = setup_inputs


def setup_inputs(seed=0):
    import zlib

    import numpy as np

    out = dict(_drawn_inputs(seed))
    spreads = {'L0_cond_log_A_real': (-0.6931471824645996, 0.2),
     'L0_ffn_ln_gamma': (1.0, 0.2),
     'L0_ffn_ln_beta': (0.0, 0.1)}
    factors = {}
    for name, (base, spread) in spreads.items():
        noise = np.random.default_rng([zlib.crc32(name.encode()), seed]).standard_normal(out[name].shape)
        drawn = base * np.exp(spread * noise) if base else spread * noise
        out[name] = jnp.asarray(drawn.astype(out[name].dtype))
    for name, factor in factors.items():
        out[name] = (out[name] * factor).astype(out[name].dtype)
    return out
```

```python
import math
from contextlib import ExitStack

import concourse.bass as bass
from concourse import mybir

F32 = mybir.dt.float32
F16 = mybir.dt.float16
BF16 = mybir.dt.bfloat16
I32 = mybir.dt.int32
I16 = mybir.dt.int16
ALU = mybir.AluOpType
ACT = mybir.ActivationFunctionType
AX = mybir.AxisListType

P = 128
B, H, L = 64, 64, 1024
N = 64
INT, LAT, NE = 2048, 512, 8
KT = L // P
CI = INT // P
CL = LAT // P
NC = CI + CL
PAIRS = H // 2
TILES = PAIRS // 2
LN_EPS = 1e-5
R = 32
KPAD = P + L

FC2_0, W1_0, UP_0, DN_0 = 0, CL, CL + 4, CL + 4 + 2 * KT
PIECES = DN_0 + CI
MAGIC = 1.5 * 2.0 ** 23
TWO_PI = 6.2831850
EXP_MASK = 0x7F800000
TINY = 2.0 ** -40


class Chain:

    def __init__(self, eng, sem):
        self.eng, self.sem, self.count, self.turn, self.per = eng, sem, 0, 0, 0

    def loop(self, turn, per):
        self.start, self.turn, self.per = self.count, turn, per

    def end_loop(self, turns):
        assert self.count - self.start == self.per
        self.count, self.turn = self.start + self.per * turns, 0

    def link(self, ins):
        ins.then_inc(self.sem, 1)
        self.count += 1
        self.eng.wait_ge(self.sem, self.count + self.turn * self.per)


def build(nc, x, itok, log_dt, C, log_A_real, A_imag, D, gate_w, up_w, down_w, fc1_w, fc2_w, expert_w,
          ln_gamma, ln_beta, out):
    k_dram = nc.dram_tensor("k_padded", (2, H, KPAD), F16)
    hid_dram = nc.dram_tensor("hidden_pairs", (PAIRS, P, 2, KT, P), F16)

    with ExitStack() as top:
        def sb(name, shape, dt, stack=top):
            return stack.enter_context(nc.sbuf_tensor(name, shape, dt))

        W = sb("weights", [P, PIECES + 1, 2 * L], F16)
        gate = sb("gate", [P, KT, 2 * NE], F16)
        id16 = sb("id16", [P, P], F16)
        id32 = sb("id32", [P, P], F32)
        ones32 = sb("ones32", [P, P], F32)
        pair_scale = sb("pair_scale", [P, PAIRS], F32)
        rho = sb("rho", [P, PAIRS], F32)
        scales = sb("scales", [P, 8], F32)
        s_up, s_w1, s_gate, s_down, s_fc2 = (scales[:, k:k + 1] for k in range(5))

        def raw(slot, n=1):
            return W[:, slot:slot + n, :].bitcast(F32)

        prepare(nc, W, raw, gate, id16, id32, ones32, pair_scale, s_up, s_w1, s_gate, s_fc2, k_dram,
                log_dt, C, log_A_real, A_imag, D, gate_w, up_w, down_w, fc1_w,
                fc2_w, expert_w)
        conv(nc, W, raw, id16, ones32, pair_scale, rho, s_up, s_down, k_dram, hid_dram, x, itok, down_w)
        ffn(nc, W, raw, gate, id32, ones32, rho, scales, hid_dram, x, ln_gamma, ln_beta, out)


def start_at_one(eng, *sems):
    for s in sems:
        eng.sem_inc(s, 1)


def first(t):
    return isinstance(t, int) and t == 0


def power_scale(dve, link, dst, src, target):
    link(dve.tensor_scalar(dst, src, TINY, None, ALU.max))
    link(dve.tensor_scalar(dst.bitcast(I32), dst.bitcast(I32), EXP_MASK, None, ALU.bitwise_and))
    link(dve.reciprocal(dst, dst))
    link(dve.tensor_scalar(dst, dst, target, None, ALU.mult))


def prepare(nc, W, raw, gate, id16, id32, ones32, pair_scale, s_up, s_w1, s_gate, s_fc2, k_dram,
            log_dt, C, log_A_real, A_imag, D, gate_w, up_w, down_w, fc1_w, fc2_w, expert_w):
    with ExitStack() as ctx:
        def sb(name, shape, dt):
            return ctx.enter_context(nc.sbuf_tensor(name, shape, dt))

        def psum(name, shape, dt=F32):
            return ctx.enter_context(nc.psum_tensor(name, shape, dt))

        def sem(name):
            return ctx.enter_context(nc.semaphore(name))

        S0 = DN_0 + 1
        fc1_sb = raw(S0, 4).rearrange("p s (k m) -> p (s k) m", m=LAT)
        fc1T = raw(S0 + 4, 4)
        expert_sb = raw(S0 + 8, 2).rearrange("p s (k m) -> p (s k) m", m=LAT)
        small = raw(S0 + 10, 3).rearrange("p s m -> p (s m)")
        up_abs = W[:, S0 + 13, :].bitcast(BF16).rearrange("p (b m) -> p b m", b=2)
        w1_abs = W[:, S0 + 14, 0:2 * LAT].bitcast(BF16).rearrange("p (b m) -> p b m", b=2)
        kpad0 = W[:, S0 + 14, 2 * LAT:2 * LAT + P]

        big = [sb(f"table{k}", [P, H, R], F32) for k in range(5)]
        count = sb("count", [P, R], F32)
        ones16 = sb("ones16", [P, P], BF16)
        half = sb("half", [P, 1], F32)
        d_row = sb("d_row", [1, H], F32)
        z_cols = sb("z_cols", [P, 4, H], F32)

        nxt = [0]

        def cut(n):
            nxt[0] += n
            return small[0:H, nxt[0] - n:nxt[0]]

        logs, C_sb, aim = cut(N + 1), cut(2 * N), cut(N)
        t0, t1, t2, ex, q, p2 = (cut(N + 1) for _ in range(6))
        alpha, w_im, turns, fhalf, sin_w, sin_h = (cut(N) for _ in range(6))
        e_re, e_im, inv, f_re, f_im, s_re, s_im, u0, u1 = (cut(N) for _ in range(9))
        z_rows = cut(4 * P).rearrange("p (z s) -> p z s", z=4)
        kf = big[1][0:R, :, :]
        abs_sum = big[2][0:R, :, 0]
        k_sc = big[3][0:R, :, :]
        k_hi = big[4][0:R, :, :].bitcast(F16)[:, :, 0:R]
        k_lo = big[4][0:R, :, :].bitcast(F16)[:, :, R:2 * R]
        nxt_g = small[:, nxt[0]:nxt[0] + 512]
        gate_raw = nxt_g[:, 0:64].rearrange("p (k e) -> p k e", e=NE)
        gate_abs = nxt_g[:, 64:128]
        gate_sum = nxt_g[:, 128:136]
        gate_hl = nxt_g[:, 136:137]
        fc2_max = nxt_g[:, 137:138]
        sk = nxt_g[:, 192:256]
        bound = nxt_g[:, 256:260]

        up_sum = psum("up_sum", [P, 4, 512])
        ring = psum("ring", [P, 2, 512])
        w1_sum = psum("w1_sum", [P, 512])
        misc = psum("misc", [P, 512])
        z_ps, gate_ps = misc[:, 0:4 * H].rearrange("p (z h) -> p z h", z=4), misc[:, 256:320]
        fc2_ps, sk_ps = misc[:, 320:321], misc[:, 384:448]

        fc1_in, expert_in, cond_in, gate_in, fc2_in = map(sem, ("fc1_in", "expert_in", "cond_in", "gate_in", "fc2_in"))
        up_in = [sem(f"up_in{k}") for k in range(4)]
        consts, consts_a = sem("consts"), sem("consts_a")
        dve_c = sem("dve_chain")
        sines_asked, sines_done, z_ready, z_turned = map(sem, ("sines_asked", "sines_done", "z_ready", "z_turned"))
        ring_full, ring_free = sem("ring_full"), sem("ring_free")
        w1_abs_ready, w1_abs_used, w1_summed = map(sem, ("w1_abs_ready", "w1_abs_used", "w1_summed"))
        up_abs_ready, up_abs_used = sem("up_abs_ready"), sem("up_abs_used")
        table_asked, table_done, tables = map(sem, ("table_asked", "table_done", "tables"))
        sums_in, sums_out, k_ready, k_scaled, k_split, k_out = map(
            sem, ("sums_in", "sums_out", "k_ready", "k_scaled", "k_split", "k_out"))
        w_scaled, piece_hi, piece_lo, gate_scaled, gate_hi = map(
            sem, ("w_scaled", "piece_hi", "piece_lo", "gate_scaled", "gate_hi"))
        pad_ready, down_in = sem("pad_ready"), sem("down_early")

        block = ctx.enter_context(nc.Block())

        @block.sync
        def _(sp):
            sp.dma_start(fc1_sb, fc1_w.rearrange("(c p) m -> p c m", p=P)).then_inc(fc1_in, 16)
            sp.dma_start(expert_sb, expert_w.rearrange("(c p) m -> p c m", p=P)).then_inc(expert_in, 16)
            sp.dma_start(raw(FC2_0 + 1, CL), fc2_w.rearrange("(c p) m -> p c m", p=P)).then_inc(fc2_in, 16)
            for k in range(4):
                sp.dma_start(raw(UP_0 + 1 + 4 * k, 4).rearrange("p (c s) m -> p c (s m)", s=2),
                             up_w.rearrange("(c p) m -> p c m", p=P)[:, 2 * k:2 * k + 2, :]).then_inc(up_in[k], 16)
            sp.wait_ge(ring_full, 16)
            sp.dma_start(raw(DN_0 + 1, 10), down_w.rearrange("(c p) m -> p c m", p=P)[:, 0:10, :]).then_inc(down_in, 16)
            sp.wait_ge(pad_ready, 1)
            for part in range(2):
                sp.dma_start(k_dram.ap()[part, :, 0:P], kpad0[0:H, :]).then_inc(k_out, 16)
            sp.wait_ge(k_split, 2)
            for part, k in enumerate((k_hi, k_lo)):
                sp.dma_start(bass.AP(k_dram, part * H * KPAD + P, [[R, R], [KPAD, H], [1, R]]), k).then_inc(k_out, 16)
            sp.wait_ge(k_out, 64)
            sp.wait_ge(down_in, 16)

        @block.gpsimd
        def _(pool):
            pool.memset(id32[:, :], 0.0).then_inc(consts, 1)
            pool.wait_ge(consts, 1)
            pool.affine_select(out=id32[:, :], in_=id32[:, :], compare_op=ALU.not_equal, fill=1.0, base=0,
                               pattern=[[-1, P]], channel_multiplier=1).then_inc(consts, 1)
            pool.memset(ones32[:, :], 1.0).then_inc(consts, 1)
            pool.memset(ones16[:, :], 1.0).then_inc(consts, 1)
            pool.wait_ge(consts, 2)
            pool.tensor_copy(id16[:, :], id32[:, :]).then_inc(consts, 1)
            pool.iota(count[:, :], pattern=[[1, R]], base=0, channel_multiplier=0,
                      allow_small_or_imprecise_dtypes=True).then_inc(consts_a, 1)
            pool.memset(kpad0, 0.0).then_inc(pad_ready, 1)

        @block.scalar
        def _(act):
            act.dma_start(logs[:, 0:N], log_A_real).then_inc(cond_in, 16)
            act.dma_start(logs[:, N:N + 1], log_dt.rearrange("(h o) -> h o", o=1)).then_inc(cond_in, 16)
            act.dma_start(C_sb, C.rearrange("h n c -> h (n c)")).then_inc(cond_in, 16)
            act.dma_start(aim, A_imag).then_inc(cond_in, 16)
            act.dma_start(d_row[:, :], D.rearrange("(o h) -> o h", o=1)).then_inc(cond_in, 16)
            act.dma_start(gate_raw, gate_w.rearrange("(c p) e -> p c e", p=P)).then_inc(gate_in, 16)
            act.wait_ge(sines_asked, 1)
            act.activation(sin_w, turns, ACT.Sin, scale=TWO_PI).then_inc(sines_done, 1)
            act.activation(sin_h, fhalf, ACT.Sin, scale=TWO_PI).then_inc(sines_done, 1)
            for u in range(8):
                act.wait_ge(ring_full, u + 1)
                act.activation(fc1T[:, u // 2, u % 2 * 512:u % 2 * 512 + 512], ring[:, u % 2, :],
                               ACT.Copy).then_inc(ring_free, 1)

            def table(n, func, t, scale=1.0):
                act.wait_ge(table_asked, n)
                act.activation(t[:, :, :], t[:, :, :], func, scale=scale).then_inc(table_done, 1)

            def up_abs_piece(j):
                if j % 4 == 0:
                    act.wait_ge(up_in[j // 4], 16)
                if j >= 2:
                    act.wait_ge(up_abs_used, j - 1)
                act.activation(up_abs[:, j % 2, :], raw(UP_0 + 1 + j)[:, 0, :], ACT.Abs).then_inc(up_abs_ready, 1)

            for k in range(KT):
                u = 8 + k
                act.wait_ge(ring_full, u + 1)
                if k >= 2:
                    act.wait_ge(w1_abs_used, k - 1)
                act.activation(w1_abs[:, k % 2, :], ring[:, u % 2, :], ACT.Abs).then_inc(w1_abs_ready, 1)
                act.activation(raw(W1_0 + 1 + k // 2)[:, 0, k % 2 * 512:k % 2 * 512 + 512], ring[:, u % 2, :],
                               ACT.Copy).then_inc(ring_free, 1)
                up_abs_piece(2 * k)
                up_abs_piece(2 * k + 1)
            table(1, ACT.Sin, big[0], TWO_PI)
            table(2, ACT.Exp, big[1])
            table(3, ACT.Sin, big[3], TWO_PI)
            table(4, ACT.Sin, big[4], TWO_PI)
            table(5, ACT.Exp, big[2])
            for g in range(4):
                u = 16 + g
                act.wait_ge(ring_full, u + 1)
                act.activation(kf[:, 16 * g:16 * g + 16, :], ring[0:R, u % 2, :].rearrange("p (h r) -> p h r", r=R),
                               ACT.Copy).then_inc(ring_free, 1)
            for j in range(UP_0):
                act.wait_ge(w_scaled, 1 if j < W1_0 else 2)
                if j:
                    act.wait_ge(piece_lo, j)
                act.activation(W[:, j, 0:L], raw(j + 1)[:, 0, :], ACT.Copy,
                               scale=s_fc2 if j < W1_0 else s_w1).then_inc(piece_hi, 1)
            act.wait_ge(gate_scaled, 1)
            act.activation(gate[:, :, 0:NE], gate_raw, ACT.Copy, scale=s_gate).then_inc(gate_hi, 1)
            act.wait_ge(k_scaled, 1)
            act.activation(k_hi, k_sc, ACT.Copy).then_inc(k_split, 1)

        @block.tensor
        def _(pe):
            pe.wait_ge(consts, 5)
            pe.wait_ge(fc1_in, 16)
            for u in range(8):
                if u >= 2:
                    pe.wait_ge(ring_free, u - 1)
                for k in range(4):
                    c = u % 2 * 4 + k
                    ins = pe.transpose(ring[:, u % 2, k * P:k * P + P], fc1_sb[:, c, u // 2 * P:u // 2 * P + P], id32[:, :])
                ins.then_inc(ring_full, 1)
            pe.wait_ge(z_ready, 1)
            for z in range(4):
                ins = pe.transpose(z_ps[:, z, :], z_rows[:, z, :], id32[0:H, 0:H])
            ins.then_inc(z_turned, 1)
            pe.wait_ge(expert_in, 16)
            pe.wait_ge(ring_free, 8)

            def w1_colsum(k):
                pe.wait_ge(w1_abs_ready, k + 1)
                pe.matmul(w1_sum[:, :], ones16[:, :], w1_abs[:, k % 2, :], start=(k == 0),
                          stop=(k == KT - 1)).then_inc(w1_abs_used, 1)

            def up_colsum(j):
                pe.wait_ge(up_abs_ready, j + 1)
                for k in range(2):
                    ins = pe.matmul(up_sum[:, j % 2 * 2 + k, :], ones16[:, :], up_abs[:, j % 2, k * 512:k * 512 + 512],
                                    start=(j < 2), stop=(j >= 2 * KT - 2))
                ins.then_inc(up_abs_used, 1)

            def colsums(k):
                w1_colsum(k)
                up_colsum(2 * k)
                up_colsum(2 * k + 1)

            for k in range(KT):
                u = 8 + k
                pe.wait_ge(ring_free, u - 1)
                for c in range(CL):
                    ins = pe.matmul(ring[:, u % 2, :], fc1T[:, c, k * P:k * P + P], expert_sb[:, c, :],
                                    start=(c == 0), stop=(c == CL - 1))
                ins.then_inc(ring_full, 1)
                if k:
                    colsums(k - 1)
            colsums(KT - 1)
            pe.wait_ge(sums_in, 2)
            pe.matmul(fc2_ps, ones32[:, :], fc2_max, start=True, stop=True)
            pe.matmul(gate_ps, ones32[:, :], gate_abs, start=True, stop=True).then_inc(sums_out, 1)
            pe.wait_ge(tables, 2)
            for g in range(4):
                u = 16 + g
                pe.wait_ge(ring_free, u - 1)
                for k in range(16):
                    h = 16 * g + k
                    ins = pe.matmul(ring[0:R, u % 2, k * R:k * R + R], big[3][:, h, :], big[0][:, h, :],
                                    start=True, stop=True)
                ins.then_inc(ring_full, 1)
            pe.wait_ge(sums_in, 3)
            pe.matmul(sk_ps, ones32[0:R, :], abs_sum, start=True, stop=True).then_inc(sums_out, 1)

        @block.vector
        def _(dve):
            chain = Chain(dve, dve_c)
            link = chain.link

            def expm1_parts(v, n):
                a, b, c, qq, pp = t0[:, 0:n], t1[:, 0:n], t2[:, 0:n], q[:, 0:n], p2[:, 0:n]
                link(dve.tensor_scalar(a, v, 1.0 / math.log(2.0), MAGIC, ALU.mult, ALU.add))
                link(dve.tensor_scalar(a, a, MAGIC, None, ALU.subtract))
                link(dve.scalar_tensor_tensor(out=b, in0=a, scalar=-0.693359375, in1=v, op0=ALU.mult, op1=ALU.add))
                link(dve.scalar_tensor_tensor(out=b, in0=a, scalar=2.12194440e-4, in1=b, op0=ALU.mult, op1=ALU.add))
                link(dve.tensor_scalar(qq, b, 1.0 / math.factorial(8), None, ALU.mult))
                for k in range(7, 0, -1):
                    link(dve.scalar_tensor_tensor(out=qq, in0=qq, scalar=1.0 / math.factorial(k), in1=b,
                                                  op0=ALU.add, op1=ALU.mult))
                link(dve.tensor_scalar(a, a, -126.0, 127.0, ALU.max, ALU.min))
                link(dve.tensor_scalar(pp.bitcast(I32), a, 127.0, 2.0 ** 23, ALU.add, ALU.mult))
                link(dve.tensor_tensor(c, pp, qq, ALU.mult))
                return c, pp

            def tt(o, a, b, op):
                link(dve.tensor_tensor(o, a, b, op))

            def to_fraction(o, a, k):
                link(dve.tensor_scalar(k, a, MAGIC, MAGIC, ALU.add, ALU.subtract))
                tt(o, a, k, ALU.subtract)

            dve.wait_ge(cond_in, 80)
            c, pp = expm1_parts(logs, N + 1)
            tt(ex, c, pp, ALU.add)
            ea, dt = ex[:, 0:N], ex[:, N:N + 1]
            link(dve.tensor_scalar(alpha, ea, dt, -1.0, ALU.mult, ALU.mult))
            link(dve.tensor_scalar(w_im, aim, dt, None, ALU.mult))
            link(dve.tensor_scalar(u0, w_im, 1.0 / (2.0 * math.pi), None, ALU.mult))
            to_fraction(turns, u0, u1)
            link(dve.tensor_scalar(u0, w_im, 1.0 / (4.0 * math.pi), None, ALU.mult))
            link(dve.tensor_scalar(u1, u0, MAGIC, MAGIC, ALU.add, ALU.subtract))
            dve.tensor_tensor(fhalf, u0, u1, ALU.subtract).then_inc(sines_asked, 1)
            c, pp = expm1_parts(alpha, N)
            link(dve.scalar_tensor_tensor(out=s_re, in0=pp, scalar=-1.0, in1=c, op0=ALU.add, op1=ALU.add))
            tt(s_im, c, pp, ALU.add)
            dve.wait_ge(sines_done, 2)
            tt(e_im, s_im, sin_w, ALU.mult)
            tt(u0, s_im, sin_h, ALU.mult)
            tt(u0, u0, sin_h, ALU.mult)
            link(dve.scalar_tensor_tensor(out=e_re, in0=u0, scalar=-2.0, in1=s_re, op0=ALU.mult, op1=ALU.add))
            tt(u0, ea, ea, ALU.mult)
            tt(u1, aim, aim, ALU.mult)
            tt(u0, u0, u1, ALU.add)
            link(dve.reciprocal(inv, u0))
            tt(u0, e_im, aim, ALU.mult)
            tt(u1, e_re, ea, ALU.mult)
            tt(u0, u0, u1, ALU.subtract)
            tt(f_re, u0, inv, ALU.mult)
            tt(u0, e_re, aim, ALU.mult)
            tt(u1, e_im, ea, ALU.mult)
            tt(u0, u0, u1, ALU.add)
            link(dve.scalar_tensor_tensor(out=f_im, in0=u0, scalar=-1.0, in1=inv, op0=ALU.mult, op1=ALU.mult))
            cc = C_sb.rearrange("p (n c) -> p n c", c=2)
            tt(u0, f_re, cc[:, :, 0], ALU.mult)
            tt(u1, f_im, cc[:, :, 1], ALU.mult)
            tt(s_re, u0, u1, ALU.subtract)
            tt(u0, f_im, cc[:, :, 0], ALU.mult)
            tt(u1, f_re, cc[:, :, 1], ALU.mult)
            tt(s_im, u0, u1, ALU.add)
            for z, (a, fa, b, fb) in enumerate(((alpha, 1.0, alpha, 1.0), (turns, 1.0, turns, 1.0),
                                                (s_re, 2.0, s_im, -2.0), (s_im, -2.0, s_re, -2.0))):
                link(dve.tensor_scalar(z_rows[:, z, 0:N], a, fa, None, ALU.mult))
                link(dve.tensor_scalar(z_rows[:, z, N:2 * N], b, fb, None, ALU.mult))
            dve.memset(half[0:N, :], 0.25).then_inc(z_ready, 1)
            link(dve.memset(half[N:P, :], 0.0))
            dve.wait_ge(z_turned, 1)
            link(dve.tensor_copy(z_cols[:, :, :], z_ps))
            dve.wait_ge(consts_a, 1)

            def wide(col):
                return col.unsqueeze(2).to_broadcast([P, H, R])

            def steps(row):
                return row.unsqueeze(1).to_broadcast([P, H, R])

            t_alpha, t_turns, p1, pq = (z_cols[:, z, :] for z in range(4))
            b0, b1, b2, b3, b4 = (b_[:, :, :] for b_ in big)
            tt(b0, wide(t_turns), steps(count[:, :]), ALU.mult)
            link(dve.tensor_scalar(b0, b0, half[:, 0:1], None, ALU.add))
            link(dve.tensor_scalar(b1, b0, MAGIC, MAGIC, ALU.add, ALU.subtract))
            dve.tensor_tensor(b0, b0, b1, ALU.subtract).then_inc(table_asked, 1)
            dve.wait_ge(table_asked, 1)
            dve.tensor_tensor(b1, wide(t_alpha), steps(count[:, :]), ALU.mult).then_inc(table_asked, 1)
            link(dve.tensor_scalar(t_turns, t_turns, float(R), None, ALU.mult))
            link(dve.tensor_scalar(b2[:, :, 0], t_turns, MAGIC, MAGIC, ALU.add, ALU.subtract))
            tt(t_turns, t_turns, b2[:, :, 0], ALU.subtract)
            link(dve.tensor_scalar(t_alpha, t_alpha, float(R), None, ALU.mult))
            tt(b2, wide(t_turns), steps(count[:, :]), ALU.mult)
            link(dve.tensor_scalar(b3, b2, MAGIC, MAGIC, ALU.add, ALU.subtract))
            dve.tensor_tensor(b3, b2, b3, ALU.subtract).then_inc(table_asked, 1)
            dve.wait_ge(table_asked, 3)
            link(dve.tensor_scalar(b2, b2, 0.25, None, ALU.add))
            link(dve.tensor_scalar(b4, b2, MAGIC, MAGIC, ALU.add, ALU.subtract))
            dve.tensor_tensor(b4, b2, b4, ALU.subtract).then_inc(table_asked, 1)
            dve.wait_ge(table_asked, 4)
            dve.tensor_tensor(b2, wide(t_alpha), steps(count[:, :]), ALU.mult).then_inc(table_asked, 1)
            dve.wait_ge(fc2_in, 16)
            dve.tensor_reduce(fc2_max, raw(FC2_0 + 1, CL), AX.XY, ALU.max, apply_absolute_value=True).then_inc(sums_in, 1)
            dve.wait_ge(gate_in, 16)
            dve.tensor_scalar(gate_abs.bitcast(I32), gate_raw.rearrange("p k e -> p (k e)").bitcast(I32), 0x7FFFFFFF, None,
                              ALU.bitwise_and).then_inc(sums_in, 1)
            dve.wait_ge(table_done, 2)
            dve.tensor_tensor(b0, b0, b1, ALU.mult).then_inc(tables, 1)
            dve.wait_ge(table_done, 5)
            tt(b3, b3, wide(pq), ALU.mult)
            tt(b4, b4, wide(p1), ALU.mult)
            tt(b3, b3, b4, ALU.add)
            dve.tensor_tensor(b3, b3, b2, ALU.mult).then_inc(tables, 1)
            dve.wait_ge(sums_out, 1)
            power_scale(dve, link, s_fc2, fc2_ps, 2.0 ** 14)
            dve.sem_inc(w_scaled, 1)
            dve.wait_ge(w1_abs_used, KT)
            link(dve.tensor_reduce(bound[:, 1:2], w1_sum[:, :], AX.X, ALU.max))
            power_scale(dve, link, s_w1, bound[:, 1:2], 2.0 ** 14)
            dve.sem_inc(w_scaled, 1)
            link(dve.tensor_reduce(gate_sum, gate_ps.rearrange("p (k e) -> p e k", e=NE), AX.X, ALU.add))
            link(dve.tensor_reduce(gate_hl, gate_sum, AX.X, ALU.max))
            power_scale(dve, link, s_gate, gate_hl, 2.0 ** 14)
            dve.sem_inc(gate_scaled, 1)
            dve.wait_ge(up_abs_used, 2 * KT)
            link(dve.tensor_reduce(bound[:, 2:3], up_sum[:, :, :], AX.XY, ALU.max))
            power_scale(dve, link, s_up, bound[:, 2:3], 2.0 ** 14)
            dve.wait_ge(ring_free, 20)
            link(dve.tensor_tensor(kf[0:1, :, 0], kf[0:1, :, 0], d_row[:, :], ALU.add))
            dve.tensor_reduce(abs_sum, kf, AX.X, ALU.add, apply_absolute_value=True).then_inc(sums_in, 1)
            dve.wait_ge(sums_out, 2)
            power_scale(dve, link, sk, sk_ps, 2.0 ** 14)
            dve.tensor_tensor(k_sc, kf, sk[0:R, :].unsqueeze(2).to_broadcast([R, H, R]), ALU.mult).then_inc(k_scaled, 1)
            sk2 = sk.rearrange("p (t j) -> p t j", j=2)
            link(dve.tensor_scalar(pair_scale[0:B, :], sk2[0:B, :, 0], 2.0 ** -15, None, ALU.mult))
            link(dve.tensor_scalar(pair_scale[B:P, :], sk2[B:P, :, 1], 2.0 ** -15, None, ALU.mult))
            for j in range(UP_0):
                dve.wait_ge(piece_hi, j + 1)
                dve.scalar_tensor_tensor(out=W[:, j, L:2 * L], in0=raw(j + 1)[:, 0, :], scalar=s_fc2 if j < W1_0 else s_w1,
                                         in1=W[:, j, 0:L], op0=ALU.mult, op1=ALU.subtract).then_inc(piece_lo, 1)
            dve.wait_ge(gate_hi, 1)
            link(dve.scalar_tensor_tensor(out=gate[:, :, NE:2 * NE], in0=gate_raw, scalar=s_gate, in1=gate[:, :, 0:NE],
                                          op0=ALU.mult, op1=ALU.subtract))
            dve.wait_ge(k_split, 1)
            dve.wait_ge(k_scaled, 1)
            dve.tensor_tensor(k_lo, k_sc, k_hi, ALU.subtract).then_inc(k_split, 1)


def conv(nc, W, raw, id16, ones32, pair_scale, rho, s_up, s_down, k_dram, hid_dram, x, itok, down_w):
    EARLY = 10
    with ExitStack() as ctx:
        def sb(name, shape, dt):
            return ctx.enter_context(nc.sbuf_tensor(name, shape, dt))

        def psum(name, shape, dt=F32):
            return ctx.enter_context(nc.psum_tensor(name, shape, dt))

        def sem(name):
            return ctx.enter_context(nc.semaphore(name))

        time_row = sb("time_row", [P, L], I16)
        mask = sb("mask", [P, KT, B], BF16)
        len_i = sb("len_i", [P, 1], I32)
        len_col = sb("len_col", [P, 1], F32)
        len_row = sb("len_row", [P, B], I32)
        xn = sb("xn", [P, 2, L], F32)
        x_hl = sb("x_hl", [P, 2, KT, P], F16)
        uT = sb("uT", [P, 2, 2, KT, P], F16)
        slab = sb("slab", [P, 2, 2, L], F16)
        hid32 = sb("hid32", [P, KT, B], F32)
        hid = sb("hid", [P, 2, 2, KT, P], F16)
        amax = sb("amax", [P, 2], F32)
        tau = sb("tau", [P, 2], F32)
        down_max = sb("down_max", [P, CI], F32)
        down_row = sb("down_row", [P, 1], F32)

        turned = [psum(f"turned{k}", [P, KT, P], F16) for k in range(2)]
        conv_ps = [psum(f"conv_ps{j}", [P, KT, B]) for j in range(2)]
        sum_ps = psum("sum_ps", [P, 512])

        len_in, down_in = sem("len_in"), sem("down_in")
        x_in = [sem(f"x_in{b}") for b in range(2)]
        slab_in = [sem(f"slab_in{j}") for j in range(2)]
        stored = [sem(f"stored{b}") for b in range(2)]
        iotas = sem("iotas")
        dve_c = sem("dve_chain2")
        tau_ready, x_hi, x_lo, x_turned, u_ready = map(sem, ("tau_ready", "x_hi", "x_lo", "x_turned", "u_ready"))
        convolved, masked, hid_hi, hid_lo = map(sem, ("convolved", "masked", "hid_hi", "hid_lo"))
        piece_hi, piece_lo = sem("piece_hi2"), sem("piece_lo2")
        row_max, row_sum = sem("row_max"), sem("row_sum")
        down_scaled = sem("down_scaled")

        block = ctx.enter_context(nc.Block())
        LOOP1, LOOP2 = (1, 9), (9, PAIRS // 2)

        def backwards(part):
            return bass.AP(x_hl, part * L + P - 1, [[2 * L, P], [P, KT], [-1, P]])

        def chunks(rows):
            return rows.rearrange("p (k m) -> p k m", k=KT)

        def x_rows(t, j):
            return x[:, bass.ds(2 * t + j, 1), :].rearrange("b o l -> (b o) l")

        @block.sync
        def _(sp):
            def load_x(t, b):
                for j in range(2):
                    sp.dma_start(xn[j * B:j * B + B, b, :], x_rows(t, j)).then_inc(x_in[b], 16)

            def load_slab(t, j):
                src = bass.AP(k_dram, (2 * t + j) * KPAD + 1, [[1, P], [H * KPAD, 2], [1, L]])
                sp.dma_start(slab[:, j, :, :], src).then_inc(slab_in[j], 16)

            def store(t, b):
                sp.wait_ge(hid_lo, 1 + 2 * t + 2)
                sp.dma_start(hid_dram.ap()[bass.ds(t, 1), :, :, :, :].rearrange("o p a k m -> p (o a k m)"),
                             hid[:, b, :, :, :].rearrange("p a k m -> p (a k m)")).then_inc(stored[b], 16)

            def step(t, b, last=False):
                if not last:
                    sp.wait_ge(x_lo, t)
                    load_x(t + 1, 1 - b)
                for j in range(2):
                    sp.wait_ge(convolved, 2 * t - 3 + j)
                    load_slab(t - 1, j)
                store(t - 2, b)

            for b in range(2):
                sp.sem_inc(stored[b], 16)
            load_x(0, 0)
            load_x(1, 1)
            load_slab(0, 0)
            load_slab(0, 1)
            sp.wait_ge(x_lo, 1)
            load_x(2, 0)
            with sp.Fori(1, PAIRS // 2 - 1) as i:
                for b in range(2):
                    step(2 * i + b, b)
            step(PAIRS - 2, 0)
            step(PAIRS - 1, 1, last=True)
            for j in range(2):
                sp.wait_ge(convolved, 2 * PAIRS - 3 + j)
                load_slab(PAIRS - 1, j)
            store(PAIRS - 2, 0)
            store(PAIRS - 1, 1)
            for b in range(2):
                sp.wait_ge(stored[b], 16 + 16 * (PAIRS // 2))

        @block.gpsimd
        def _(pool):
            start_at_one(pool, hid_lo)
            pool.iota(time_row[:, :], pattern=[[1, L]], base=0, channel_multiplier=0).then_inc(iotas, 1)
            pool.iota(hid32[:, :, :].bitcast(I32), pattern=[[P, KT], [0, B]], base=0,
                      channel_multiplier=1).then_inc(iotas, 1)

            def low_halves(t, b):
                for j in range(2):
                    pool.wait_ge(hid_hi, 2 * t + j + 1)
                    cols = hid[:, b, :, :, j * B:j * B + B]
                    pool.tensor_tensor(cols[:, 1], hid32[:, :, :], cols[:, 0], ALU.subtract).then_inc(hid_lo, 1)

            with pool.Fori(1, PAIRS // 2) as i:
                for b in range(2):
                    low_halves(2 * i + b - 2, b)
            low_halves(PAIRS - 2, 0)
            low_halves(PAIRS - 1, 1)

        @block.scalar
        def _(act):
            for j in range(2):
                act.dma_start(len_i[j * B:j * B + B, :], itok.rearrange("(b o) -> b o", o=1)).then_inc(len_in, 16)
            act.dma_start(len_row[:, :], itok.rearrange("(o b) -> o b", o=1).to_broadcast([P, B])).then_inc(len_in, 16)
            act.dma_start(raw(DN_0 + 1 + EARLY, CI - EARLY),
                          down_w.rearrange("(c p) m -> p c m", p=P)[:, EARLY:CI, :]).then_inc(down_in, 16)

            def x_high(t, b):
                act.wait_ge(tau_ready, t + 1)
                if not first(t):
                    act.wait_ge(x_turned, t)
                act.activation(backwards(0), chunks(xn[:, b, :]), ACT.Copy, scale=tau[:, b:b + 1]).then_inc(x_hi, 1)

            def piece_high(t, scale):
                act.wait_ge(piece_lo, 1 + t - 2)
                j = UP_0 + t - 2
                act.activation(W[:, bass.ds(j, 1), 0:L], W[:, bass.ds(j + 1, 1), :].bitcast(F32), ACT.Copy,
                               scale=scale).then_inc(piece_hi, 1)

            def hid_high(t, b):
                for j in range(2):
                    act.wait_ge(masked, 2 * t + j + 1)
                    act.activation(hid[:, b, 0, :, j * B:j * B + B], hid32[:, :, :], ACT.Copy).then_inc(hid_hi, 1)

            def u_copy(t, b):
                act.wait_ge(x_turned, t + 1)
                for k in range(2):
                    act.activation(uT[:, b, k, :, :], turned[k][:, :, :], ACT.Copy).then_inc(u_ready, 1)

            x_high(0, 0)
            u_copy(0, 0)
            x_high(1, 1)
            u_copy(1, 1)
            for (lo, hi), scale in ((LOOP1, s_up), (LOOP2, s_down)):
                if scale is s_down:
                    act.wait_ge(down_scaled, 1)
                with act.Fori(lo, hi) as i:
                    for b in range(2):
                        t = 2 * i + b
                        x_high(t, b)
                        piece_high(t, scale)
                        act.wait_ge(stored[b], 16 + 16 * i - 16)
                        hid_high(t - 2, b)
                        act.wait_ge(convolved, 2 * t - 2)
                        u_copy(t, b)
            for b in range(2):
                t = PAIRS + b
                piece_high(t, s_down)
                act.wait_ge(stored[b], 16 + 16 * (PAIRS // 2 - 1))
                hid_high(t - 2, b)

        @block.tensor
        def _(pe):
            def turn(t):
                pe.wait_ge(x_lo, t + 1)
                if not first(t):
                    pe.wait_ge(u_ready, 2 * t)
                for k in range(2):
                    for c in range(KT):
                        ins = pe.transpose(turned[k][:, c, :], x_hl[:, k, c, :], id16[:, :])
                ins.then_inc(x_turned, 1)

            def convolve(t, b):
                pe.wait_ge(u_ready, 2 * t + 2)
                for j in range(2):
                    pe.wait_ge(slab_in[j], 16 * t + 16)
                    if not first(t):
                        pe.wait_ge(masked, 2 * t - 1 + j)
                    for d in range(KT):
                        for ks, ku in ((0, 0), (0, 1), (1, 0)):
                            c0 = d * P
                            ins = pe.matmul(conv_ps[j][:, d:KT, :], slab[:, j, ks, c0:c0 + P],
                                            uT[:, b, ku, 0:KT - d, j * B:j * B + B],
                                            start=(d == ks == ku == 0), stop=(d == KT - 1 and ks == 1))
                    ins.then_inc(convolved, 1)

            turn(0)
            turn(1)
            convolve(0, 0)
            for n, (lo, hi) in enumerate((LOOP1, LOOP2)):
                if n:
                    pe.wait_ge(row_max, 1)
                    pe.matmul(sum_ps[:, 0:1], ones32[:, :], down_row[:, :], start=True, stop=True).then_inc(row_sum, 1)
                with pe.Fori(lo, hi) as i:
                    for b in range(2):
                        t = 2 * i + b
                        turn(t)
                        convolve(t - 1, 1 - b)
            convolve(PAIRS - 1, 1)

        @block.vector
        def _(dve):
            chain = Chain(dve, dve_c)
            link = chain.link
            dve.wait_ge(len_in, 48)
            dve.wait_ge(iotas, 2)
            link(dve.tensor_copy(len_col[:, :], len_i[:, :]))
            link(dve.tensor_tensor(mask[:, :, :], hid32[:, :, :].bitcast(I32), len_row[:, :].unsqueeze(1).to_broadcast([P, KT, B]), ALU.is_lt))
            link(dve.tensor_scalar(mask[:, :, :], mask[:, :, :], 2.0 ** -15, None, ALU.mult))

            def prep_x(t, b, i):
                dve.wait_ge(x_in[b], 32 * i + 32)
                xb = xn[:, b, :]
                link(dve.scalar_tensor_tensor(out=xb, in0=time_row[:, :], scalar=len_col[:, 0:1], in1=xb,
                                              op0=ALU.is_lt, op1=ALU.mult))
                link(dve.tensor_reduce(amax[:, b:b + 1], xb, AX.X, ALU.max, apply_absolute_value=True))
                power_scale(dve, link, tau[:, b:b + 1], amax[:, b:b + 1], 2.0 ** 14)
                dve.tensor_tensor(rho[:, bass.ds(t, 1)], tau[:, b:b + 1], pair_scale[:, bass.ds(t, 1)],
                                  ALU.mult).then_inc(tau_ready, 1)
                dve.wait_ge(x_hi, t + 1)
                dve.scalar_tensor_tensor(out=backwards(1), in0=chunks(xb), scalar=tau[:, b:b + 1], in1=backwards(0),
                                         op0=ALU.mult, op1=ALU.subtract).then_inc(x_lo, 1)

            def mask_hid(t):
                for j in range(2):
                    dve.wait_ge(convolved, 2 * t + j + 1)
                    if not first(t) or j:
                        dve.wait_ge(hid_lo, 1 + 2 * t + j)
                    dve.tensor_tensor(hid32[:, :, :], conv_ps[j][:, :, :], mask[:, :, :], ALU.mult).then_inc(masked, 1)

            def piece_low(t, scale):
                dve.wait_ge(piece_hi, t - 1)
                j = UP_0 + t - 2
                dve.scalar_tensor_tensor(out=W[:, bass.ds(j, 1), L:2 * L], in0=W[:, bass.ds(j + 1, 1), :].bitcast(F32),
                                         scalar=scale, in1=W[:, bass.ds(j, 1), 0:L], op0=ALU.mult,
                                         op1=ALU.subtract).then_inc(piece_lo, 1)

            start_at_one(dve, piece_lo)
            prep_x(0, 0, 0)
            prep_x(1, 1, 0)
            dve.wait_ge(down_in, 16)
            with dve.Fori(*LOOP1) as i:
                chain.loop(i - 1, 2 * 7)
                for b in range(2):
                    t = 2 * i + b
                    prep_x(t, b, i)
                    mask_hid(t - 2)
                    piece_low(t, s_up)
                    link(dve.tensor_reduce(down_max[:, bass.ds(t - 2, 1)], W[:, bass.ds(DN_0 + 1 + t - 2, 1), :].bitcast(F32),
                                           AX.XY, ALU.max, apply_absolute_value=True))
            chain.end_loop(8)
            dve.tensor_reduce(down_row[:, :], down_max[:, :], AX.X, ALU.max).then_inc(row_max, 1)
            dve.wait_ge(row_sum, 1)
            power_scale(dve, link, s_down, sum_ps[:, 0:1], 2.0 ** 14)
            dve.sem_inc(down_scaled, 1)
            with dve.Fori(*LOOP2) as i:
                chain.loop(i - 9, 2 * 6)
                for b in range(2):
                    t = 2 * i + b
                    prep_x(t, b, i)
                    mask_hid(t - 2)
                    piece_low(t, s_down)
            chain.end_loop(7)
            for b in range(2):
                mask_hid(PAIRS - 2 + b)
                piece_low(PAIRS + b, s_down)


def ffn(nc, W, raw, gate, id32, ones32, rho, scales, hid_dram, x, ln_gamma, ln_beta, out):
    s_up, s_w1, s_gate, s_down, s_fc2 = (scales[:, k:k + 1] for k in range(5))
    TT = 2 * P
    HR = 4
    LAG = 3
    with ExitStack() as ctx:
        def sb(name, shape, dt):
            return ctx.enter_context(nc.sbuf_tensor(name, shape, dt))

        def psum(name, shape, dt=F32):
            return ctx.enter_context(nc.psum_tensor(name, shape, dt))

        def sem(name):
            return ctx.enter_context(nc.semaphore(name))

        hid = sb("hid_tile", [P, 2, 2, 2, KT, P], F16)
        h_hl = sb("h_hl", [P, HR, 2, TT], F16)
        r_buf = sb("r_buf", [P, 2, TT], F32)
        h32 = sb("h32", [P, 2, TT], F32)
        route = sb("route", [P, TT], F32)
        gamma = sb("gamma", [P, L], F32)
        beta = sb("beta", [P, L], F32)
        xr = sb("xr", [P, 2, L], F32)
        z = raw(PIECES)[:, 0, :].rearrange("p (b m) -> p b m", b=2)
        theta = sb("theta", [P, PAIRS], F32)
        k_relu = sb("k_relu", [P, 1], F32)
        k_route = sb("k_route", [P, 1], F32)
        kappa = sb("kappa", [P, 1], F32)
        tmp = sb("tmp", [P, 4], F32)
        g_lo = sb("g_lo", [P, 2, NE], F32)
        logits = sb("logits", [P, 2, NE], F32)
        top = sb("top", [P, 2, NE], F32)
        s_tok = sb("s_tok", [P, 2], F32)
        diag = route[:, :].rearrange("p (s m) -> p s m", s=2)
        stats = sb("stats", [P, 2, 6], F32)
        mv = sb("mv", [P, 2], F32)
        ln = sb("ln", [P, 6], F32)

        acc = psum("acc", [P, 2, 2, 512])
        up_ps = psum("up_ps", [P, 3, 512])
        route_bank = psum("route_bank", [P, 512])
        gate_ps = route_bank[:, 0:4 * NE].rearrange("p (s e) -> p s e", s=2)
        route_ps = route_bank[:, TT:2 * TT].rearrange("p (s m) -> p s m", s=2)

        hid_in = [sem(f"hid_in{b}") for b in range(2)]
        xr_in = [sem(f"xr_in{s}") for s in range(2)]
        out_stored = [sem(f"out_stored{s}") for s in range(2)]
        ln_in, dve_c, consts = sem("ln_in"), sem("dve_chain3"), sem("consts3")
        up_done, relu_done, up_free, h_hi, h_lo, down_done = map(
            sem, ("up_done", "relu_done", "up_free", "h_hi", "h_lo", "down_done"))
        gate_done, diag_ready, route_done, acc_done = map(sem, ("gate_done", "diag_ready", "route_done", "acc_done"))
        root_asked, root_done, norm_ready, z_done, z_scaled, z_added = map(
            sem, ("root_asked", "root_done", "norm_ready", "z_done", "z_scaled", "z_added"))
        xb_done = sem("xb_done")

        block = ctx.enter_context(nc.Block())

        def slot_of(c):
            return up_ps[:, c % 3, 0:TT]

        @block.sync
        def _(sp):
            def load_hid(T, b):
                for s in range(2):
                    sp.dma_start(hid[:, b, s, :, :, :].rearrange("p a k m -> p (a k m)"),
                                 hid_dram.ap()[bass.ds(2 * T + s, 1), :, :, :, :].rearrange("o p a k m -> p (o a k m)")
                                 ).then_inc(hid_in[b], 16)

            def load_x(T):
                for s in range(2):
                    if not first(T):
                        sp.wait_ge(out_stored[s], 32 * T)
                    for j in range(2):
                        sp.dma_start(xr[j * B:j * B + B, s, :],
                                     x[:, bass.ds(4 * T + 2 * s + j, 1), :].rearrange("b o l -> (b o) l")
                                     ).then_inc(xr_in[s], 16)

            load_hid(0, 0)
            load_hid(1, 1)
            load_x(0)
            with sp.Fori(1, TILES // 2) as i:
                for b in range(2):
                    T = 2 * i + b
                    sp.wait_ge(up_done, (T - 1) * NC)
                    load_hid(T, b)
                    load_x(T - 1)
            load_x(TILES - 1)

        @block.gpsimd
        def _(pool):
            def low_half(T, c):
                pool.wait_ge(h_hi, T * NC + c + 1)
                pool.tensor_tensor(h_hl[:, c % HR, 1, :], h32[:, c % 2, :], h_hl[:, c % HR, 0, :],
                                   ALU.subtract).then_inc(h_lo, 1)

            pool.wait_ge(ln_in, 32)
            with pool.Fori(0, TILES // 2) as i:
                for b in range(2):
                    T = 2 * i + b
                    for c in range(NC):
                        low_half(T, c)
                        if c in (9, 11):
                            s = (c - 9) // 2
                            pool.wait_ge(xr_in[s], 32 * T + 32)
                            pool.tensor_tensor(xr[:, s, :], xr[:, s, :], beta[:, :], ALU.add).then_inc(xb_done, 1)
                    for s in range(2):
                        for k in range(2):
                            n = 4 * T + 2 * s + k
                            pool.wait_ge(z_done, 1 + n + 1)
                            pool.tensor_tensor(z[:, k, :], z[:, k, :], gamma[:, k * 512:k * 512 + 512],
                                               ALU.mult).then_inc(z_scaled, 1)
                    for s in range(2):
                        pool.wait_ge(z_added, 1 + 4 * T + 2 * s + 2)
                        for j in range(2):
                            pool.dma_start(out[:, bass.ds(4 * T + 2 * s + j, 1), :].rearrange("b o l -> (b o) l"),
                                           xr[j * B:j * B + B, s, :]).then_inc(out_stored[s], 16)
            for s in range(2):
                pool.wait_ge(out_stored[s], 32 * TILES)

        @block.scalar
        def _(act):
            act.dma_start(gamma[:, :], ln_gamma.rearrange("(o l) -> o l", o=1).to_broadcast([P, L])).then_inc(ln_in, 16)
            act.dma_start(beta[:, :], ln_beta.rearrange("(o l) -> o l", o=1).to_broadcast([P, L])).then_inc(ln_in, 16)
            start_at_one(act, z_done)
            act.wait_ge(consts, 1)
            with act.Fori(0, TILES // 2) as i:
                for b in range(2):
                    T = 2 * i + b
                    for c in range(NC + 1):
                        n = T * NC + c
                        if c < CI:
                            act.wait_ge(up_done, n + 1)
                            act.activation(r_buf[:, c % 2, :], slot_of(c), ACT.Relu, scale=k_relu[:, 0:1]).then_inc(relu_done, 1)
                        if c >= 1:
                            act.wait_ge(up_free, 1 + n)
                            act.wait_ge(down_done, 1 + T * NC + max(c - HR, 0))
                            act.activation(h_hl[:, (c - 1) % HR, 0, :], h32[:, (c - 1) % 2, :], ACT.Copy).then_inc(h_hi, 1)
                    for s in range(2):
                        act.wait_ge(root_asked, 2 * T + s + 1)
                        act.activation(ln[:, 1:2], ln[:, 0:1], ACT.Sqrt).then_inc(root_done, 1)
                        act.wait_ge(norm_ready, 2 * T + s + 1)
                        for k in range(2):
                            act.wait_ge(z_added, 1 + 4 * T + (k + 1) * s)
                            act.activation(z[:, k, :], acc[:, s, k, :], ACT.Identity, bias=ln[:, 5:6],
                                           scale=ln[:, 4:5]).then_inc(z_done, 1)

        @block.tensor
        def _(pe):
            def three(o, stat, mov, first, last):
                for n, (a, m) in enumerate(((0, 0), (0, 1), (1, 0))):
                    ins = pe.matmul(o, stat[a], mov[m], start=(first and n == 0), stop=(last and n == 2))
                return ins

            def up(T, c, b):
                pe.wait_ge(up_free, 1 + T * NC + max(c - 2, 0))
                for k in range(KT):
                    if c < CI:
                        piece, col = UP_0 + 2 * k + c // 8, c % 8 * P
                    else:
                        piece, col = W1_0 + k // 2, k % 2 * LAT + (c - CI) * P
                    stat = [W[:, piece, a * L + col:a * L + col + P] for a in range(2)]
                    mov = [hid[:, b, :, a, k, :] for a in range(2)]
                    ins = three(slot_of(c), stat, mov, k == 0, k == KT - 1)
                ins.then_inc(up_done, 1)

            def down(T, c):
                pe.wait_ge(h_lo, T * NC + c + 1)
                piece = DN_0 + c if c < CI else FC2_0 + c - CI
                for s in range(2):
                    for k in range(2):
                        stat = [h_hl[:, c % HR, a, s * P:s * P + P] for a in range(2)]
                        mov = [W[:, piece, a * L + k * 512:a * L + k * 512 + 512] for a in range(2)]
                        ins = three(acc[:, s, k, :], stat, mov, c == 0, c == NC - 1)
                    if c == NC - 1 and s == 0:
                        ins.then_inc(acc_done, 1)
                ins.then_inc(down_done, 1)

            def gate_logits(T, b):
                pe.wait_ge(diag_ready, 1 + T)
                for s in range(2):
                    for k in range(KT):
                        for a in ((0, 1) if k == 0 else (1, 0)):
                            w = NE if a else 2 * NE
                            ins = pe.matmul(gate_ps[:, s, 0:w], hid[:, b, s, a, k, :], gate[:, k, 0:w],
                                            start=(k == a == 0), stop=(k == KT - 1 and a == 0), skip_group_check=bool(a))
                ins.then_inc(gate_done, 1)

            start_at_one(pe, down_done)
            pe.wait_ge(consts, 1)
            with pe.Fori(0, TILES // 2) as i:
                for b in range(2):
                    T = 2 * i + b
                    pe.wait_ge(hid_in[b], 32 * i + 32)
                    gate_logits(T, b)
                    for c in range(NC):
                        up(T, c, b)
                        if c == 2:
                            pe.wait_ge(diag_ready, 1 + T + 1)
                            for s in range(2):
                                ins = pe.matmul(route_ps[:, s, :], ones32[:, :], diag[:, s, :], start=True, stop=True)
                            ins.then_inc(route_done, 1)
                        if c == LAG:
                            pe.wait_ge(z_done, 1 + 4 * T)
                        if c >= LAG:
                            down(T, c - LAG)
                    for c in range(NC - LAG, NC):
                        down(T, c)

        @block.vector
        def _(dve):
            chain = Chain(dve, dve_c)
            link = chain.link

            def tt(o, a, b_, op):
                link(dve.tensor_tensor(o, a, b_, op))

            start_at_one(dve, up_free, diag_ready, z_added)
            tt(tmp[:, 0:1], s_w1, s_gate, ALU.mult)
            tt(tmp[:, 0:1], tmp[:, 0:1], s_fc2, ALU.mult)
            link(dve.reciprocal(tmp[:, 0:1], tmp[:, 0:1]))
            tt(tmp[:, 1:2], s_up, s_up, ALU.mult)
            tt(tmp[:, 1:2], tmp[:, 1:2], s_down, ALU.mult)
            tt(tmp[:, 2:3], tmp[:, 0:1], tmp[:, 1:2], ALU.mult)
            link(dve.reciprocal(tmp[:, 3:4], tmp[:, 2:3]))
            link(dve.tensor_scalar(k_relu[:, :], tmp[:, 3:4], 1.0, 2.0 ** -46, ALU.min, ALU.mult))
            link(dve.tensor_scalar(k_route[:, :], tmp[:, 2:3], 1.0, 2.0 ** -46, ALU.min, ALU.mult))
            tt(kappa[:, :], tmp[:, 1:2], k_relu[:, :], ALU.mult)
            tt(theta[:, :], rho[:, :], rho[:, :], ALU.mult)
            link(dve.tensor_scalar(theta[:, :], theta[:, :], kappa[:, 0:1], 2.0 ** 62, ALU.mult, ALU.min))
            link(dve.scalar_tensor_tensor(out=theta[:, :], in0=theta[:, :], scalar=LN_EPS, in1=theta[:, :],
                                          op0=ALU.mult, op1=ALU.mult))
            dve.sem_inc(consts, 1)

            def carry_wait():
                dve.tensor_copy(tmp[0:1, 1:2], tmp[0:1, 0:1])

            def route_weights(T):
                dve.wait_ge(gate_done, T + 1)
                link(dve.tensor_copy(g_lo[:, :, :], gate_ps[:, :, NE:2 * NE]))
                tt(logits[:, :, :], gate_ps[:, :, 0:NE], g_lo[:, :, :], ALU.add)
                carry_wait()
                dve.max(top[:, 0, :], logits[:, 0, :])
                link(dve.max(top[:, 1, :], logits[:, 1, :]))
                tt(s_tok[:, :], top[:, :, 0], top[:, :, 1], ALU.add)
                for s in range(2):
                    link(dve.tensor_scalar(diag[:, s, :], id32[:, :], s_tok[:, s:s + 1], k_route[:, 0:1], ALU.mult, ALU.mult))
                dve.sem_inc(diag_ready, 1)

            def evacuate(T, c):
                n = T * NC + c
                if c < CI:
                    dve.wait_ge(relu_done, T * CI + c + 1)
                    dve.scalar_tensor_tensor(out=h32[:, c % 2, :], in0=slot_of(c), scalar=0.0, in1=r_buf[:, c % 2, :],
                                             op0=ALU.max, op1=ALU.mult).then_inc(up_free, 1)
                else:
                    dve.wait_ge(up_done, n + 1)
                    dve.tensor_tensor(h32[:, c % 2, :], slot_of(c), route[:, :], ALU.mult).then_inc(up_free, 1)

            def layernorm(T, s):
                if s == 0:
                    dve.wait_ge(acc_done, T + 1)
                else:
                    dve.wait_ge(down_done, 1 + (T + 1) * NC)
                for k in range(2):
                    link(dve.bn_stats(stats[:, k, :], acc[:, s, k, :]))
                carry_wait()
                link(dve.bn_aggr(mv[:, :], stats[:, :, :]))
                dve.tensor_tensor(ln[:, 0:1], mv[:, 1:2], theta[:, bass.ds(2 * T + s, 1)], ALU.add).then_inc(root_asked, 1)
                dve.wait_ge(root_done, 2 * T + s + 1)
                link(dve.reciprocal(ln[:, 2:3], ln[:, 1:2]))
                link(dve.scalar_tensor_tensor(out=ln[:, 3:4], in0=ln[:, 0:1], scalar=ln[:, 2:3], in1=ln[:, 2:3],
                                              op0=ALU.mult, op1=ALU.mult))
                link(dve.tensor_scalar(ln[:, 3:4], ln[:, 3:4], -0.5, 1.5, ALU.mult, ALU.add))
                dve.wait_ge(z_done, 1 + 4 * T + 2 * s)
                tt(ln[:, 4:5], ln[:, 2:3], ln[:, 3:4], ALU.mult)
                dve.scalar_tensor_tensor(out=ln[:, 5:6], in0=mv[:, 0:1], scalar=-1.0, in1=ln[:, 4:5],
                                         op0=ALU.mult, op1=ALU.mult).then_inc(norm_ready, 1)

            def add_z(T, s):
                for k in range(2):
                    n = 4 * T + 2 * s + k
                    dve.wait_ge(z_scaled, n + 1)
                    if k == 0:
                        dve.wait_ge(xb_done, 2 * T + s + 1)
                    cols = xr[:, s, k * 512:k * 512 + 512]
                    dve.tensor_tensor(cols, cols, z[:, k, :], ALU.add).then_inc(z_added, 1)

            with dve.Fori(0, TILES // 2) as i:
                chain.loop(i, 2 * (6 + 2 * 7 + 1))
                for b in range(2):
                    T = 2 * i + b
                    route_weights(T)
                    for c in range(NC):
                        if c >= 2:
                            dve.wait_ge(h_lo, T * NC + c - 1)
                        evacuate(T, c)
                        if c == 5:
                            dve.wait_ge(route_done, T + 1)
                            link(dve.tensor_copy(route[:, :], route_ps[:, :, :].rearrange("p s m -> p (s m)")))
                    layernorm(T, 0)
                    layernorm(T, 1)
                    add_z(T, 0)
                    add_z(T, 1)
            chain.end_loop(TILES // 2)


_INS = ["x", "itok_B_8_3872", "L0_cond_log_dt", "L0_cond_C", "L0_cond_log_A_real", "L0_cond_A_imag", "L0_cond_D",
        "L0_ffn_gate_w", "L0_ffn_up_w", "L0_ffn_down_w", "L0_ffn_fc1_w", "L0_ffn_fc2_w", "L0_ffn_expert_w",
        "L0_ffn_ln_gamma", "L0_ffn_ln_beta"]


def kernel(**inputs):
    import numpy as np
    import concourse.bacc as bacc
    from concourse.bass_utils import run_bass_kernel_spmd

    nc = bacc.Bacc("TRN2", target_bir_lowering=False, num_devices=1)
    arrays, args = {}, []
    for name in _INS:
        a = np.ascontiguousarray(inputs[name])
        arrays[f"in_{name}"] = a
        args.append(nc.dram_tensor(f"in_{name}", a.shape, mybir.dt.from_np(a.dtype), kind="ExternalInput").ap())
    args.append(nc.dram_tensor("out_0", (B, H, L), F32, kind="ExternalOutput").ap())
    build(nc, *args)
    r = run_bass_kernel_spmd(nc, [arrays], core_ids=[0])
    return r.results[0]["out_0"]
```

```python
import math
from contextlib import ExitStack

import concourse.bass as bass
from concourse import mybir

F32 = mybir.dt.float32
F16 = mybir.dt.float16
BF16 = mybir.dt.bfloat16
I32 = mybir.dt.int32
I16 = mybir.dt.int16
U8 = mybir.dt.uint8
ALU = mybir.AluOpType
ACT = mybir.ActivationFunctionType
AX = mybir.AxisListType

P = 128
B, H, L = 64, 64, 1024
N = 64
INT, LAT, NE = 2048, 512, 8
KT = L // P
CI = INT // P
CL = LAT // P
NC = CI + CL
PAIRS = H // 2
TILES = PAIRS // 2
LN_EPS = 1e-5
R = 32
KPAD = P + L

FC2_0, W1_0, UP_0, DN_0 = 0, CL, CL + 4, CL + 4 + 2 * KT
PIECES = DN_0 + CI
MAGIC = 1.5 * 2.0 ** 23
TWO_PI = 6.2831850
EXP_MASK = 0x7F800000
TINY = 2.0 ** -40


class Chain:

    def __init__(self, eng, sem):
        self.eng, self.sem, self.count, self.turn, self.per = eng, sem, 0, 0, 0

    def loop(self, turn, per):
        self.start, self.turn, self.per = self.count, turn, per

    def end_loop(self, turns):
        assert self.count - self.start == self.per
        self.count, self.turn = self.start + self.per * turns, 0

    def link(self, ins):
        ins.then_inc(self.sem, 1)
        self.count += 1
        self.eng.wait_ge(self.sem, self.count + self.turn * self.per)


def build(nc, x, itok, log_dt, C, log_A_real, A_imag, D, gate_w, up_w, down_w, fc1_w, fc2_w, expert_w,
          ln_gamma, ln_beta, out):
    k_dram = nc.dram_tensor("k_padded", (2, H, KPAD), F16)
    hid_dram = nc.dram_tensor("hidden_pairs", (PAIRS, P, 2, KT, P), F16)
    relu_dram = nc.dram_tensor("relu_scales", (PAIRS, P), BF16)

    with ExitStack() as top:
        def sb(name, shape, dt, stack=top):
            return stack.enter_context(nc.sbuf_tensor(name, shape, dt))

        W = sb("weights", [P, PIECES + 1, 2 * L], F16)
        gate = sb("gate", [P, KT, 2 * NE], F16)
        id16 = sb("id16", [P, P], F16)
        ones16 = sb("ones16", [P, P], BF16)
        pair_scale = sb("pair_scale", [P, PAIRS], F32)
        rho = sb("rho", [P, PAIRS], F32)
        energy = sb("energy", [P, PAIRS], F32)
        scales = sb("scales", [P, 8], F32)
        s_up, s_w1, s_gate, s_down, s_fc2 = (scales[:, k:k + 1] for k in range(5))

        def raw(slot, n=1):
            return W[:, slot:slot + n, :].bitcast(F32)

        prepare(nc, W, raw, gate, id16, ones16, pair_scale, s_up, s_w1, s_gate, s_fc2, k_dram,
                log_dt, C, log_A_real, A_imag, D, gate_w, up_w, down_w, fc1_w,
                fc2_w, expert_w)
        conv(nc, W, raw, id16, ones16, pair_scale, rho, energy, s_up, s_w1, s_down, k_dram, hid_dram, x, itok, down_w)
        ffn(nc, W, raw, gate, id16, rho, energy, scales, hid_dram, relu_dram, x, ln_gamma, ln_beta, out)


def start_at_one(eng, *sems):
    for s in sems:
        eng.sem_inc(s, 1)


def first(t):
    return isinstance(t, int) and t == 0


def power_scale(dve, link, dst, src, target):
    link(dve.tensor_scalar(dst, src, TINY, None, ALU.max))
    link(dve.tensor_scalar(dst.bitcast(I32), dst.bitcast(I32), EXP_MASK, None, ALU.bitwise_and))
    link(dve.reciprocal(dst, dst))
    link(dve.tensor_scalar(dst, dst, target, None, ALU.mult))


def root_power(dve, link, dst, src, least):
    link(dve.tensor_scalar(dst, src, least, None, ALU.max))
    link(dve.tensor_scalar(dst.bitcast(I32), dst.bitcast(I32), EXP_MASK, None, ALU.bitwise_and))
    link(dve.tensor_scalar(dst.bitcast(I32), dst.bitcast(I32), 0.5, 127.0 * 2.0 ** 22, ALU.mult, ALU.add))
    link(dve.tensor_scalar(dst.bitcast(I32), dst.bitcast(I32), EXP_MASK, None, ALU.bitwise_and))


def norm_scale(dve, link, dst, src, target, least=TINY ** 2):
    root_power(dve, link, dst, src, least)
    link(dve.reciprocal(dst, dst))
    link(dve.tensor_scalar(dst, dst, target, None, ALU.mult))


def prepare(nc, W, raw, gate, id16, ones16, pair_scale, s_up, s_w1, s_gate, s_fc2, k_dram,
            log_dt, C, log_A_real, A_imag, D, gate_w, up_w, down_w, fc1_w, fc2_w, expert_w):
    with ExitStack() as ctx:
        def sb(name, shape, dt):
            return ctx.enter_context(nc.sbuf_tensor(name, shape, dt))

        def psum(name, shape, dt=F32):
            return ctx.enter_context(nc.psum_tensor(name, shape, dt))

        def sem(name):
            return ctx.enter_context(nc.semaphore(name))

        S0 = DN_0 + 1
        fc1_sb = raw(S0, 4).rearrange("p s (k m) -> p (s k) m", m=LAT)
        fc1T = raw(S0 + 4, 4)
        expert_sb = raw(S0 + 8, 2).rearrange("p s (k m) -> p (s k) m", m=LAT)
        small = raw(S0 + 10, 3).rearrange("p s m -> p (s m)")
        up_sq = W[:, S0 + 13, :].bitcast(BF16).rearrange("p (b m) -> p b m", b=2)
        w1_sq = W[:, S0 + 14, 0:2 * LAT].bitcast(BF16).rearrange("p (b m) -> p b m", b=2)
        kpad0 = W[:, S0 + 14, 2 * LAT:2 * LAT + P]

        big = [sb(f"table{k}", [P, H, R], F32) for k in range(5)]
        count = sb("count", [P, R], F32)
        id32 = sb("id32", [P, P], F32)
        ones32 = sb("ones32", [P, P], F32)
        half = sb("half", [P, 1], F32)
        d_row = sb("d_row", [1, H], F32)
        z_cols = sb("z_cols", [P, 4, H], F32)

        nxt = [0]

        def cut(n):
            nxt[0] += n
            return small[0:H, nxt[0] - n:nxt[0]]

        logs, C_sb, aim = cut(N + 1), cut(2 * N), cut(N)
        t0, t1, t2, ex, q, p2 = (cut(N + 1) for _ in range(6))
        alpha, w_im, turns, fhalf, sin_w, sin_h = (cut(N) for _ in range(6))
        e_re, e_im, inv, f_re, f_im, s_re, s_im, u0, u1 = (cut(N) for _ in range(9))
        z_rows = cut(4 * P).rearrange("p (z s) -> p z s", z=4)
        kf = big[1][0:R, :, :]
        abs_sum = big[2][0:R, :, 0]
        k_sc = big[3][0:R, :, :]
        k_hi = big[4][0:R, :, :].bitcast(F16)[:, :, 0:R]
        k_lo = big[4][0:R, :, :].bitcast(F16)[:, :, R:2 * R]
        nxt_g = small[:, nxt[0]:nxt[0] + 512]
        gate_raw = nxt_g[:, 0:64].rearrange("p (k e) -> p k e", e=NE)
        gate_sq = nxt_g[:, 64:128]
        gate_sum = nxt_g[:, 128:136]
        gate_hl = nxt_g[:, 136:137]
        fc2_max = nxt_g[:, 137:138]
        sk = nxt_g[:, 192:256]
        bound = nxt_g[:, 256:260]

        up_sum = psum("up_sum", [P, 4, 512])
        ring = psum("ring", [P, 2, 512])
        w1_sum = psum("w1_sum", [P, 512])
        misc = psum("misc", [P, 512])
        z_ps, gate_ps = misc[:, 0:4 * H].rearrange("p (z h) -> p z h", z=4), misc[:, 256:320]
        fc2_ps, sk_ps = misc[:, 320:321], misc[:, 384:448]

        fc1_in, expert_in, cond_in, gate_in, fc2_in = map(sem, ("fc1_in", "expert_in", "cond_in", "gate_in", "fc2_in"))
        up_in = [sem(f"up_in{k}") for k in range(4)]
        consts, consts_a = sem("consts"), sem("consts_a")
        dve_c = sem("dve_chain")
        sines_asked, sines_done, z_ready, z_turned = map(sem, ("sines_asked", "sines_done", "z_ready", "z_turned"))
        ring_full, ring_free = sem("ring_full"), sem("ring_free")
        w1_sq_ready, w1_sq_used, w1_summed = map(sem, ("w1_sq_ready", "w1_sq_used", "w1_summed"))
        up_sq_ready, up_sq_used = sem("up_sq_ready"), sem("up_sq_used")
        table_asked, table_done, tables = map(sem, ("table_asked", "table_done", "tables"))
        sums_in, sums_out, k_ready, k_scaled, k_split, k_out = map(
            sem, ("sums_in", "sums_out", "k_ready", "k_scaled", "k_split", "k_out"))
        w_scaled, piece_hi, piece_lo, gate_scaled, gate_hi = map(
            sem, ("w_scaled", "piece_hi", "piece_lo", "gate_scaled", "gate_hi"))
        pad_ready, down_in = sem("pad_ready"), sem("down_early")

        block = ctx.enter_context(nc.Block())

        @block.sync
        def _(sp):
            sp.dma_start(logs[:, 0:N], log_A_real).then_inc(cond_in, 16)
            sp.dma_start(logs[:, N:N + 1], log_dt.rearrange("(h o) -> h o", o=1)).then_inc(cond_in, 16)
            sp.dma_start(C_sb, C.rearrange("h n c -> h (n c)")).then_inc(cond_in, 16)
            sp.dma_start(aim, A_imag).then_inc(cond_in, 16)
            sp.dma_start(d_row[:, :], D.rearrange("(o h) -> o h", o=1)).then_inc(cond_in, 16)
            sp.dma_start(fc1_sb, fc1_w.rearrange("(c p) m -> p c m", p=P)).then_inc(fc1_in, 16)
            sp.dma_start(expert_sb, expert_w.rearrange("(c p) m -> p c m", p=P)).then_inc(expert_in, 16)
            sp.dma_start(raw(FC2_0 + 1, CL), fc2_w.rearrange("(c p) m -> p c m", p=P)).then_inc(fc2_in, 16)
            for k in range(4):
                sp.dma_start(raw(UP_0 + 1 + 4 * k, 4).rearrange("p (c s) m -> p c (s m)", s=2),
                             up_w.rearrange("(c p) m -> p c m", p=P)[:, 2 * k:2 * k + 2, :]).then_inc(up_in[k], 16)
            sp.dma_start(gate_raw, gate_w.rearrange("(c p) e -> p c e", p=P)).then_inc(gate_in, 16)
            sp.wait_ge(ring_full, 16)
            sp.dma_start(raw(DN_0 + 1, 10), down_w.rearrange("(c p) m -> p c m", p=P)[:, 0:10, :]).then_inc(down_in, 16)
            sp.wait_ge(pad_ready, 1)
            for part in range(2):
                sp.dma_start(k_dram.ap()[part, :, 0:P], kpad0[0:H, :]).then_inc(k_out, 16)
            sp.wait_ge(k_split, 2)
            for part, k in enumerate((k_hi, k_lo)):
                sp.dma_start(bass.AP(k_dram, part * H * KPAD + P, [[R, R], [KPAD, H], [1, R]]), k).then_inc(k_out, 16)
            sp.wait_ge(k_out, 64)
            sp.wait_ge(down_in, 16)

        @block.gpsimd
        def _(pool):
            pool.memset(id32[:, :], 0.0).then_inc(consts, 1)
            pool.wait_ge(consts, 1)
            pool.affine_select(out=id32[:, :], in_=id32[:, :], compare_op=ALU.not_equal, fill=1.0, base=0,
                               pattern=[[-1, P]], channel_multiplier=1).then_inc(consts, 1)
            pool.memset(ones32[:, :], 1.0).then_inc(consts, 1)
            pool.memset(ones16[:, :], 1.0).then_inc(consts, 1)
            pool.wait_ge(consts, 2)
            pool.tensor_copy(id16[:, :], id32[:, :]).then_inc(consts, 1)
            pool.iota(count[:, :], pattern=[[1, R]], base=0, channel_multiplier=0,
                      allow_small_or_imprecise_dtypes=True).then_inc(consts_a, 1)
            pool.memset(kpad0, 0.0).then_inc(pad_ready, 1)

        @block.scalar
        def _(act):
            for u in range(8):
                act.wait_ge(ring_full, u + 1)
                act.activation(fc1T[:, u // 2, u % 2 * 512:u % 2 * 512 + 512], ring[:, u % 2, :],
                               ACT.Copy).then_inc(ring_free, 1)
            act.wait_ge(sines_asked, 1)
            act.activation(sin_w, turns, ACT.Sin, scale=TWO_PI).then_inc(sines_done, 1)
            act.activation(sin_h, fhalf, ACT.Sin, scale=TWO_PI).then_inc(sines_done, 1)

            def table(n, func, t, scale=1.0):
                act.wait_ge(table_asked, n)
                act.activation(t[:, :, :], t[:, :, :], func, scale=scale).then_inc(table_done, 1)

            def up_square(j):
                if j % 4 == 0:
                    act.wait_ge(up_in[j // 4], 16)
                if j >= 2:
                    act.wait_ge(up_sq_used, j - 1)
                act.activation(up_sq[:, j % 2, :], raw(UP_0 + 1 + j)[:, 0, :], ACT.Square).then_inc(up_sq_ready, 1)

            for k in range(KT):
                u = 8 + k
                act.wait_ge(ring_full, u + 1)
                if k >= 2:
                    act.wait_ge(w1_sq_used, k - 1)
                act.activation(w1_sq[:, k % 2, :], ring[:, u % 2, :], ACT.Square).then_inc(w1_sq_ready, 1)
                act.activation(raw(W1_0 + 1 + k // 2)[:, 0, k % 2 * 512:k % 2 * 512 + 512], ring[:, u % 2, :],
                               ACT.Copy).then_inc(ring_free, 1)
                up_square(k)
            table(1, ACT.Sin, big[0], TWO_PI)
            table(2, ACT.Exp, big[1])
            table(3, ACT.Sin, big[3], TWO_PI)
            table(4, ACT.Sin, big[4], TWO_PI)
            table(5, ACT.Exp, big[2])
            for j in range(KT, 2 * KT):
                up_square(j)
            for g in range(4):
                u = 16 + g
                act.wait_ge(ring_full, u + 1)
                act.activation(kf[:, 16 * g:16 * g + 16, :], ring[0:R, u % 2, :].rearrange("p (h r) -> p h r", r=R),
                               ACT.Copy).then_inc(ring_free, 1)
            act.wait_ge(k_scaled, 1)
            act.activation(k_hi, k_sc, ACT.Copy).then_inc(k_split, 1)
            for j in range(W1_0):
                act.wait_ge(w_scaled, 1)
                if j:
                    act.wait_ge(piece_lo, j)
                act.activation(W[:, j, 0:L], raw(j + 1)[:, 0, :], ACT.Copy, scale=s_fc2).then_inc(piece_hi, 1)
            act.wait_ge(gate_scaled, 1)
            act.activation(gate[:, :, 0:NE], gate_raw, ACT.Copy, scale=s_gate).then_inc(gate_hi, 1)

        @block.tensor
        def _(pe):
            pe.wait_ge(consts, 5)
            pe.wait_ge(fc1_in, 16)
            for u in range(8):
                if u >= 2:
                    pe.wait_ge(ring_free, u - 1)
                for k in range(4):
                    c = u % 2 * 4 + k
                    ins = pe.transpose(ring[:, u % 2, k * P:k * P + P], fc1_sb[:, c, u // 2 * P:u // 2 * P + P], id32[:, :])
                ins.then_inc(ring_full, 1)
            pe.wait_ge(z_ready, 1)
            for z in range(4):
                ins = pe.transpose(z_ps[:, z, :], z_rows[:, z, :], id32[0:H, 0:H])
            ins.then_inc(z_turned, 1)
            pe.wait_ge(expert_in, 16)
            pe.wait_ge(ring_free, 8)

            def w1_colsum(k):
                pe.wait_ge(w1_sq_ready, k + 1)
                pe.matmul(w1_sum[:, :], ones16[:, :], w1_sq[:, k % 2, :], start=(k == 0),
                          stop=(k == KT - 1)).then_inc(w1_sq_used, 1)

            def up_colsum(j):
                pe.wait_ge(up_sq_ready, j + 1)
                for k in range(2):
                    ins = pe.matmul(up_sum[:, j % 2 * 2 + k, :], ones16[:, :], up_sq[:, j % 2, k * 512:k * 512 + 512],
                                    start=(j < 2), stop=(j >= 2 * KT - 2))
                ins.then_inc(up_sq_used, 1)

            def colsums(k):
                w1_colsum(k)
                up_colsum(k)

            for k in range(KT):
                u = 8 + k
                pe.wait_ge(ring_free, u - 1)
                for c in range(CL):
                    ins = pe.matmul(ring[:, u % 2, :], fc1T[:, c, k * P:k * P + P], expert_sb[:, c, :],
                                    start=(c == 0), stop=(c == CL - 1))
                ins.then_inc(ring_full, 1)
                if k:
                    colsums(k - 1)
            colsums(KT - 1)
            pe.wait_ge(sums_in, 2)
            pe.matmul(fc2_ps, ones32[:, :], fc2_max, start=True, stop=True)
            pe.matmul(gate_ps, ones32[:, :], gate_sq, start=True, stop=True).then_inc(sums_out, 1)
            for j in range(KT, 2 * KT):
                up_colsum(j)
            pe.wait_ge(tables, 2)
            for g in range(4):
                u = 16 + g
                pe.wait_ge(ring_free, u - 1)
                for k in range(16):
                    h = 16 * g + k
                    ins = pe.matmul(ring[0:R, u % 2, k * R:k * R + R], big[3][:, h, :], big[0][:, h, :],
                                    start=True, stop=True)
                ins.then_inc(ring_full, 1)
            pe.wait_ge(sums_in, 3)
            pe.matmul(sk_ps, ones32[0:R, :], abs_sum, start=True, stop=True).then_inc(sums_out, 1)

        @block.vector
        def _(dve):
            chain = Chain(dve, dve_c)
            link = chain.link

            def expm1_parts(v, n):
                a, b, c, qq, pp = t0[:, 0:n], t1[:, 0:n], t2[:, 0:n], q[:, 0:n], p2[:, 0:n]
                link(dve.tensor_scalar(a, v, 1.0 / math.log(2.0), MAGIC, ALU.mult, ALU.add))
                link(dve.tensor_scalar(a, a, MAGIC, None, ALU.subtract))
                link(dve.scalar_tensor_tensor(out=b, in0=a, scalar=-0.693359375, in1=v, op0=ALU.mult, op1=ALU.add))
                link(dve.scalar_tensor_tensor(out=b, in0=a, scalar=2.12194440e-4, in1=b, op0=ALU.mult, op1=ALU.add))
                link(dve.tensor_scalar(qq, b, 1.0 / math.factorial(8), None, ALU.mult))
                for k in range(7, 0, -1):
                    link(dve.scalar_tensor_tensor(out=qq, in0=qq, scalar=1.0 / math.factorial(k), in1=b,
                                                  op0=ALU.add, op1=ALU.mult))
                link(dve.tensor_scalar(a, a, -126.0, 127.0, ALU.max, ALU.min))
                link(dve.tensor_scalar(pp.bitcast(I32), a, 127.0, 2.0 ** 23, ALU.add, ALU.mult))
                link(dve.tensor_tensor(c, pp, qq, ALU.mult))
                return c, pp

            def tt(o, a, b, op):
                link(dve.tensor_tensor(o, a, b, op))

            def to_fraction(o, a, k):
                link(dve.tensor_scalar(k, a, MAGIC, MAGIC, ALU.add, ALU.subtract))
                tt(o, a, k, ALU.subtract)

            dve.wait_ge(cond_in, 80)
            c, pp = expm1_parts(logs, N + 1)
            tt(ex, c, pp, ALU.add)
            ea, dt = ex[:, 0:N], ex[:, N:N + 1]
            link(dve.tensor_scalar(alpha, ea, dt, -1.0, ALU.mult, ALU.mult))
            link(dve.tensor_scalar(w_im, aim, dt, None, ALU.mult))
            link(dve.tensor_scalar(u0, w_im, 1.0 / (2.0 * math.pi), None, ALU.mult))
            to_fraction(turns, u0, u1)
            link(dve.tensor_scalar(u0, w_im, 1.0 / (4.0 * math.pi), None, ALU.mult))
            link(dve.tensor_scalar(u1, u0, MAGIC, MAGIC, ALU.add, ALU.subtract))
            dve.tensor_tensor(fhalf, u0, u1, ALU.subtract).then_inc(sines_asked, 1)
            c, pp = expm1_parts(alpha, N)
            link(dve.scalar_tensor_tensor(out=s_re, in0=pp, scalar=-1.0, in1=c, op0=ALU.add, op1=ALU.add))
            tt(s_im, c, pp, ALU.add)
            dve.wait_ge(sines_done, 2)
            tt(e_im, s_im, sin_w, ALU.mult)
            tt(u0, s_im, sin_h, ALU.mult)
            tt(u0, u0, sin_h, ALU.mult)
            link(dve.scalar_tensor_tensor(out=e_re, in0=u0, scalar=-2.0, in1=s_re, op0=ALU.mult, op1=ALU.add))
            tt(u0, ea, ea, ALU.mult)
            tt(u1, aim, aim, ALU.mult)
            tt(u0, u0, u1, ALU.add)
            link(dve.reciprocal(inv, u0))
            tt(u0, e_im, aim, ALU.mult)
            tt(u1, e_re, ea, ALU.mult)
            tt(u0, u0, u1, ALU.subtract)
            tt(f_re, u0, inv, ALU.mult)
            tt(u0, e_re, aim, ALU.mult)
            tt(u1, e_im, ea, ALU.mult)
            tt(u0, u0, u1, ALU.add)
            link(dve.scalar_tensor_tensor(out=f_im, in0=u0, scalar=-1.0, in1=inv, op0=ALU.mult, op1=ALU.mult))
            cc = C_sb.rearrange("p (n c) -> p n c", c=2)
            tt(u0, f_re, cc[:, :, 0], ALU.mult)
            tt(u1, f_im, cc[:, :, 1], ALU.mult)
            tt(s_re, u0, u1, ALU.subtract)
            tt(u0, f_im, cc[:, :, 0], ALU.mult)
            tt(u1, f_re, cc[:, :, 1], ALU.mult)
            tt(s_im, u0, u1, ALU.add)
            for z, (a, fa, b, fb) in enumerate(((alpha, 1.0, alpha, 1.0), (turns, 1.0, turns, 1.0),
                                                (s_re, 2.0, s_im, -2.0), (s_im, -2.0, s_re, -2.0))):
                link(dve.tensor_scalar(z_rows[:, z, 0:N], a, fa, None, ALU.mult))
                link(dve.tensor_scalar(z_rows[:, z, N:2 * N], b, fb, None, ALU.mult))
            dve.memset(half[0:N, :], 0.25).then_inc(z_ready, 1)
            link(dve.memset(half[N:P, :], 0.0))
            dve.wait_ge(z_turned, 1)
            link(dve.tensor_copy(z_cols[:, :, :], z_ps))
            dve.wait_ge(consts_a, 1)

            def wide(col):
                return col.unsqueeze(2).to_broadcast([P, H, R])

            def steps(row):
                return row.unsqueeze(1).to_broadcast([P, H, R])

            t_alpha, t_turns, p1, pq = (z_cols[:, z, :] for z in range(4))
            b0, b1, b2, b3, b4 = (b_[:, :, :] for b_ in big)
            tt(b0, wide(t_turns), steps(count[:, :]), ALU.mult)
            link(dve.tensor_scalar(b0, b0, half[:, 0:1], None, ALU.add))
            link(dve.tensor_scalar(b1, b0, MAGIC, MAGIC, ALU.add, ALU.subtract))
            dve.tensor_tensor(b0, b0, b1, ALU.subtract).then_inc(table_asked, 1)
            dve.wait_ge(table_asked, 1)
            dve.tensor_tensor(b1, wide(t_alpha), steps(count[:, :]), ALU.mult).then_inc(table_asked, 1)
            link(dve.tensor_scalar(t_turns, t_turns, float(R), None, ALU.mult))
            link(dve.tensor_scalar(b2[:, :, 0], t_turns, MAGIC, MAGIC, ALU.add, ALU.subtract))
            tt(t_turns, t_turns, b2[:, :, 0], ALU.subtract)
            link(dve.tensor_scalar(t_alpha, t_alpha, float(R), None, ALU.mult))
            tt(b2, wide(t_turns), steps(count[:, :]), ALU.mult)
            link(dve.tensor_scalar(b3, b2, MAGIC, MAGIC, ALU.add, ALU.subtract))
            dve.tensor_tensor(b3, b2, b3, ALU.subtract).then_inc(table_asked, 1)
            dve.wait_ge(table_asked, 3)
            link(dve.tensor_scalar(b2, b2, 0.25, None, ALU.add))
            link(dve.tensor_scalar(b4, b2, MAGIC, MAGIC, ALU.add, ALU.subtract))
            dve.tensor_tensor(b4, b2, b4, ALU.subtract).then_inc(table_asked, 1)
            dve.wait_ge(table_asked, 4)
            dve.tensor_tensor(b2, wide(t_alpha), steps(count[:, :]), ALU.mult).then_inc(table_asked, 1)
            dve.wait_ge(fc2_in, 16)
            dve.tensor_reduce(fc2_max, raw(FC2_0 + 1, CL), AX.XY, ALU.max, apply_absolute_value=True).then_inc(sums_in, 1)
            dve.wait_ge(gate_in, 16)
            gate_in_sb = gate_raw.rearrange("p k e -> p (k e)")
            dve.tensor_tensor(gate_sq, gate_in_sb, gate_in_sb, ALU.mult).then_inc(sums_in, 1)
            dve.wait_ge(table_done, 2)
            dve.tensor_tensor(b0, b0, b1, ALU.mult).then_inc(tables, 1)
            dve.wait_ge(table_done, 5)
            tt(b3, b3, wide(pq), ALU.mult)
            tt(b4, b4, wide(p1), ALU.mult)
            tt(b3, b3, b4, ALU.add)
            dve.tensor_tensor(b3, b3, b2, ALU.mult).then_inc(tables, 1)
            dve.wait_ge(ring_free, 20)
            link(dve.tensor_tensor(kf[0:1, :, 0], kf[0:1, :, 0], d_row[:, :], ALU.add))
            dve.tensor_reduce(abs_sum, kf, AX.X, ALU.add, apply_absolute_value=True).then_inc(sums_in, 1)
            dve.wait_ge(sums_out, 2)
            power_scale(dve, link, sk, sk_ps, 2.0 ** 14)
            dve.tensor_tensor(k_sc, kf, sk[0:R, :].unsqueeze(2).to_broadcast([R, H, R]), ALU.mult).then_inc(k_scaled, 1)
            sk2 = sk.rearrange("p (t j) -> p t j", j=2)
            link(dve.tensor_scalar(pair_scale[0:B, :], sk2[0:B, :, 0], 2.0 ** -15, None, ALU.mult))
            link(dve.tensor_scalar(pair_scale[B:P, :], sk2[B:P, :, 1], 2.0 ** -15, None, ALU.mult))
            dve.wait_ge(k_split, 1)
            dve.wait_ge(k_scaled, 1)
            dve.tensor_tensor(k_lo, k_sc, k_hi, ALU.subtract).then_inc(k_split, 1)
            dve.wait_ge(sums_out, 1)
            power_scale(dve, link, s_fc2, fc2_ps, 2.0 ** 14)
            dve.sem_inc(w_scaled, 1)
            dve.wait_ge(w1_sq_used, KT)
            link(dve.tensor_reduce(bound[:, 1:2], w1_sum[:, :], AX.X, ALU.max))
            norm_scale(dve, link, s_w1, bound[:, 1:2], 2.0 ** 14)
            dve.sem_inc(w_scaled, 1)
            link(dve.tensor_reduce(gate_sum, gate_ps.rearrange("p (k e) -> p e k", e=NE), AX.X, ALU.add))
            link(dve.tensor_reduce(gate_hl, gate_sum, AX.X, ALU.max))
            norm_scale(dve, link, s_gate, gate_hl, 2.0 ** 14)
            dve.sem_inc(gate_scaled, 1)
            dve.wait_ge(up_sq_used, 2 * KT)
            link(dve.tensor_reduce(bound[:, 2:3], up_sum[:, :, :], AX.XY, ALU.max))
            norm_scale(dve, link, s_up, bound[:, 2:3], 2.0 ** 14)
            for j in range(W1_0):
                dve.wait_ge(piece_hi, j + 1)
                dve.scalar_tensor_tensor(out=W[:, j, L:2 * L], in0=raw(j + 1)[:, 0, :], scalar=s_fc2,
                                         in1=W[:, j, 0:L], op0=ALU.mult, op1=ALU.subtract).then_inc(piece_lo, 1)
            dve.wait_ge(gate_hi, 1)
            link(dve.scalar_tensor_tensor(out=gate[:, :, NE:2 * NE], in0=gate_raw, scalar=s_gate, in1=gate[:, :, 0:NE],
                                          op0=ALU.mult, op1=ALU.subtract))


def conv(nc, W, raw, id16, ones16, pair_scale, rho, energy, s_up, s_w1, s_down, k_dram, hid_dram, x, itok, down_w):
    EARLY = 10
    with ExitStack() as ctx:
        def sb(name, shape, dt):
            return ctx.enter_context(nc.sbuf_tensor(name, shape, dt))

        def psum(name, shape, dt=F32):
            return ctx.enter_context(nc.psum_tensor(name, shape, dt))

        def sem(name):
            return ctx.enter_context(nc.semaphore(name))

        x_mask = sb("x_mask", [P, L], BF16)
        mask = sb("mask", [P, KT, B], U8)
        len_col = sb("len_col", [P, 1], F32)
        xn = sb("xn", [P, 2, L], F32)
        x_hl = sb("x_hl", [P, 2, KT, P], F16)
        uT = sb("uT", [P, 2, 2, KT, P], F16)
        slab = sb("slab", [P, 2, 2, L], F16)
        hid32 = sb("hid32", [P, 2, KT, B], F32)
        hid = sb("hid", [P, 2, 2, KT, P], F16)
        time_row = uT[:, 1, 0, :, :].rearrange("p k m -> p (k m)").bitcast(I16)
        position, len_row = hid32[:, 0, :, :].bitcast(I32), hid32[:, 1, 0, :].bitcast(I32)
        len_i = hid32[:, 1, 1, 0:1].bitcast(I32)
        amax = sb("amax", [P, 2], F32)
        tau = sb("tau", [P, 2], F32)
        down_sq = sb("down_sq", [P, CI], F32)
        down_row = sb("down_row", [P, 1], BF16)

        turned = [psum(f"turned{k}", [P, KT, P], F16) for k in range(2)]
        conv_ps = [psum(f"conv_ps{j}", [P, KT, B]) for j in range(2)]
        gram_diag = psum("gram_diag", [P, 512])[:, 0:P]
        squares = psum("squares", [P, L])
        sum_ps = squares[:, 0:1]
        gram_ps = psum("gram_ps", [P, 512])[:, 0:P]

        len_in, down_in = sem("len_in"), sem("down_in")
        x_in = [sem(f"x_in{b}") for b in range(2)]
        slab_in = [sem(f"slab_in{j}") for j in range(2)]
        stored = [sem(f"stored{b}") for b in range(2)]
        iotas = sem("iotas")
        dve_c = sem("dve_chain2")
        tau_ready, x_hi, x_lo, x_turned, u_ready = map(sem, ("tau_ready", "x_hi", "x_lo", "x_turned", "u_ready"))
        convolved, masked, hid_hi, hid_lo = map(sem, ("convolved", "masked", "hid_hi", "hid_lo"))
        piece_hi, piece_lo = sem("piece_hi2"), sem("piece_lo2")
        rows_squared, down_summed = sem("rows_squared"), sem("down_summed")
        piece_squared, x_masked, x_mask_ready = map(sem, ("piece_squared", "x_masked", "x_mask_ready"))
        w1_hi, w1_lo, gram_done, gram_used = map(sem, ("w1_hi", "w1_lo", "gram_done", "gram_used"))
        down_scaled = sem("down_scaled")

        block = ctx.enter_context(nc.Block())
        LOOP1, LOOP2 = (1, 9), (9, PAIRS // 2)

        def backwards(part):
            return bass.AP(x_hl, part * L + P - 1, [[2 * L, P], [P, KT], [-1, P]])

        def chunks(rows):
            return rows.rearrange("p (k m) -> p k m", k=KT)

        def x_rows(t, j):
            return x[:, bass.ds(2 * t + j, 1), :].rearrange("b o l -> (b o) l")

        @block.sync
        def _(sp):
            def load_x(t, b):
                for j in range(2):
                    sp.dma_start(xn[j * B:j * B + B, b, :], x_rows(t, j)).then_inc(x_in[b], 16)

            def load_slab(t, j):
                src = bass.AP(k_dram, (2 * t + j) * KPAD + 1, [[1, P], [H * KPAD, 2], [1, L]])
                sp.dma_start(slab[:, j, :, :], src).then_inc(slab_in[j], 16)

            def store(t, b):
                sp.wait_ge(hid_lo, 1 + 2 * t + 2)
                sp.dma_start(hid_dram.ap()[bass.ds(t, 1), :, :, :, :].rearrange("o p a k m -> p (o a k m)"),
                             hid[:, b, :, :, :].rearrange("p a k m -> p (a k m)")).then_inc(stored[b], 16)

            def step(t, b, more=True):
                if more:
                    sp.wait_ge(x_lo, t + 1)
                    load_x(t + 2, b)
                sp.wait_ge(convolved, 2 * t - 2)
                load_slab(t - 1, 1)
                store(t - 2, b)
                sp.wait_ge(convolved, 2 * t - 1)
                load_slab(t, 0)

            for b in range(2):
                sp.sem_inc(stored[b], 16)
            load_x(0, 0)
            load_x(1, 1)
            load_slab(0, 0)
            load_slab(0, 1)
            for t in range(2):
                sp.wait_ge(x_lo, t + 1)
                load_x(t + 2, t)
            sp.wait_ge(convolved, 1)
            load_slab(1, 0)
            with sp.Fori(1, PAIRS // 2 - 1) as i:
                for b in range(2):
                    step(2 * i + b, b)
            step(PAIRS - 2, 0, more=False)
            step(PAIRS - 1, 1, more=False)
            sp.wait_ge(convolved, 2 * PAIRS - 2)
            load_slab(PAIRS - 1, 1)
            store(PAIRS - 2, 0)
            store(PAIRS - 1, 1)
            for b in range(2):
                sp.wait_ge(stored[b], 16 + 16 * (PAIRS // 2))

        @block.gpsimd
        def _(pool):
            start_at_one(pool, hid_lo)
            pool.iota(time_row, pattern=[[1, L]], base=0, channel_multiplier=0).then_inc(iotas, 1)
            pool.iota(position, pattern=[[P, KT], [0, B]], base=0,
                      channel_multiplier=1).then_inc(iotas, 1)

            def mask_x(t, b, i):
                pool.wait_ge(x_in[b], 32 * i + 32)
                pool.tensor_tensor(xn[:, b, :], xn[:, b, :], x_mask[:, :], ALU.mult).then_inc(x_masked, 1)

            def low_half(t, b, j):
                pool.wait_ge(hid_hi, 2 * t + j + 1)
                cols = hid[:, b, :, :, j * B:j * B + B]
                pool.tensor_tensor(cols[:, 1], hid32[:, j, :, :], cols[:, 0], ALU.subtract).then_inc(hid_lo, 1)

            def step(t, b, i):
                if i is not None:
                    mask_x(t + 1, 1 - b, i + b)
                low_half(t - 2, b, 0)
                low_half(t - 2, b, 1)

            pool.wait_ge(x_mask_ready, 1)
            mask_x(0, 0, 0)
            mask_x(1, 1, 0)
            mask_x(2, 0, 1)
            with pool.Fori(1, PAIRS // 2 - 1) as i:
                for b in range(2):
                    step(2 * i + b, b, i)
            step(PAIRS - 2, 0, PAIRS // 2 - 1)
            for t in range(PAIRS - 1, PAIRS + 2):
                step(t, t % 2, None)

        @block.scalar
        def _(act):
            for j in range(2):
                act.dma_start(len_i[j * B:j * B + B, :], itok.rearrange("(b o) -> b o", o=1)).then_inc(len_in, 16)
            act.dma_start(len_row, itok.rearrange("(o b) -> o b", o=1).to_broadcast([P, B])).then_inc(len_in, 16)
            act.dma_start(raw(DN_0 + 1 + EARLY, CI - EARLY),
                          down_w.rearrange("(c p) m -> p c m", p=P)[:, EARLY:CI, :]).then_inc(down_in, 16)

            def x_high(t, b):
                act.wait_ge(tau_ready, t + 1)
                if not first(t):
                    act.wait_ge(x_turned, t)
                act.activation(backwards(0), chunks(xn[:, b, :]), ACT.Copy, scale=tau[:, b:b + 1]).then_inc(x_hi, 1)

            def piece_high(t, scale):
                act.wait_ge(piece_lo, 1 + t - 2)
                j = UP_0 + t - 2
                act.activation(W[:, bass.ds(j, 1), 0:L], W[:, bass.ds(j + 1, 1), :].bitcast(F32), ACT.Copy,
                               scale=scale).then_inc(piece_hi, 1)

            def hid_high(t, b, j):
                act.wait_ge(masked, 2 * t + j + 1)
                act.activation(hid[:, b, 0, :, j * B:j * B + B], hid32[:, j, :, :], ACT.Copy).then_inc(hid_hi, 1)

            def u_copy(t, b):
                act.wait_ge(x_turned, t + 1)
                for k in range(2):
                    act.activation(uT[:, b, k, :, :], turned[k][:, :, :], ACT.Copy).then_inc(u_ready, 1)

            x_high(0, 0)
            u_copy(0, 0)
            x_high(1, 1)
            u_copy(1, 1)
            for j in range(W1_0, UP_0):
                if j > W1_0:
                    act.wait_ge(w1_lo, j - W1_0)
                act.activation(W[:, j, 0:L], raw(j + 1)[:, 0, :], ACT.Copy, scale=s_w1).then_inc(w1_hi, 1)
            for (lo, hi), scale in ((LOOP1, s_up), (LOOP2, s_down)):
                act.wait_ge(*((down_in, 16) if scale is s_up else (down_scaled, 1)))
                with act.Fori(lo, hi) as i:
                    for b in range(2):
                        t = 2 * i + b
                        x_high(t, b)
                        act.wait_ge(stored[b], 16 + 16 * i - 16)
                        act.wait_ge(gram_done, 2 + t - 3)
                        hid_high(t - 2, b, 0)
                        piece_high(t, scale)
                        if scale is s_up:
                            act.activation(squares[:, :], W[:, bass.ds(DN_0 + 1 + t - 2, 1), :].bitcast(F32), ACT.Square,
                                           accum_out=down_sq[:, bass.ds(t - 2, 1)]).then_inc(piece_squared, 1)
                        hid_high(t - 2, b, 1)
                        act.wait_ge(convolved, 2 * t - 2)
                        u_copy(t, b)
            for b in range(2):
                t = PAIRS + b
                piece_high(t, s_down)
                act.wait_ge(stored[b], 16 + 16 * (PAIRS // 2 - 1))
                act.wait_ge(gram_done, 2 + t - 3)
                for j in range(2):
                    hid_high(t - 2, b, j)

        @block.tensor
        def _(pe):
            def turn(t):
                pe.wait_ge(x_lo, t + 1)
                if not first(t):
                    pe.wait_ge(u_ready, 2 * t)
                for k in range(2):
                    for c in range(KT):
                        ins = pe.transpose(turned[k][:, c, :], x_hl[:, k, c, :], id16[:, :])
                ins.then_inc(x_turned, 1)

            def gram(t, b):
                pe.wait_ge(hid_hi, 2 * t + 2)
                pe.wait_ge(gram_used, 1 + t)
                for c in range(KT):
                    ins = pe.matmul(gram_ps, hid[:, b, 0, c, :], hid[:, b, 0, c, :], start=(c == 0), stop=(c == KT - 1))
                ins.then_inc(gram_done, 1)

            def convolve(t, b, before=True):
                pe.wait_ge(u_ready, 2 * t + 2)
                for j in range(2):
                    pe.wait_ge(slab_in[j], 16 * t + 16)
                    if not first(t):
                        pe.wait_ge(masked, 2 * t - 1 + j)
                    for d in range(KT):
                        for ks, ku in ((0, 0), (0, 1), (1, 0)):
                            c0 = d * P
                            ins = pe.matmul(conv_ps[j][:, d:KT, :], slab[:, j, ks, c0:c0 + P],
                                            uT[:, b, ku, 0:KT - d, j * B:j * B + B],
                                            start=(d == ks == ku == 0), stop=(d == KT - 1 and ks == 1))
                        if before and j == d == 0:
                            gram(t - 1, 1 - b)
                    ins.then_inc(convolved, 1)

            start_at_one(pe, gram_used, gram_done)
            turn(0)
            turn(1)
            convolve(0, 0, before=False)
            for n, (lo, hi) in enumerate((LOOP1, LOOP2)):
                if n:
                    pe.wait_ge(rows_squared, 1)
                    pe.matmul(sum_ps, ones16[:, :], down_row[:, :], start=True, stop=True).then_inc(down_summed, 1)
                with pe.Fori(lo, hi) as i:
                    for b in range(2):
                        t = 2 * i + b
                        turn(t)
                        convolve(t - 1, 1 - b)
            convolve(PAIRS - 1, 1)
            gram(PAIRS - 1, 1)

        @block.vector
        def _(dve):
            chain = Chain(dve, dve_c)
            link = chain.link
            dve.wait_ge(len_in, 48)
            dve.wait_ge(iotas, 2)
            link(dve.tensor_copy(len_col[:, :], len_i[:, :]))
            link(dve.tensor_tensor(mask[:, :, :], position, len_row.unsqueeze(1).to_broadcast([P, KT, B]), ALU.is_lt))
            dve.tensor_scalar(x_mask[:, :], time_row, len_col[:, 0:1], None, ALU.is_lt).then_inc(x_mask_ready, 1)

            def scale_x(t, b):
                dve.wait_ge(x_masked, t + 1)
                link(dve.tensor_reduce(amax[:, b:b + 1], xn[:, b, :], AX.X, ALU.max, apply_absolute_value=True))
                power_scale(dve, link, tau[:, b:b + 1], amax[:, b:b + 1], 2.0 ** 14)
                dve.tensor_tensor(rho[:, bass.ds(t, 1)], tau[:, b:b + 1], pair_scale[:, bass.ds(t, 1)],
                                  ALU.mult).then_inc(tau_ready, 1)

            def x_low(t, b):
                dve.wait_ge(x_hi, t + 1)
                dve.scalar_tensor_tensor(out=backwards(1), in0=chunks(xn[:, b, :]), scalar=tau[:, b:b + 1],
                                         in1=backwards(0), op0=ALU.mult, op1=ALU.subtract).then_inc(x_lo, 1)

            def mask_hid(t, j):
                dve.wait_ge(convolved, 2 * t + j + 1)
                if not first(t):
                    dve.wait_ge(hid_lo, 1 + 2 * t + j - 1)
                dve.scalar_tensor_tensor(out=hid32[:, j, :, :], in0=conv_ps[j][:, :, :], scalar=2.0 ** -15,
                                         in1=mask[:, :, :], op0=ALU.mult, op1=ALU.mult).then_inc(masked, 1)

            def token_energy(t):
                dve.wait_ge(gram_done, 1 + t + 1)
                link(dve.tensor_tensor(gram_diag, gram_ps, id16[:, :], ALU.mult))
                dve.tensor_reduce(energy[:, bass.ds(t, 1)], gram_diag, AX.X, ALU.add).then_inc(gram_used, 1)

            def piece_low(t, scale):
                dve.wait_ge(piece_hi, t - 1)
                j = UP_0 + t - 2
                dve.scalar_tensor_tensor(out=W[:, bass.ds(j, 1), L:2 * L], in0=W[:, bass.ds(j + 1, 1), :].bitcast(F32),
                                         scalar=scale, in1=W[:, bass.ds(j, 1), 0:L], op0=ALU.mult,
                                         op1=ALU.subtract).then_inc(piece_lo, 1)

            def step(t, b, scale, last=False):
                mask_hid(t - 2, 0)
                x_low(t, b)
                mask_hid(t - 2, 1)
                piece_low(t, scale)
                if not last:
                    scale_x(t + 1, 1 - b)
                token_energy(t - 2)

            start_at_one(dve, piece_lo)
            for t in range(2):
                scale_x(t, t)
                x_low(t, t)
            for j in range(W1_0, UP_0):
                dve.wait_ge(w1_hi, j - W1_0 + 1)
                dve.scalar_tensor_tensor(out=W[:, j, L:2 * L], in0=raw(j + 1)[:, 0, :], scalar=s_w1, in1=W[:, j, 0:L],
                                         op0=ALU.mult, op1=ALU.subtract).then_inc(w1_lo, 1)
            scale_x(2, 0)
            with dve.Fori(*LOOP1) as i:
                chain.loop(i - 1, 2 * 6)
                for b in range(2):
                    t = 2 * i + b
                    step(t, b, s_up)
            chain.end_loop(8)
            dve.wait_ge(piece_squared, CI)
            dve.tensor_reduce(down_row[:, :], down_sq[:, :], AX.X, ALU.max).then_inc(rows_squared, 1)
            dve.wait_ge(down_summed, 1)
            norm_scale(dve, link, s_down, sum_ps, 2.0 ** 14)
            dve.sem_inc(down_scaled, 1)
            with dve.Fori(LOOP2[0], LOOP2[1] - 1) as i:
                chain.loop(i - LOOP2[0], 2 * 6)
                for b in range(2):
                    step(2 * i + b, b, s_down)
            chain.end_loop(LOOP2[1] - 1 - LOOP2[0])
            step(PAIRS - 2, 0, s_down)
            step(PAIRS - 1, 1, s_down, last=True)
            for b in range(2):
                for j in range(2):
                    mask_hid(PAIRS - 2 + b, j)
                piece_low(PAIRS + b, s_down)
                token_energy(PAIRS - 2 + b)


def ffn(nc, W, raw, gate, id16, rho, energy, scales, hid_dram, relu_dram, x, ln_gamma, ln_beta, out):
    s_up, s_w1, s_gate, s_down, s_fc2 = (scales[:, k:k + 1] for k in range(5))
    TT = 2 * P
    HR = 4
    LAG = 3
    with ExitStack() as ctx:
        def sb(name, shape, dt):
            return ctx.enter_context(nc.sbuf_tensor(name, shape, dt))

        def psum(name, shape, dt=F32):
            return ctx.enter_context(nc.psum_tensor(name, shape, dt))

        def sem(name):
            return ctx.enter_context(nc.semaphore(name))

        hid = sb("hid_tile", [P, 2, 2, 2, KT, P], F16)
        h_hl = sb("h_hl", [P, HR, 2, TT], F16)
        r_buf = sb("r_buf", [P, 2, TT], F32)
        h32 = sb("h32", [P, 2, TT], F32)
        route = sb("route", [P, TT], F32)
        gamma = sb("gamma", [P, L], F32)
        beta = sb("beta", [P, L], F32)
        xr = sb("xr", [P, 2, L], F32)
        z = raw(PIECES)[:, 0, :].rearrange("p (b m) -> p b m", b=2)
        ones32 = sb("ones_f", [P, P], F32)
        theta = rho[:, :]
        k_route = energy[:, :]
        relu_scale = sb("relu_scale", [P, TT], BF16)
        tmp = sb("tmp", [P, 4], F32)
        g_lo, logits, top = (sb(name, [P, 2, NE], F32)[:, :, :] for name in ("g_lo", "logits", "top"))
        s_tok = sb("s_tok", [P, 2], F32)
        diag = route[:, :].rearrange("p (s m) -> p s m", s=2)
        stats = sb("stats", [P, 2, 6], F32)
        mv = sb("mv", [P, 2], F32)
        ln = sb("ln", [P, 6], F32)

        acc = psum("acc", [P, 2, 2, 512])
        up_ps = psum("up_ps", [P, 3, 512])
        route_bank = psum("route_bank", [P, 512])
        gate_ps = route_bank[:, 0:4 * NE].rearrange("p (s e) -> p s e", s=2)
        route_ps = route_bank[:, TT:2 * TT].rearrange("p (s m) -> p s m", s=2)
        nu_ps = up_ps[0:PAIRS, 2, TT:TT + P]
        nu, nu_rows = z[:, 0, 0:PAIRS], z[0:PAIRS, 0, 64:128].bitcast(BF16)
        nu16, id_bf = z[:, 0, 128:144].bitcast(BF16), z[:, 0, 192:256].bitcast(BF16)

        hid_in = [sem(f"hid_in{b}") for b in range(2)]
        xr_in = [sem(f"xr_in{s}") for s in range(2)]
        out_stored = [sem(f"out_stored{s}") for s in range(2)]
        ln_in, dve_c, consts = sem("ln_in"), sem("dve_chain3"), sem("consts3")
        up_done, up_free, h_hi, h_lo, down_done = map(
            sem, ("up_done", "up_free", "h_hi", "h_lo", "down_done"))
        gate_done, diag_ready, route_done, acc_done = map(sem, ("gate_done", "diag_ready", "route_done", "acc_done"))
        root_asked, root_done, norm_ready, z_done, z_scaled, z_added = map(
            sem, ("root_asked", "root_done", "norm_ready", "z_done", "z_scaled", "z_added"))
        xb_done, nu_ready, nu_turned, nu_copied, nu_stored, relu_scale_in, squared = map(
            sem, ("xb_done", "nu_ready", "nu_turned", "nu_copied", "nu_stored", "relu_scale_in", "squared3"))

        block = ctx.enter_context(nc.Block())

        def slot_of(c):
            return up_ps[:, c % 3, 0:TT]

        @block.sync
        def _(sp):
            def load_hid(T, b):
                for s in range(2):
                    sp.dma_start(hid[:, b, s, :, :, :].rearrange("p a k m -> p (a k m)"),
                                 hid_dram.ap()[bass.ds(2 * T + s, 1), :, :, :, :].rearrange("o p a k m -> p (o a k m)")
                                 ).then_inc(hid_in[b], 16)

            def load_x(T):
                for s in range(2):
                    if not first(T):
                        sp.wait_ge(out_stored[s], 32 * T)
                    for j in range(2):
                        sp.dma_start(xr[j * B:j * B + B, s, :],
                                     x[:, bass.ds(4 * T + 2 * s + j, 1), :].rearrange("b o l -> (b o) l")
                                     ).then_inc(xr_in[s], 16)

            def load_relu_scale(T):
                sp.wait_ge(up_free, 1 + T * NC - CL)
                sp.dma_start(relu_scale[:, :], bass.AP(relu_dram, T * TT, [[0, P], [1, TT]])).then_inc(relu_scale_in, 16)

            load_hid(0, 0)
            load_hid(1, 1)
            load_x(0)
            sp.wait_ge(nu_copied, 1)
            sp.dma_start(relu_dram.ap(), nu_rows).then_inc(nu_stored, 16)
            sp.wait_ge(nu_stored, 16)
            sp.dma_start(relu_scale[:, :], bass.AP(relu_dram, 0, [[0, P], [1, TT]])).then_inc(relu_scale_in, 16)
            load_relu_scale(1)
            with sp.Fori(1, TILES // 2) as i:
                for b in range(2):
                    T = 2 * i + b
                    sp.wait_ge(up_done, (T - 1) * NC)
                    load_hid(T, b)
                    load_x(T - 1)
                    load_relu_scale(T)
            load_x(TILES - 1)

        @block.gpsimd
        def _(pool):
            def low_half(T, c):
                if c < CI:
                    pool.wait_ge(squared, T * CI + c + 1)
                pool.wait_ge(h_hi, T * NC + c + 1)
                pool.tensor_tensor(h_hl[:, c % HR, 1, :], h32[:, c % 2, :], h_hl[:, c % HR, 0, :],
                                   ALU.subtract).then_inc(h_lo, 1)

            pool.memset(ones32[:, :], 1.0).then_inc(consts, 1)
            pool.wait_ge(ln_in, 32)
            with pool.Fori(0, TILES // 2) as i:
                for b in range(2):
                    T = 2 * i + b
                    for c in range(NC):
                        low_half(T, c)
                        if c in (9, 11):
                            s = (c - 9) // 2
                            pool.wait_ge(xr_in[s], 32 * T + 32)
                            pool.tensor_tensor(xr[:, s, :], xr[:, s, :], beta[:, :], ALU.add).then_inc(xb_done, 1)
                    for s in range(2):
                        for k in range(2):
                            n = 4 * T + 2 * s + k
                            pool.wait_ge(z_done, 1 + n + 1)
                            pool.tensor_tensor(z[:, k, :], z[:, k, :], gamma[:, k * 512:k * 512 + 512],
                                               ALU.mult).then_inc(z_scaled, 1)
                    for s in range(2):
                        pool.wait_ge(z_added, 1 + 4 * T + 2 * s + 2)
                        for j in range(2):
                            pool.dma_start(out[:, bass.ds(4 * T + 2 * s + j, 1), :].rearrange("b o l -> (b o) l"),
                                           xr[j * B:j * B + B, s, :]).then_inc(out_stored[s], 16)
            for s in range(2):
                pool.wait_ge(out_stored[s], 32 * TILES)

        @block.scalar
        def _(act):
            act.dma_start(gamma[:, :], ln_gamma.rearrange("(o l) -> o l", o=1).to_broadcast([P, L])).then_inc(ln_in, 16)
            act.dma_start(beta[:, :], ln_beta.rearrange("(o l) -> o l", o=1).to_broadcast([P, L])).then_inc(ln_in, 16)
            start_at_one(act, z_done)
            with act.Fori(0, TILES // 2) as i:
                for b in range(2):
                    T = 2 * i + b
                    for c in range(NC):
                        n = T * NC + c
                        act.wait_ge(up_free, 1 + n + 1)
                        if c < CI:
                            if c >= 2:
                                act.wait_ge(h_lo, n - 1)
                            act.activation(h32[:, c % 2, :], r_buf[:, c % 2, :], ACT.Square).then_inc(squared, 1)
                        act.wait_ge(down_done, 1 + T * NC + max(c + 1 - HR, 0))
                        if c < CI:
                            act.activation(h_hl[:, c % HR, 0, :], r_buf[:, c % 2, :], ACT.Square).then_inc(h_hi, 1)
                        else:
                            act.activation(h_hl[:, c % HR, 0, :], h32[:, c % 2, :], ACT.Copy).then_inc(h_hi, 1)
                    for s in range(2):
                        act.wait_ge(root_asked, 2 * T + s + 1)
                        act.activation(ln[:, 1:2], ln[:, 0:1], ACT.Sqrt).then_inc(root_done, 1)
                        act.wait_ge(norm_ready, 2 * T + s + 1)
                        for k in range(2):
                            act.wait_ge(z_added, 1 + 4 * T + (k + 1) * s)
                            act.activation(z[:, k, :], acc[:, s, k, :], ACT.Identity, bias=ln[:, 5:6],
                                           scale=ln[:, 4:5]).then_inc(z_done, 1)

        @block.tensor
        def _(pe):
            def three(o, stat, mov, first, last):
                for n, (a, m) in enumerate(((0, 0), (0, 1), (1, 0))):
                    ins = pe.matmul(o, stat[a], mov[m], start=(first and n == 0), stop=(last and n == 2))
                return ins

            def up(T, c, b):
                pe.wait_ge(up_free, 1 + T * NC + max(c - 2, 0))
                for k in range(KT):
                    if c < CI:
                        piece, col = UP_0 + 2 * k + c // 8, c % 8 * P
                    else:
                        piece, col = W1_0 + k // 2, k % 2 * LAT + (c - CI) * P
                    stat = [W[:, piece, a * L + col:a * L + col + P] for a in range(2)]
                    mov = [hid[:, b, :, a, k, :] for a in range(2)]
                    ins = three(slot_of(c), stat, mov, k == 0, k == KT - 1)
                ins.then_inc(up_done, 1)

            def down(T, c):
                pe.wait_ge(h_lo, T * NC + c + 1)
                piece = DN_0 + c if c < CI else FC2_0 + c - CI
                for s in range(2):
                    for k in range(2):
                        stat = [h_hl[:, c % HR, a, s * P:s * P + P] for a in range(2)]
                        mov = [W[:, piece, a * L + k * 512:a * L + k * 512 + 512] for a in range(2)]
                        ins = three(acc[:, s, k, :], stat, mov, c == 0, c == NC - 1)
                    if c == NC - 1 and s == 0:
                        ins.then_inc(acc_done, 1)
                ins.then_inc(down_done, 1)

            def gate_logits(T, b):
                pe.wait_ge(diag_ready, 1 + T)
                for s in range(2):
                    for k in range(KT):
                        for a in ((0, 1) if k == 0 else (1, 0)):
                            w = NE if a else 2 * NE
                            ins = pe.matmul(gate_ps[:, s, 0:w], hid[:, b, s, a, k, :], gate[:, k, 0:w],
                                            start=(k == a == 0), stop=(k == KT - 1 and a == 0), skip_group_check=bool(a))
                ins.then_inc(gate_done, 1)

            start_at_one(pe, down_done)
            pe.wait_ge(consts, 1)
            pe.wait_ge(nu_ready, 1)
            pe.matmul(nu_ps, nu16, id_bf, start=True, stop=True).then_inc(nu_turned, 1)
            pe.wait_ge(nu_copied, 1)
            with pe.Fori(0, TILES // 2) as i:
                for b in range(2):
                    T = 2 * i + b
                    pe.wait_ge(hid_in[b], 32 * i + 32)
                    gate_logits(T, b)
                    for c in range(NC):
                        up(T, c, b)
                        if c == 2:
                            pe.wait_ge(diag_ready, 1 + T + 1)
                            for s in range(2):
                                ins = pe.matmul(route_ps[:, s, :], ones32[:, :], diag[:, s, :], start=True, stop=True)
                            ins.then_inc(route_done, 1)
                        if c == LAG:
                            pe.wait_ge(z_done, 1 + 4 * T)
                        if c >= LAG:
                            down(T, c - LAG)
                    for c in range(NC - LAG, NC):
                        down(T, c)

        @block.vector
        def _(dve):
            chain = Chain(dve, dve_c)
            link = chain.link

            def tt(o, a, b_, op):
                link(dve.tensor_tensor(o, a, b_, op))

            start_at_one(dve, up_free, diag_ready, z_added)
            root, q = tmp[:, 0:1], tmp[:, 1:2]
            tt(tmp[:, 2:3], s_w1, s_gate, ALU.mult)
            tt(tmp[:, 2:3], tmp[:, 2:3], s_fc2, ALU.mult)
            link(dve.reciprocal(q, tmp[:, 2:3]))
            for factor in (s_up, s_down, s_up):
                tt(q, q, factor, ALU.mult)
            link(dve.tensor_scalar(q, q, 2.0 ** -60, 2.0 ** 60, ALU.max, ALU.min))
            link(dve.reciprocal(tmp[:, 2:3], q))
            link(dve.tensor_scalar(tmp[:, 2:3], tmp[:, 2:3], 1.0, None, ALU.min))
            root_power(dve, link, root, tmp[:, 2:3], 2.0 ** -100)
            link(dve.tensor_scalar(root, root, 2.0 ** -8, None, ALU.mult))
            norm_scale(dve, link, k_route, energy[:, :], 0.5, TINY)
            link(dve.tensor_scalar(nu, k_route, root, None, ALU.mult))
            link(dve.tensor_copy(id_bf, id16[:, :]))
            dve.tensor_copy(nu16, nu).then_inc(nu_ready, 1)
            dve.wait_ge(nu_turned, 1)
            dve.tensor_copy(nu_rows, nu_ps).then_inc(nu_copied, 1)
            tt(theta, theta, nu, ALU.mult)
            tt(theta, theta, theta, ALU.mult)
            for factor in (s_up, s_down, s_up):
                link(dve.tensor_scalar(theta, theta, factor, 2.0 ** 62, ALU.mult, ALU.min))
            link(dve.scalar_tensor_tensor(out=theta, in0=theta, scalar=LN_EPS, in1=theta,
                                          op0=ALU.mult, op1=ALU.mult))
            tt(k_route, nu, nu, ALU.mult)
            link(dve.tensor_scalar(k_route, k_route, q, None, ALU.mult))

            def carry_wait():
                dve.tensor_copy(tmp[0:1, 3:4], tmp[0:1, 2:3])

            def route_weights(T):
                dve.wait_ge(gate_done, T + 1)
                link(dve.tensor_copy(g_lo, gate_ps[:, :, NE:2 * NE]))
                tt(logits, gate_ps[:, :, 0:NE], g_lo, ALU.add)
                carry_wait()
                dve.max(top[:, 0, :], logits[:, 0, :])
                link(dve.max(top[:, 1, :], logits[:, 1, :]))
                tt(s_tok[:, :], top[:, :, 0], top[:, :, 1], ALU.add)
                for s in range(2):
                    link(dve.tensor_scalar(diag[:, s, :], id16[:, :], s_tok[:, s:s + 1], k_route[:, bass.ds(2 * T + s, 1)],
                                           ALU.mult, ALU.mult))
                dve.sem_inc(diag_ready, 1)

            def evacuate(T, c):
                n = T * NC + c
                dve.wait_ge(up_done, n + 1)
                if c < CI:
                    dve.scalar_tensor_tensor(out=r_buf[:, c % 2, :], in0=slot_of(c), scalar=0.0, in1=relu_scale[:, :],
                                             op0=ALU.max, op1=ALU.mult).then_inc(up_free, 1)
                else:
                    dve.tensor_tensor(h32[:, c % 2, :], slot_of(c), route[:, :], ALU.mult).then_inc(up_free, 1)

            def layernorm(T, s):
                if s == 0:
                    dve.wait_ge(acc_done, T + 1)
                else:
                    dve.wait_ge(down_done, 1 + (T + 1) * NC)
                for k in range(2):
                    link(dve.bn_stats(stats[:, k, :], acc[:, s, k, :]))
                carry_wait()
                link(dve.bn_aggr(mv[:, :], stats[:, :, :]))
                dve.tensor_tensor(ln[:, 0:1], mv[:, 1:2], theta[:, bass.ds(2 * T + s, 1)], ALU.add).then_inc(root_asked, 1)
                dve.wait_ge(root_done, 2 * T + s + 1)
                link(dve.reciprocal(ln[:, 2:3], ln[:, 1:2]))
                link(dve.scalar_tensor_tensor(out=ln[:, 3:4], in0=ln[:, 0:1], scalar=ln[:, 2:3], in1=ln[:, 2:3],
                                              op0=ALU.mult, op1=ALU.mult))
                link(dve.tensor_scalar(ln[:, 3:4], ln[:, 3:4], -0.5, 1.5, ALU.mult, ALU.add))
                dve.wait_ge(z_done, 1 + 4 * T + 2 * s)
                tt(ln[:, 4:5], ln[:, 2:3], ln[:, 3:4], ALU.mult)
                dve.scalar_tensor_tensor(out=ln[:, 5:6], in0=mv[:, 0:1], scalar=-1.0, in1=ln[:, 4:5],
                                         op0=ALU.mult, op1=ALU.mult).then_inc(norm_ready, 1)

            def add_z(T, s):
                for k in range(2):
                    n = 4 * T + 2 * s + k
                    dve.wait_ge(z_scaled, n + 1)
                    if k == 0:
                        dve.wait_ge(xb_done, 2 * T + s + 1)
                    cols = xr[:, s, k * 512:k * 512 + 512]
                    dve.tensor_tensor(cols, cols, z[:, k, :], ALU.add).then_inc(z_added, 1)

            with dve.Fori(0, TILES // 2) as i:
                chain.loop(i, 2 * (6 + 2 * 7 + 1))
                for b in range(2):
                    T = 2 * i + b
                    route_weights(T)
                    dve.wait_ge(relu_scale_in, 16 * T + 16)
                    for c in range(NC):
                        if c >= 2:
                            dve.wait_ge(h_lo, T * NC + c - 1)
                        evacuate(T, c)
                        if c == 5:
                            dve.wait_ge(route_done, T + 1)
                            link(dve.tensor_copy(route[:, :], route_ps[:, :, :].rearrange("p s m -> p (s m)")))
                    layernorm(T, 0)
                    layernorm(T, 1)
                    add_z(T, 0)
                    add_z(T, 1)
            chain.end_loop(TILES // 2)


_INS = ["x", "itok_B_8_3872", "L0_cond_log_dt", "L0_cond_C", "L0_cond_log_A_real", "L0_cond_A_imag", "L0_cond_D",
        "L0_ffn_gate_w", "L0_ffn_up_w", "L0_ffn_down_w", "L0_ffn_fc1_w", "L0_ffn_fc2_w", "L0_ffn_expert_w",
        "L0_ffn_ln_gamma", "L0_ffn_ln_beta"]


def kernel(**inputs):
    import numpy as np
    import concourse.bacc as bacc
    from concourse.bass_utils import run_bass_kernel_spmd

    nc = bacc.Bacc("TRN2", target_bir_lowering=False, num_devices=1)
    arrays, args = {}, []
    for name in _INS:
        a = np.ascontiguousarray(inputs[name])
        arrays[f"in_{name}"] = a
        args.append(nc.dram_tensor(f"in_{name}", a.shape, mybir.dt.from_np(a.dtype), kind="ExternalInput").ap())
    args.append(nc.dram_tensor("out_0", (B, H, L), F32, kind="ExternalOutput").ap())
    build(nc, *args)
    r = run_bass_kernel_spmd(nc, [arrays], core_ids=[0])
    return r.results[0]["out_0"]
```

```python
import math
from contextlib import ExitStack

import concourse.bass as bass
from concourse import mybir

F32 = mybir.dt.float32
F16 = mybir.dt.float16
BF16 = mybir.dt.bfloat16
I32 = mybir.dt.int32
I16 = mybir.dt.int16
U8 = mybir.dt.uint8
ALU = mybir.AluOpType
ACT = mybir.ActivationFunctionType
AX = mybir.AxisListType

P = 128
B, H, L = 64, 64, 1024
N = 64
INT, LAT, NE = 2048, 512, 8
KT = L // P
CI = INT // P
CL = LAT // P
NC = CI + CL
PAIRS = H // 2
TILES = PAIRS // 2
LN_EPS = 1e-5
R = 32
KPAD = P + L

FC2_0, W1_0, UP_0, DN_0 = 0, CL, CL + 4, CL + 4 + 2 * KT
PIECES = DN_0 + CI
MAGIC = 1.5 * 2.0 ** 23
TWO_PI = 6.2831850
EXP_MASK = 0x7F800000
TINY = 2.0 ** -40


class Chain:

    def __init__(self, eng, sem):
        self.eng, self.sem, self.count, self.turn, self.per = eng, sem, 0, 0, 0

    def loop(self, turn, per):
        self.start, self.turn, self.per = self.count, turn, per

    def end_loop(self, turns):
        assert self.count - self.start == self.per
        self.count, self.turn = self.start + self.per * turns, 0

    def link(self, ins):
        ins.then_inc(self.sem, 1)
        self.count += 1
        self.eng.wait_ge(self.sem, self.count + self.turn * self.per)


def build(nc, x, itok, log_dt, C, log_A_real, A_imag, D, gate_w, up_w, down_w, fc1_w, fc2_w, expert_w,
          ln_gamma, ln_beta, out):
    k_dram = nc.dram_tensor("k_padded", (2, H, KPAD), F16)
    hid_dram = nc.dram_tensor("hidden_pairs", (PAIRS, P, 2, KT, P), F16)
    relu_dram = nc.dram_tensor("relu_scales", (PAIRS, P), BF16)

    with ExitStack() as top:
        def sb(name, shape, dt, stack=top):
            return stack.enter_context(nc.sbuf_tensor(name, shape, dt))

        W = sb("weights", [P, PIECES + 1, 2 * L], F16)
        gate = sb("gate", [P, KT, 2 * NE], F16)
        id16 = sb("id16", [P, P], F16)
        ones16 = sb("ones16", [P, P], BF16)
        pair_scale = sb("pair_scale", [P, PAIRS], F32)
        rho = sb("rho", [P, PAIRS], F32)
        energy = sb("energy", [P, PAIRS], F32)
        scales = sb("scales", [P, 8], F32)
        s_up, s_w1, s_gate, s_down, s_fc2 = (scales[:, k:k + 1] for k in range(5))

        def raw(slot, n=1):
            return W[:, slot:slot + n, :].bitcast(F32)

        x0 = raw(PIECES)[:, 0, :]
        with ExitStack() as both:
            x_mask = sb("x_mask", [P, L], BF16, both)
            mask = sb("mask", [P, KT, B], U8, both)
            prepare(nc, W, raw, gate, id16, ones16, x0, x_mask, mask, pair_scale, s_up, s_w1, s_gate, s_fc2, k_dram,
                    x, itok, log_dt, C, log_A_real, A_imag, D, gate_w, up_w, down_w, fc1_w, fc2_w, expert_w)
            conv(nc, W, raw, gate, id16, ones16, x0, x_mask, mask, pair_scale, rho, energy, scales, k_dram, hid_dram,
                 x, down_w)
        ffn(nc, W, raw, gate, id16, rho, energy, scales, hid_dram, relu_dram, x, ln_gamma, ln_beta, out)


def start_at_one(eng, *sems):
    for s in sems:
        eng.sem_inc(s, 1)


def first(t):
    return isinstance(t, int) and t == 0


def power_scale(dve, link, dst, src, target):
    link(dve.tensor_scalar(dst, src, TINY, None, ALU.max))
    link(dve.tensor_scalar(dst.bitcast(I32), dst.bitcast(I32), EXP_MASK, None, ALU.bitwise_and))
    link(dve.reciprocal(dst, dst))
    link(dve.tensor_scalar(dst, dst, target, None, ALU.mult))


def root_power(dve, link, dst, src, least):
    link(dve.tensor_scalar(dst, src, least, None, ALU.max))
    link(dve.tensor_scalar(dst.bitcast(I32), dst.bitcast(I32), EXP_MASK, None, ALU.bitwise_and))
    link(dve.tensor_scalar(dst.bitcast(I32), dst.bitcast(I32), 0.5, 127.0 * 2.0 ** 22, ALU.mult, ALU.add))
    link(dve.tensor_scalar(dst.bitcast(I32), dst.bitcast(I32), EXP_MASK, None, ALU.bitwise_and))


def norm_scale(dve, link, dst, src, target, least=TINY ** 2):
    root_power(dve, link, dst, src, least)
    link(dve.reciprocal(dst, dst))
    link(dve.tensor_scalar(dst, dst, target, None, ALU.mult))


def load_x_pair(eng, x, dst, t, done):
    for j in range(2):
        eng.dma_start(dst[j * B:j * B + B, :], x[:, bass.ds(2 * t + j, 1), :].rearrange("b o l -> (b o) l")).then_inc(done, 16)


def prepare(nc, W, raw, gate, id16, ones16, x0, x_mask, mask, pair_scale, s_up, s_w1, s_gate, s_fc2, k_dram,
            x, itok, log_dt, C, log_A_real, A_imag, D, gate_w, up_w, down_w, fc1_w, fc2_w, expert_w):
    with ExitStack() as ctx:
        def sb(name, shape, dt):
            return ctx.enter_context(nc.sbuf_tensor(name, shape, dt))

        def psum(name, shape, dt=F32):
            return ctx.enter_context(nc.psum_tensor(name, shape, dt))

        def sem(name):
            return ctx.enter_context(nc.semaphore(name))

        S0 = DN_0 + 1
        fc1_sb = raw(S0, 4).rearrange("p s (k m) -> p (s k) m", m=LAT)
        fc1T = raw(S0 + 4, 4)
        expert_sb = raw(S0 + 8, 2).rearrange("p s (k m) -> p (s k) m", m=LAT)
        small = raw(S0 + 10, 3).rearrange("p s m -> p (s m)")
        up_sq = W[:, S0 + 13, :].bitcast(BF16).rearrange("p (b m) -> p b m", b=2)
        w1_sq = W[:, S0 + 14, 0:2 * LAT].bitcast(BF16).rearrange("p (b m) -> p b m", b=2)
        kpad0 = W[:, S0 + 14, 2 * LAT:2 * LAT + P]

        big = [sb(f"table{k}", [P, H, R], F32) for k in range(5)]
        id32, ones32 = (W[:, S0 + 14, 2 * LAT + P * k:2 * LAT + P * (k + 2)].bitcast(F32) for k in (1, 3))
        half = sb("half", [P, 1], F32)
        time_row = big[1][:, :, :].rearrange("p h r -> p (h r)")[:, 0:L // 2].bitcast(I16)
        position = big[2][:, 0:P * 4 // R, :].rearrange("p h r -> p (h r)").bitcast(I32).rearrange("p (k b) -> p k b", b=B)
        len_row = big[3][:, 0:B // R, :].rearrange("p h r -> p (h r)").bitcast(I32)
        len_i = sb("len_i", [P, 1], I32)
        len_col = sb("len_col", [P, 1], F32)

        nxt = [0]

        def cut(n):
            nxt[0] += n
            return small[0:H, nxt[0] - n:nxt[0]]

        logs, C_sb, aim = cut(N + 1), cut(2 * N), cut(N)
        t0, t1, t2, ex, q, p2 = (cut(N + 1) for _ in range(6))
        alpha, w_im, turns, fhalf, sin_w, sin_h = (cut(N) for _ in range(6))
        e_re, e_im, inv, f_re, f_im, s_re, s_im, u0, u1 = (cut(N) for _ in range(9))
        z_rows = cut(4 * P).rearrange("p (z s) -> p z s", z=4)
        kf = big[1][0:R, :, :]
        abs_sum = big[2][0:R, :, 0]
        k_sc = big[3][0:R, :, :]
        k_hi = big[4][0:R, :, :].bitcast(F16)[:, :, 0:R]
        k_lo = big[4][0:R, :, :].bitcast(F16)[:, :, R:2 * R]
        nxt_g = small[:, nxt[0]:nxt[0] + 512]
        gate_raw = nxt_g[:, 0:64].rearrange("p (k e) -> p k e", e=NE)
        gate_sq = nxt_g[:, 64:128]
        gate_sum = nxt_g[:, 128:136]
        gate_hl = nxt_g[:, 136:137]
        fc2_max = nxt_g[:, 137:138]
        sk = nxt_g[:, 192:256]
        bound = nxt_g[:, 256:260]
        d_row = nxt_g[0:1, 320:320 + H]
        count = nxt_g[:, 384:384 + R]
        z_cols = small[:, nxt[0] + 512:nxt[0] + 512 + 4 * H].rearrange("p (z h) -> p z h", z=4)

        up_sum = psum("up_sum", [P, 4, 512])
        ring = psum("ring", [P, 2, 512])
        w1_sum = psum("w1_sum", [P, 512])
        misc = psum("misc", [P, 512])
        z_ps, gate_ps = misc[:, 0:4 * H].rearrange("p (z h) -> p z h", z=4), misc[:, 256:320]
        fc2_ps, sk_ps = misc[:, 320:321], misc[:, 384:448]

        fc1_in, expert_in, cond_in, gate_in, fc2_in = map(sem, ("fc1_in", "expert_in", "cond_in", "gate_in", "fc2_in"))
        up_in = [sem(f"up_in{k}") for k in range(4)]
        consts, consts_a = sem("consts"), sem("consts_a")
        dve_c = sem("dve_chain")
        sines_asked, sines_done, z_ready, z_turned = map(sem, ("sines_asked", "sines_done", "z_ready", "z_turned"))
        ring_full, ring_free = sem("ring_full"), sem("ring_free")
        w1_sq_ready, w1_sq_used, w1_summed = map(sem, ("w1_sq_ready", "w1_sq_used", "w1_summed"))
        up_sq_ready, up_sq_used = sem("up_sq_ready"), sem("up_sq_used")
        table_asked, table_done, tables = map(sem, ("table_asked", "table_done", "tables"))
        sums_in, sums_out, k_ready, k_scaled, k_split, k_out = map(
            sem, ("sums_in", "sums_out", "k_ready", "k_scaled", "k_split", "k_out"))
        gate_scaled, gate_hi = sem("gate_scaled"), sem("gate_hi")
        pad_ready, down_in = sem("pad_ready"), sem("down_early")
        len_in, iotas, masks_ready, x_masked = map(sem, ("len_in", "iotas", "masks_ready", "x_masked0"))
        x_in = sem("x_in")

        block = ctx.enter_context(nc.Block())

        @block.sync
        def _(sp):
            sp.dma_start(logs[:, 0:N], log_A_real).then_inc(cond_in, 16)
            sp.dma_start(logs[:, N:N + 1], log_dt.rearrange("(h o) -> h o", o=1)).then_inc(cond_in, 16)
            sp.dma_start(C_sb, C.rearrange("h n c -> h (n c)")).then_inc(cond_in, 16)
            sp.dma_start(aim, A_imag).then_inc(cond_in, 16)
            sp.dma_start(d_row, D.rearrange("(o h) -> o h", o=1)).then_inc(cond_in, 16)
            for j in range(2):
                sp.dma_start(len_i[j * B:j * B + B, :], itok.rearrange("(b o) -> b o", o=1)).then_inc(len_in, 16)
            sp.dma_start(len_row, itok.rearrange("(o b) -> o b", o=1).to_broadcast([P, B])).then_inc(len_in, 16)
            sp.dma_start(fc1_sb, fc1_w.rearrange("(c p) m -> p c m", p=P)).then_inc(fc1_in, 16)
            sp.dma_start(expert_sb, expert_w.rearrange("(c p) m -> p c m", p=P)).then_inc(expert_in, 16)
            sp.dma_start(raw(FC2_0 + 1, CL), fc2_w.rearrange("(c p) m -> p c m", p=P)).then_inc(fc2_in, 16)
            for k in range(4):
                sp.dma_start(raw(UP_0 + 1 + 4 * k, 4).rearrange("p (c s) m -> p c (s m)", s=2),
                             up_w.rearrange("(c p) m -> p c m", p=P)[:, 2 * k:2 * k + 2, :]).then_inc(up_in[k], 16)
            sp.dma_start(gate_raw, gate_w.rearrange("(c p) e -> p c e", p=P)).then_inc(gate_in, 16)
            load_x_pair(sp, x, x0, 0, x_in)
            sp.wait_ge(ring_full, 16)
            sp.dma_start(raw(DN_0 + 1, 10), down_w.rearrange("(c p) m -> p c m", p=P)[:, 0:10, :]).then_inc(down_in, 16)
            sp.wait_ge(pad_ready, 1)
            for part in range(2):
                sp.dma_start(k_dram.ap()[part, :, 0:P], kpad0[0:H, :]).then_inc(k_out, 16)
            sp.wait_ge(k_split, 2)
            for part, k in enumerate((k_hi, k_lo)):
                sp.dma_start(bass.AP(k_dram, part * H * KPAD + P, [[R, R], [KPAD, H], [1, R]]), k).then_inc(k_out, 16)
            sp.wait_ge(k_out, 64)
            sp.wait_ge(down_in, 16)

        @block.gpsimd
        def _(pool):
            pool.memset(id32, 0.0).then_inc(consts, 1)
            pool.wait_ge(consts, 1)
            pool.affine_select(out=id32, in_=id32, compare_op=ALU.not_equal, fill=1.0, base=0,
                               pattern=[[-1, P]], channel_multiplier=1).then_inc(consts, 1)
            pool.memset(ones32, 1.0).then_inc(consts, 1)
            pool.memset(ones16[:, :], 1.0).then_inc(consts, 1)
            pool.wait_ge(consts, 2)
            pool.tensor_copy(id16[:, :], id32).then_inc(consts, 1)
            pool.iota(count, pattern=[[1, R]], base=0, channel_multiplier=0,
                      allow_small_or_imprecise_dtypes=True).then_inc(consts_a, 1)
            pool.memset(kpad0, 0.0).then_inc(pad_ready, 1)
            pool.iota(time_row, pattern=[[1, L]], base=0, channel_multiplier=0).then_inc(iotas, 1)
            pool.iota(position, pattern=[[P, KT], [0, B]], base=0, channel_multiplier=1).then_inc(iotas, 1)
            pool.wait_ge(masks_ready, 1)
            pool.wait_ge(x_in, 32)
            pool.tensor_tensor(x0, x0, x_mask[:, :], ALU.mult).then_inc(x_masked, 1)

        @block.scalar
        def _(act):
            for u in range(8):
                act.wait_ge(ring_full, u + 1)
                act.activation(fc1T[:, u // 2, u % 2 * 512:u % 2 * 512 + 512], ring[:, u % 2, :],
                               ACT.Copy).then_inc(ring_free, 1)
            act.wait_ge(sines_asked, 1)
            act.activation(sin_w, turns, ACT.Sin, scale=TWO_PI).then_inc(sines_done, 1)
            act.activation(sin_h, fhalf, ACT.Sin, scale=TWO_PI).then_inc(sines_done, 1)

            def table(n, func, t, scale=1.0):
                act.wait_ge(table_asked, n)
                act.activation(t[:, :, :], t[:, :, :], func, scale=scale).then_inc(table_done, 1)

            def up_square(j):
                if j % 4 == 0:
                    act.wait_ge(up_in[j // 4], 16)
                if j >= 2:
                    act.wait_ge(up_sq_used, j - 1)
                act.activation(up_sq[:, j % 2, :], raw(UP_0 + 1 + j)[:, 0, :], ACT.Square).then_inc(up_sq_ready, 1)

            def w1_chunk(k):
                u = 8 + k
                act.wait_ge(ring_full, u + 1)
                if k >= 2:
                    act.wait_ge(w1_sq_used, k - 1)
                act.activation(w1_sq[:, k % 2, :], ring[:, u % 2, :], ACT.Square).then_inc(w1_sq_ready, 1)
                act.activation(raw(W1_0 + 1 + k // 2)[:, 0, k % 2 * 512:k % 2 * 512 + 512], ring[:, u % 2, :],
                               ACT.Copy).then_inc(ring_free, 1)
                up_square(k)

            for k in range(5):
                w1_chunk(k)
            table(1, ACT.Sin, big[0], TWO_PI)
            w1_chunk(5)
            w1_chunk(6)
            table(3, ACT.Sin, big[3], TWO_PI)
            w1_chunk(7)
            table(4, ACT.Sin, big[4], TWO_PI)
            table(2, ACT.Exp, big[1])
            table(5, ACT.Exp, big[2])
            for j in range(KT, KT + 4):
                up_square(j)
            for g in range(4):
                u = 16 + g
                act.wait_ge(ring_full, u + 1)
                act.activation(kf[:, 16 * g:16 * g + 16, :], ring[0:R, u % 2, :].rearrange("p (h r) -> p h r", r=R),
                               ACT.Copy).then_inc(ring_free, 1)
            for j in range(KT + 4, 2 * KT):
                up_square(j)
            act.wait_ge(k_scaled, 1)
            act.activation(k_hi, k_sc, ACT.Copy).then_inc(k_split, 1)
            act.wait_ge(gate_scaled, 1)
            act.activation(gate[:, :, 0:NE], gate_raw, ACT.Copy, scale=s_gate).then_inc(gate_hi, 1)

        @block.tensor
        def _(pe):
            pe.wait_ge(consts, 5)
            pe.wait_ge(fc1_in, 16)
            for u in range(8):
                if u >= 2:
                    pe.wait_ge(ring_free, u - 1)
                for k in range(4):
                    c = u % 2 * 4 + k
                    ins = pe.transpose(ring[:, u % 2, k * P:k * P + P], fc1_sb[:, c, u // 2 * P:u // 2 * P + P], id32)
                ins.then_inc(ring_full, 1)
            pe.wait_ge(expert_in, 16)
            pe.wait_ge(ring_free, 8)

            def w1_colsum(k):
                pe.wait_ge(w1_sq_ready, k + 1)
                pe.matmul(w1_sum[:, :], ones16[:, :], w1_sq[:, k % 2, :], start=(k == 0),
                          stop=(k == KT - 1)).then_inc(w1_sq_used, 1)

            def up_colsum(j):
                pe.wait_ge(up_sq_ready, j + 1)
                for k in range(2):
                    ins = pe.matmul(up_sum[:, j % 2 * 2 + k, :], ones16[:, :], up_sq[:, j % 2, k * 512:k * 512 + 512],
                                    start=(j < 2), stop=(j >= 2 * KT - 2))
                ins.then_inc(up_sq_used, 1)

            def colsums(k):
                w1_colsum(k)
                up_colsum(k)

            for k in range(KT):
                u = 8 + k
                pe.wait_ge(ring_free, u - 1)
                for c in range(CL):
                    ins = pe.matmul(ring[:, u % 2, :], fc1T[:, c, k * P:k * P + P], expert_sb[:, c, :],
                                    start=(c == 0), stop=(c == CL - 1))
                ins.then_inc(ring_full, 1)
                if k == 1:
                    pe.wait_ge(z_ready, 1)
                    for z in range(4):
                        ins = pe.transpose(z_ps[:, z, :], z_rows[:, z, :], id32[0:H, 0:H])
                    ins.then_inc(z_turned, 1)
                if k:
                    colsums(k - 1)
            colsums(KT - 1)
            for j in range(KT, KT + 4):
                up_colsum(j)
            pe.wait_ge(tables, 2)
            for g in range(4):
                u = 16 + g
                pe.wait_ge(ring_free, u - 1)
                for k in range(16):
                    h = 16 * g + k
                    ins = pe.matmul(ring[0:R, u % 2, k * R:k * R + R], big[3][:, h, :], big[0][:, h, :],
                                    start=True, stop=True)
                ins.then_inc(ring_full, 1)
            pe.wait_ge(sums_in, 2)
            pe.matmul(fc2_ps, ones32, fc2_max, start=True, stop=True)
            pe.matmul(gate_ps, ones32, gate_sq, start=True, stop=True).then_inc(sums_out, 1)
            pe.wait_ge(sums_in, 3)
            pe.matmul(sk_ps, ones32[0:R, :], abs_sum, start=True, stop=True).then_inc(sums_out, 1)
            for j in range(KT + 4, 2 * KT):
                up_colsum(j)

        @block.vector
        def _(dve):
            chain = Chain(dve, dve_c)
            link = chain.link

            def expm1_parts(v, n):
                a, b, c, qq, pp = t0[:, 0:n], t1[:, 0:n], t2[:, 0:n], q[:, 0:n], p2[:, 0:n]
                link(dve.tensor_scalar(a, v, 1.0 / math.log(2.0), MAGIC, ALU.mult, ALU.add))
                link(dve.tensor_scalar(a, a, MAGIC, None, ALU.subtract))
                link(dve.scalar_tensor_tensor(out=b, in0=a, scalar=-0.693359375, in1=v, op0=ALU.mult, op1=ALU.add))
                link(dve.scalar_tensor_tensor(out=b, in0=a, scalar=2.12194440e-4, in1=b, op0=ALU.mult, op1=ALU.add))
                link(dve.tensor_scalar(qq, b, 1.0 / math.factorial(8), None, ALU.mult))
                for k in range(7, 0, -1):
                    link(dve.scalar_tensor_tensor(out=qq, in0=qq, scalar=1.0 / math.factorial(k), in1=b,
                                                  op0=ALU.add, op1=ALU.mult))
                link(dve.tensor_scalar(a, a, -126.0, 127.0, ALU.max, ALU.min))
                link(dve.tensor_scalar(pp.bitcast(I32), a, 127.0, 2.0 ** 23, ALU.add, ALU.mult))
                link(dve.tensor_tensor(c, pp, qq, ALU.mult))
                return c, pp

            def tt(o, a, b, op):
                link(dve.tensor_tensor(o, a, b, op))

            def to_fraction(o, a, k):
                link(dve.tensor_scalar(k, a, MAGIC, MAGIC, ALU.add, ALU.subtract))
                tt(o, a, k, ALU.subtract)

            dve.wait_ge(cond_in, 80)
            c, pp = expm1_parts(logs, N + 1)
            tt(ex, c, pp, ALU.add)
            ea, dt = ex[:, 0:N], ex[:, N:N + 1]
            link(dve.tensor_scalar(alpha, ea, dt, -1.0, ALU.mult, ALU.mult))
            link(dve.tensor_scalar(w_im, aim, dt, None, ALU.mult))
            link(dve.tensor_scalar(u0, w_im, 1.0 / (2.0 * math.pi), None, ALU.mult))
            to_fraction(turns, u0, u1)
            link(dve.tensor_scalar(u0, w_im, 1.0 / (4.0 * math.pi), None, ALU.mult))
            link(dve.tensor_scalar(u1, u0, MAGIC, MAGIC, ALU.add, ALU.subtract))
            dve.tensor_tensor(fhalf, u0, u1, ALU.subtract).then_inc(sines_asked, 1)
            c, pp = expm1_parts(alpha, N)
            link(dve.scalar_tensor_tensor(out=s_re, in0=pp, scalar=-1.0, in1=c, op0=ALU.add, op1=ALU.add))
            tt(s_im, c, pp, ALU.add)
            dve.wait_ge(len_in, 48)
            dve.wait_ge(iotas, 2)
            link(dve.tensor_copy(len_col[:, :], len_i[:, :]))
            link(dve.tensor_scalar(x_mask[:, :], time_row, len_col[:, 0:1], None, ALU.is_lt))
            link(dve.tensor_tensor(mask[:, :, :], position, len_row.unsqueeze(1).to_broadcast([P, KT, B]),
                                   ALU.is_lt))
            dve.sem_inc(masks_ready, 1)
            dve.wait_ge(sines_done, 2)
            tt(e_im, s_im, sin_w, ALU.mult)
            tt(u0, s_im, sin_h, ALU.mult)
            tt(u0, u0, sin_h, ALU.mult)
            link(dve.scalar_tensor_tensor(out=e_re, in0=u0, scalar=-2.0, in1=s_re, op0=ALU.mult, op1=ALU.add))
            tt(u0, ea, ea, ALU.mult)
            tt(u1, aim, aim, ALU.mult)
            tt(u0, u0, u1, ALU.add)
            link(dve.reciprocal(inv, u0))
            tt(u0, e_im, aim, ALU.mult)
            tt(u1, e_re, ea, ALU.mult)
            tt(u0, u0, u1, ALU.subtract)
            tt(f_re, u0, inv, ALU.mult)
            tt(u0, e_re, aim, ALU.mult)
            tt(u1, e_im, ea, ALU.mult)
            tt(u0, u0, u1, ALU.add)
            link(dve.scalar_tensor_tensor(out=f_im, in0=u0, scalar=-1.0, in1=inv, op0=ALU.mult, op1=ALU.mult))
            cc = C_sb.rearrange("p (n c) -> p n c", c=2)
            tt(u0, f_re, cc[:, :, 0], ALU.mult)
            tt(u1, f_im, cc[:, :, 1], ALU.mult)
            tt(s_re, u0, u1, ALU.subtract)
            tt(u0, f_im, cc[:, :, 0], ALU.mult)
            tt(u1, f_re, cc[:, :, 1], ALU.mult)
            tt(s_im, u0, u1, ALU.add)
            for z, (a, fa, b, fb) in enumerate(((alpha, 1.0, alpha, 1.0), (turns, 1.0, turns, 1.0),
                                                (s_re, 2.0, s_im, -2.0), (s_im, -2.0, s_re, -2.0))):
                link(dve.tensor_scalar(z_rows[:, z, 0:N], a, fa, None, ALU.mult))
                link(dve.tensor_scalar(z_rows[:, z, N:2 * N], b, fb, None, ALU.mult))
            dve.memset(half[0:N, :], 0.25).then_inc(z_ready, 1)
            link(dve.memset(half[N:P, :], 0.0))
            dve.wait_ge(z_turned, 1)
            link(dve.tensor_copy(z_cols, z_ps))
            dve.wait_ge(consts_a, 1)

            def wide(col):
                return col.unsqueeze(2).to_broadcast([P, H, R])

            def steps(row):
                return row.unsqueeze(1).to_broadcast([P, H, R])

            t_alpha, t_turns, p1, pq = (z_cols[:, z, :] for z in range(4))
            b0, b1, b2, b3, b4 = (b_[:, :, :] for b_ in big)
            tt(b0, wide(t_turns), steps(count), ALU.mult)
            link(dve.tensor_scalar(b0, b0, half[:, 0:1], None, ALU.add))
            link(dve.tensor_scalar(b1, b0, MAGIC, MAGIC, ALU.add, ALU.subtract))
            dve.tensor_tensor(b0, b0, b1, ALU.subtract).then_inc(table_asked, 1)
            dve.wait_ge(table_asked, 1)
            dve.tensor_tensor(b1, wide(t_alpha), steps(count), ALU.mult).then_inc(table_asked, 1)
            link(dve.tensor_scalar(t_turns, t_turns, float(R), None, ALU.mult))
            link(dve.tensor_scalar(b2[:, :, 0], t_turns, MAGIC, MAGIC, ALU.add, ALU.subtract))
            tt(t_turns, t_turns, b2[:, :, 0], ALU.subtract)
            link(dve.tensor_scalar(t_alpha, t_alpha, float(R), None, ALU.mult))
            tt(b2, wide(t_turns), steps(count), ALU.mult)
            link(dve.tensor_scalar(b3, b2, MAGIC, MAGIC, ALU.add, ALU.subtract))
            dve.tensor_tensor(b3, b2, b3, ALU.subtract).then_inc(table_asked, 1)
            dve.wait_ge(table_asked, 3)
            link(dve.tensor_scalar(b2, b2, 0.25, None, ALU.add))
            link(dve.tensor_scalar(b4, b2, MAGIC, MAGIC, ALU.add, ALU.subtract))
            dve.tensor_tensor(b4, b2, b4, ALU.subtract).then_inc(table_asked, 1)
            dve.wait_ge(table_asked, 4)
            dve.tensor_tensor(b2, wide(t_alpha), steps(count), ALU.mult).then_inc(table_asked, 1)
            dve.wait_ge(table_done, 3)
            tt(b3, b3, wide(pq), ALU.mult)
            tt(b4, b4, wide(p1), ALU.mult)
            tt(b3, b3, b4, ALU.add)
            dve.wait_ge(table_done, 4)
            dve.tensor_tensor(b0, b0, b1, ALU.mult).then_inc(tables, 1)
            dve.wait_ge(table_done, 5)
            dve.tensor_tensor(b3, b3, b2, ALU.mult).then_inc(tables, 1)
            dve.wait_ge(gate_in, 16)
            gate_in_sb = gate_raw.rearrange("p k e -> p (k e)")
            dve.tensor_tensor(gate_sq, gate_in_sb, gate_in_sb, ALU.mult).then_inc(sums_in, 1)
            dve.wait_ge(fc2_in, 16)
            dve.tensor_reduce(fc2_max, raw(FC2_0 + 1, CL), AX.XY, ALU.max, apply_absolute_value=True).then_inc(sums_in, 1)
            dve.wait_ge(ring_free, 20)
            link(dve.tensor_tensor(kf[0:1, :, 0], kf[0:1, :, 0], d_row, ALU.add))
            dve.tensor_reduce(abs_sum, kf, AX.X, ALU.add, apply_absolute_value=True).then_inc(sums_in, 1)
            dve.wait_ge(sums_out, 2)
            power_scale(dve, link, sk, sk_ps, 2.0 ** 14)
            dve.tensor_tensor(k_sc, kf, sk[0:R, :].unsqueeze(2).to_broadcast([R, H, R]), ALU.mult).then_inc(k_scaled, 1)
            sk2 = sk.rearrange("p (t j) -> p t j", j=2)
            link(dve.tensor_scalar(pair_scale[0:B, :], sk2[0:B, :, 0], 2.0 ** -15, None, ALU.mult))
            link(dve.tensor_scalar(pair_scale[B:P, :], sk2[B:P, :, 1], 2.0 ** -15, None, ALU.mult))
            dve.wait_ge(sums_out, 1)
            power_scale(dve, link, s_fc2, fc2_ps, 2.0 ** 14)
            dve.wait_ge(w1_sq_used, KT)
            link(dve.tensor_reduce(bound[:, 1:2], w1_sum[:, :], AX.X, ALU.max))
            dve.wait_ge(k_split, 1)
            dve.wait_ge(k_scaled, 1)
            dve.tensor_tensor(k_lo, k_sc, k_hi, ALU.subtract).then_inc(k_split, 1)
            norm_scale(dve, link, s_w1, bound[:, 1:2], 2.0 ** 14)
            link(dve.tensor_reduce(gate_sum, gate_ps.rearrange("p (k e) -> p e k", e=NE), AX.X, ALU.add))
            link(dve.tensor_reduce(gate_hl, gate_sum, AX.X, ALU.max))
            norm_scale(dve, link, s_gate, gate_hl, 2.0 ** 14)
            dve.sem_inc(gate_scaled, 1)
            dve.wait_ge(up_sq_used, 2 * KT)
            link(dve.tensor_reduce(bound[:, 2:3], up_sum[:, :, :], AX.XY, ALU.max))
            norm_scale(dve, link, s_up, bound[:, 2:3], 2.0 ** 14)
            dve.wait_ge(gate_hi, 1)
            link(dve.scalar_tensor_tensor(out=gate[:, :, NE:2 * NE], in0=gate_raw, scalar=s_gate, in1=gate[:, :, 0:NE],
                                          op0=ALU.mult, op1=ALU.subtract))


def conv(nc, W, raw, gate, id16, ones16, x0, x_mask, mask, pair_scale, rho, energy, scales, k_dram, hid_dram, x, down_w):
    EARLY = 10
    s_up, s_w1, s_gate, s_down, s_fc2 = (scales[:, k:k + 1] for k in range(5))
    PHASES = ((1, 2, s_fc2, 2), (2, 3, s_w1, 2), (3, 5, s_up, 2), (5, 9, s_up, 1), (9, 10, s_down, 1),
              (10, PAIRS // 2, s_down, 1))
    SQUARED = 9
    with ExitStack() as ctx:
        def sb(name, shape, dt):
            return ctx.enter_context(nc.sbuf_tensor(name, shape, dt))

        def psum(name, shape, dt=F32):
            return ctx.enter_context(nc.psum_tensor(name, shape, dt))

        def sem(name):
            return ctx.enter_context(nc.semaphore(name))

        xn = sb("xn", [P, 2, L], F32)
        x_hl = sb("x_hl", [P, 2, KT, P], F16)
        uT = sb("uT", [P, 2, 2, KT, P], F16)
        slab = sb("slab", [P, 2, 2, L], F16)
        hid32 = sb("hid32", [P, 2, KT, B], F32)
        hid = sb("hid", [P, 2, 2, KT, P], F16)
        amax = sb("amax", [P, 2], F32)
        tau = sb("tau", [P, 2], F32)
        down_sq = sb("down_sq", [P, CI], F32)
        down_row = sb("down_row", [P, 1], BF16)

        turned = [psum(f"turned{k}", [P, KT, P], F16) for k in range(2)]
        conv_ps = [psum(f"conv_ps{j}", [P, KT, B]) for j in range(2)]
        gram_diag = psum("gram_diag", [P, 512])[:, 0:P]
        squares = psum("squares", [P, L])
        sum_ps = squares[:, 0:1]
        gram_ps = psum("gram_ps", [P, 512])[:, 0:P]

        down_in = sem("down_in")
        x_in = [sem(f"x_in{b}") for b in range(2)]
        slab_in = [sem(f"slab_in{j}") for j in range(2)]
        stored = [sem(f"stored{b}") for b in range(2)]
        dve_c = sem("dve_chain2")
        tau_ready, x_hi, x_lo, x_turned, u_ready = map(sem, ("tau_ready", "x_hi", "x_lo", "x_turned", "u_ready"))
        convolved, masked, hid_hi, hid_lo = map(sem, ("convolved", "masked", "hid_hi", "hid_lo"))
        piece_hi, piece_lo = sem("piece_hi2"), sem("piece_lo2")
        rows_squared, down_summed = sem("rows_squared"), sem("down_summed")
        piece_squared, x_masked = sem("piece_squared"), sem("x_masked")
        gram_done, gram_used = sem("gram_done"), sem("gram_used")
        down_scaled = sem("down_scaled")

        block = ctx.enter_context(nc.Block())

        def backwards(part):
            return bass.AP(x_hl, part * L + P - 1, [[2 * L, P], [P, KT], [-1, P]])

        def chunks(rows):
            return rows.rearrange("p (k m) -> p k m", k=KT)

        def loop(eng, lo, hi):
            if hi - lo == 1:
                yield lo
            else:
                with eng.Fori(lo, hi) as i:
                    yield i

        def rows(t, b):
            return x0 if first(t) else xn[:, b, :]

        def first_down(lo, b):
            return lo == SQUARED and b == 0

        def pieces(t, n):
            return [2 * t - 4, 2 * t - 3] if n == 2 else [UP_0 + t - 2]

        @block.sync
        def _(sp):
            def load_x(t, b):
                load_x_pair(sp, x, xn[:, b, :], t, x_in[b])

            def load_slab(t, j):
                src = bass.AP(k_dram, (2 * t + j) * KPAD + 1, [[1, P], [H * KPAD, 2], [1, L]])
                sp.dma_start(slab[:, j, :, :], src).then_inc(slab_in[j], 16)

            def store(t, b):
                sp.wait_ge(hid_lo, 1 + 2 * t + 2)
                sp.dma_start(hid_dram.ap()[bass.ds(t, 1), :, :, :, :].rearrange("o p a k m -> p (o a k m)"),
                             hid[:, b, :, :, :].rearrange("p a k m -> p (a k m)")).then_inc(stored[b], 16)

            def step(t, b, more=True):
                if more:
                    sp.wait_ge(x_lo, t + 1)
                    load_x(t + 2, b)
                sp.wait_ge(convolved, 2 * t - 2)
                load_slab(t - 1, 1)
                store(t - 2, b)
                sp.wait_ge(convolved, 2 * t - 1)
                load_slab(t, 0)

            for b in range(2):
                sp.sem_inc(stored[b], 16)
            load_slab(0, 0)
            load_slab(0, 1)
            load_x(1, 1)
            load_x(2, 0)
            sp.wait_ge(x_lo, 2)
            load_x(3, 1)
            sp.wait_ge(convolved, 1)
            load_slab(1, 0)
            LATE = 1 + (CI - EARLY) // 2
            with sp.Fori(1, LATE) as i:
                for b in range(2):
                    t = 2 * i + b
                    step(t, b)
                    sp.dma_start(W[:, bass.ds(DN_0 + 1 + EARLY + t - 2, 1), :].bitcast(F32).rearrange("p o m -> p (o m)"),
                                 down_w[bass.ds((EARLY + t - 2) * P, P), :]).then_inc(down_in, 16)
            with sp.Fori(LATE, PAIRS // 2 - 1) as i:
                for b in range(2):
                    step(2 * i + b, b)
            step(PAIRS - 2, 0, more=False)
            step(PAIRS - 1, 1, more=False)
            sp.wait_ge(convolved, 2 * PAIRS - 2)
            load_slab(PAIRS - 1, 1)
            store(PAIRS - 2, 0)
            store(PAIRS - 1, 1)
            for b in range(2):
                sp.wait_ge(stored[b], 16 + 16 * (PAIRS // 2))

        @block.gpsimd
        def _(pool):
            start_at_one(pool, hid_lo)
            def mask_x(t, b, i):
                pool.wait_ge(x_in[b], 32 * i + 32 * b)
                pool.tensor_tensor(xn[:, b, :], xn[:, b, :], x_mask[:, :], ALU.mult).then_inc(x_masked, 1)

            def low_half(t, b, j):
                pool.wait_ge(hid_hi, 2 * t + j + 1)
                cols = hid[:, b, :, :, j * B:j * B + B]
                pool.tensor_tensor(cols[:, 1], hid32[:, j, :, :], cols[:, 0], ALU.subtract).then_inc(hid_lo, 1)

            def step(t, b, i):
                if i is not None:
                    mask_x(t + 1, 1 - b, i + b)
                low_half(t - 2, b, 0)
                low_half(t - 2, b, 1)

            mask_x(1, 1, 0)
            mask_x(2, 0, 1)
            with pool.Fori(1, PAIRS // 2 - 1) as i:
                for b in range(2):
                    step(2 * i + b, b, i)
            step(PAIRS - 2, 0, PAIRS // 2 - 1)
            for t in range(PAIRS - 1, PAIRS + 2):
                step(t, t % 2, None)

        @block.scalar
        def _(act):
            def x_high(t, b):
                act.wait_ge(tau_ready, t + 1)
                if not first(t):
                    act.wait_ge(x_turned, t)
                act.activation(backwards(0), chunks(rows(t, b)), ACT.Copy, scale=tau[:, b:b + 1]).then_inc(x_hi, 1)

            def piece_high(p, scale):
                act.wait_ge(piece_lo, 1 + p)
                act.activation(W[:, bass.ds(p, 1), 0:L], W[:, bass.ds(p + 1, 1), :].bitcast(F32), ACT.Copy,
                               scale=scale).then_inc(piece_hi, 1)

            def hid_high(t, b, j):
                act.wait_ge(masked, 2 * t + j + 1)
                act.activation(hid[:, b, 0, :, j * B:j * B + B], hid32[:, j, :, :], ACT.Copy).then_inc(hid_hi, 1)

            def u_copy(t, b):
                act.wait_ge(x_turned, t + 1)
                for k in range(2):
                    act.activation(uT[:, b, k, :, :], turned[k][:, :, :], ACT.Copy).then_inc(u_ready, 1)

            x_high(0, 0)
            u_copy(0, 0)
            x_high(1, 1)
            u_copy(1, 1)
            for lo, hi, scale, n in PHASES:
                if lo == 5:
                    act.wait_ge(down_in, 16 * (CI - EARLY))
                for i in loop(act, lo, hi):
                    for b in range(2):
                        t = 2 * i + b
                        x_high(t, b)
                        act.wait_ge(stored[b], 16 + 16 * i - 16)
                        act.wait_ge(gram_done, 2 + t - 3)
                        hid_high(t - 2, b, 0)
                        if first_down(lo, b):
                            act.wait_ge(down_scaled, 1)
                        piece_high(pieces(t, n)[0], scale)
                        if lo < SQUARED:
                            act.activation(squares[:, :], W[:, bass.ds(DN_0 + 1 + t - 2, 1), :].bitcast(F32), ACT.Square,
                                           accum_out=down_sq[:, bass.ds(t - 2, 1)]).then_inc(piece_squared, 1)
                        hid_high(t - 2, b, 1)
                        act.wait_ge(convolved, 2 * t - 2)
                        u_copy(t, b)
                        if n == 2:
                            piece_high(pieces(t, n)[1], scale)
            for b in range(2):
                t = PAIRS + b
                piece_high(UP_0 + t - 2, s_down)
                act.wait_ge(stored[b], 16 + 16 * (PAIRS // 2 - 1))
                act.wait_ge(gram_done, 2 + t - 3)
                for j in range(2):
                    hid_high(t - 2, b, j)

        @block.tensor
        def _(pe):
            def turn(t):
                pe.wait_ge(x_lo, t + 1)
                if not first(t):
                    pe.wait_ge(u_ready, 2 * t)
                for k in range(2):
                    for c in range(KT):
                        ins = pe.transpose(turned[k][:, c, :], x_hl[:, k, c, :], id16[:, :])
                ins.then_inc(x_turned, 1)

            def gram(t, b):
                pe.wait_ge(hid_hi, 2 * t + 2)
                pe.wait_ge(gram_used, 1 + t)
                for c in range(KT):
                    ins = pe.matmul(gram_ps, hid[:, b, 0, c, :], hid[:, b, 0, c, :], start=(c == 0), stop=(c == KT - 1))
                ins.then_inc(gram_done, 1)

            def convolve(t, b, before=True):
                pe.wait_ge(u_ready, 2 * t + 2)
                for j in range(2):
                    pe.wait_ge(slab_in[j], 16 * t + 16)
                    if not first(t):
                        pe.wait_ge(masked, 2 * t - 1 + j)
                    for d in range(KT):
                        for ks, ku in ((0, 0), (0, 1), (1, 0)):
                            c0 = d * P
                            ins = pe.matmul(conv_ps[j][:, d:KT, :], slab[:, j, ks, c0:c0 + P],
                                            uT[:, b, ku, 0:KT - d, j * B:j * B + B],
                                            start=(d == ks == ku == 0), stop=(d == KT - 1 and ks == 1))
                        if before and j == d == 0:
                            gram(t - 1, 1 - b)
                    ins.then_inc(convolved, 1)

            start_at_one(pe, gram_used, gram_done)
            turn(0)
            convolve(0, 0, before=False)
            turn(1)
            for lo, hi in ((1, SQUARED), (SQUARED, PAIRS // 2)):
                if lo == SQUARED:
                    pe.wait_ge(rows_squared, 1)
                    pe.matmul(sum_ps, ones16[:, :], down_row[:, :], start=True, stop=True).then_inc(down_summed, 1)
                with pe.Fori(lo, hi) as i:
                    for b in range(2):
                        t = 2 * i + b
                        turn(t)
                        convolve(t - 1, 1 - b)
            convolve(PAIRS - 1, 1)
            gram(PAIRS - 1, 1)

        @block.vector
        def _(dve):
            chain = Chain(dve, dve_c)
            link = chain.link
            def scale_x(t, b):
                if not first(t):
                    dve.wait_ge(x_masked, t)
                link(dve.tensor_reduce(amax[:, b:b + 1], rows(t, b), AX.X, ALU.max, apply_absolute_value=True))
                power_scale(dve, link, tau[:, b:b + 1], amax[:, b:b + 1], 2.0 ** 14)
                dve.tensor_tensor(rho[:, bass.ds(t, 1)], tau[:, b:b + 1], pair_scale[:, bass.ds(t, 1)],
                                  ALU.mult).then_inc(tau_ready, 1)

            def x_low(t, b):
                dve.wait_ge(x_hi, t + 1)
                dve.scalar_tensor_tensor(out=backwards(1), in0=chunks(rows(t, b)), scalar=tau[:, b:b + 1],
                                         in1=backwards(0), op0=ALU.mult, op1=ALU.subtract).then_inc(x_lo, 1)

            def mask_hid(t, j):
                dve.wait_ge(convolved, 2 * t + j + 1)
                if not first(t):
                    dve.wait_ge(hid_lo, 1 + 2 * t + j - 1)
                dve.scalar_tensor_tensor(out=hid32[:, j, :, :], in0=conv_ps[j][:, :, :], scalar=2.0 ** -15,
                                         in1=mask[:, :, :], op0=ALU.mult, op1=ALU.mult).then_inc(masked, 1)

            def token_energy(t):
                dve.wait_ge(gram_done, 1 + t + 1)
                link(dve.tensor_tensor(gram_diag, gram_ps, id16[:, :], ALU.mult))
                dve.tensor_reduce(energy[:, bass.ds(t, 1)], gram_diag, AX.X, ALU.add).then_inc(gram_used, 1)

            def piece_low(p, scale):
                dve.wait_ge(piece_hi, p + 1)
                dve.scalar_tensor_tensor(out=W[:, bass.ds(p, 1), L:2 * L], in0=W[:, bass.ds(p + 1, 1), :].bitcast(F32),
                                         scalar=scale, in1=W[:, bass.ds(p, 1), 0:L], op0=ALU.mult,
                                         op1=ALU.subtract).then_inc(piece_lo, 1)

            def step(t, b, scale, n, last=False, scale_down=False):
                mask_hid(t - 2, 0)
                x_low(t, b)
                mask_hid(t - 2, 1)
                if scale_down:
                    dve.wait_ge(down_summed, 1)
                    norm_scale(dve, link, s_down, sum_ps, 2.0 ** 14)
                    dve.sem_inc(down_scaled, 1)
                piece_low(pieces(t, n)[0], scale)
                if not last:
                    scale_x(t + 1, 1 - b)
                token_energy(t - 2)
                if n == 2:
                    piece_low(pieces(t, n)[1], scale)

            start_at_one(dve, piece_lo)
            for t in range(2):
                scale_x(t, t)
                x_low(t, t)
            scale_x(2, 0)
            for lo, hi, scale, n in PHASES:
                if lo == SQUARED:
                    dve.wait_ge(piece_squared, CI)
                    dve.tensor_reduce(down_row[:, :], down_sq[:, :], AX.X, ALU.max).then_inc(rows_squared, 1)
                if hi == PAIRS // 2:
                    hi -= 1
                for i in loop(dve, lo, hi):
                    if hi - lo > 1:
                        chain.loop(i - lo, 2 * 6)
                    for b in range(2):
                        step(2 * i + b, b, scale, n, scale_down=first_down(lo, b))
                if hi - lo > 1:
                    chain.end_loop(hi - lo)
            step(PAIRS - 2, 0, s_down, 1)
            step(PAIRS - 1, 1, s_down, 1, last=True)
            for b in range(2):
                for j in range(2):
                    mask_hid(PAIRS - 2 + b, j)
                piece_low(UP_0 + PAIRS - 2 + b, s_down)
                token_energy(PAIRS - 2 + b)


def ffn(nc, W, raw, gate, id16, rho, energy, scales, hid_dram, relu_dram, x, ln_gamma, ln_beta, out):
    s_up, s_w1, s_gate, s_down, s_fc2 = (scales[:, k:k + 1] for k in range(5))
    TT = 2 * P
    HR = 4
    LAG = 3
    with ExitStack() as ctx:
        def sb(name, shape, dt):
            return ctx.enter_context(nc.sbuf_tensor(name, shape, dt))

        def psum(name, shape, dt=F32):
            return ctx.enter_context(nc.psum_tensor(name, shape, dt))

        def sem(name):
            return ctx.enter_context(nc.semaphore(name))

        hid = sb("hid_tile", [P, 2, 2, 2, KT, P], F16)
        h_hl = sb("h_hl", [P, HR, 2, TT], F16)
        r_buf = sb("r_buf", [P, 2, TT], F32)
        h32 = sb("h32", [P, 2, TT], F32)
        route = sb("route", [P, TT], F32)
        gamma = sb("gamma", [P, L], F32)
        beta = sb("beta", [P, L], F32)
        z = raw(PIECES)[:, 0, :].rearrange("p (b m) -> p b m", b=2)
        ones32 = sb("ones_f", [P, P], F32)
        xr = sb("xr", [P, 2, L], F32)
        theta = rho[:, :]
        k_route = energy[:, :]
        relu_scale = sb("relu_scale", [P, TT], BF16)
        tmp = sb("tmp", [P, 4], F32)
        g_lo, logits, top = (sb(name, [P, 2, NE], F32)[:, :, :] for name in ("g_lo", "logits", "top"))
        s_tok = sb("s_tok", [P, 2], F32)
        diag = route[:, :].rearrange("p (s m) -> p s m", s=2)
        stats = sb("stats", [P, 2, 6], F32)
        mv = sb("mv", [P, 2], F32)
        ln = sb("ln", [P, 6], F32)

        acc = psum("acc", [P, 2, 2, 512])
        up_ps = psum("up_ps", [P, 3, 512])
        route_bank = psum("route_bank", [P, 512])
        gate_ps = route_bank[:, 0:4 * NE].rearrange("p (s e) -> p s e", s=2)
        route_ps = route_bank[:, TT:2 * TT].rearrange("p (s m) -> p s m", s=2)
        nu_ps = up_ps[0:PAIRS, 2, TT:TT + P]
        nu, nu_rows = z[:, 0, 0:PAIRS], z[0:PAIRS, 0, 64:128].bitcast(BF16)
        nu16, id_bf = z[:, 0, 128:144].bitcast(BF16), z[:, 0, 192:256].bitcast(BF16)

        hid_in = [sem(f"hid_in{b}") for b in range(2)]
        xr_in = [sem(f"xr_in{s}") for s in range(2)]
        out_stored = [sem(f"out_stored{s}") for s in range(2)]
        ln_in, dve_c, consts = sem("ln_in"), sem("dve_chain3"), sem("consts3")
        up_done, up_free, h_hi, h_lo, down_done = map(
            sem, ("up_done", "up_free", "h_hi", "h_lo", "down_done"))
        gate_done, diag_ready, route_done, acc_done = map(sem, ("gate_done", "diag_ready", "route_done", "acc_done"))
        root_asked, root_done, norm_ready, z_done, z_scaled, z_added = map(
            sem, ("root_asked", "root_done", "norm_ready", "z_done", "z_scaled", "z_added"))
        xb_done, nu_ready, nu_turned, nu_copied, nu_stored, relu_scale_in, squared = map(
            sem, ("xb_done", "nu_ready", "nu_turned", "nu_copied", "nu_stored", "relu_scale_in", "squared3"))

        block = ctx.enter_context(nc.Block())

        def slot_of(c):
            return up_ps[:, c % 3, 0:TT]

        def tiles(eng, body):
            with eng.Fori(0, TILES // 2 - 1) as i:
                for b in range(2):
                    body(2 * i + b, True)
            body(TILES - 2, True)
            body(TILES - 1, False)

        @block.sync
        def _(sp):
            def load_hid(T, b):
                for s in range(2):
                    sp.dma_start(hid[:, b, s, :, :, :].rearrange("p a k m -> p (a k m)"),
                                 hid_dram.ap()[bass.ds(2 * T + s, 1), :, :, :, :].rearrange("o p a k m -> p (o a k m)")
                                 ).then_inc(hid_in[b], 16)

            def load_x(T):
                for s in range(2):
                    if not first(T):
                        sp.wait_ge(out_stored[s], 32 * T)
                    for j in range(2):
                        sp.dma_start(xr[j * B:j * B + B, s, :],
                                     x[:, bass.ds(4 * T + 2 * s + j, 1), :].rearrange("b o l -> (b o) l")
                                     ).then_inc(xr_in[s], 16)

            def load_relu_scale(T):
                sp.wait_ge(up_free, 1 + T * NC - CL)
                sp.dma_start(relu_scale[:, :], bass.AP(relu_dram, T * TT, [[0, P], [1, TT]])).then_inc(relu_scale_in, 16)

            def store_out(T):
                for s in range(2):
                    sp.wait_ge(z_added, 1 + 4 * T + 2 * s + 2)
                    for j in range(2):
                        sp.dma_start(out[:, bass.ds(4 * T + 2 * s + j, 1), :].rearrange("b o l -> (b o) l"),
                                     xr[j * B:j * B + B, s, :]).then_inc(out_stored[s], 16)

            load_hid(0, 0)
            load_hid(1, 1)
            load_x(0)
            sp.wait_ge(nu_copied, 1)
            sp.dma_start(relu_dram.ap(), nu_rows).then_inc(nu_stored, 16)
            sp.wait_ge(nu_stored, 16)
            sp.dma_start(relu_scale[:, :], bass.AP(relu_dram, 0, [[0, P], [1, TT]])).then_inc(relu_scale_in, 16)
            load_relu_scale(1)
            with sp.Fori(1, TILES // 2) as i:
                for b in range(2):
                    T = 2 * i + b
                    sp.wait_ge(up_done, (T - 1) * NC)
                    load_hid(T, b)
                    store_out(T - 2)
                    load_x(T - 1)
                    load_relu_scale(T)
            store_out(TILES - 2)
            load_x(TILES - 1)
            store_out(TILES - 1)
            for s in range(2):
                sp.wait_ge(out_stored[s], 32 * TILES)

        @block.gpsimd
        def _(pool):
            def low_half(T, c):
                if c < CI:
                    pool.wait_ge(squared, T * CI + c + 1)
                pool.wait_ge(h_hi, T * NC + c + 1)
                pool.tensor_tensor(h_hl[:, c % HR, 1, :], h32[:, c % 2, :], h_hl[:, c % HR, 0, :],
                                   ALU.subtract).then_inc(h_lo, 1)

            pool.memset(ones32[:, :], 1.0).then_inc(consts, 1)
            pool.wait_ge(ln_in, 32)
            def gamma_half(T, s):
                for k in range(2):
                    pool.wait_ge(z_done, 1 + 4 * T + 2 * s + k + 1)
                    pool.tensor_tensor(z[:, k, :], z[:, k, :], gamma[:, k * 512:k * 512 + 512],
                                       ALU.mult).then_inc(z_scaled, 1)

            def tile(T, more):
                for c in range(2, NC):
                    low_half(T, c)
                    if c in (9, 11):
                        s = (c - 9) // 2
                        pool.wait_ge(xr_in[s], 32 * T + 32)
                        pool.tensor_tensor(xr[:, s, :], xr[:, s, :], beta[:, :], ALU.add).then_inc(xb_done, 1)
                for s in range(2):
                    gamma_half(T, s)
                    if more:
                        low_half(T + 1, s)

            low_half(0, 0)
            low_half(0, 1)
            tiles(pool, tile)

        @block.scalar
        def _(act):
            act.dma_start(gamma[:, :], ln_gamma.rearrange("(o l) -> o l", o=1).to_broadcast([P, L])).then_inc(ln_in, 16)
            act.dma_start(beta[:, :], ln_beta.rearrange("(o l) -> o l", o=1).to_broadcast([P, L])).then_inc(ln_in, 16)
            start_at_one(act, z_done)
            def split(T, c):
                n = T * NC + c
                act.wait_ge(up_free, 1 + n + 1)
                if c < CI:
                    if c >= 2:
                        act.wait_ge(h_lo, n - 1)
                    act.activation(h32[:, c % 2, :], r_buf[:, c % 2, :], ACT.Square).then_inc(squared, 1)
                act.wait_ge(down_done, 1 + T * NC + max(c + 1 - HR, 0))
                if c < CI:
                    act.activation(h_hl[:, c % HR, 0, :], r_buf[:, c % 2, :], ACT.Square).then_inc(h_hi, 1)
                else:
                    act.activation(h_hl[:, c % HR, 0, :], h32[:, c % 2, :], ACT.Copy).then_inc(h_hi, 1)

            def root(T, s):
                act.wait_ge(root_asked, 2 * T + s + 1)
                act.activation(ln[:, 1:2], ln[:, 0:1], ACT.Sqrt).then_inc(root_done, 1)

            def norm(T, s):
                act.wait_ge(norm_ready, 2 * T + s + 1)
                for k in range(2):
                    act.wait_ge(z_added, 1 + 4 * T + (k + 1) * s)
                    act.activation(z[:, k, :], acc[:, s, k, :], ACT.Identity, bias=ln[:, 5:6],
                                   scale=ln[:, 4:5]).then_inc(z_done, 1)

            def tile(T, more):
                for c in range(1, NC):
                    split(T, c)
                root(T, 0)
                norm(T, 0)
                root(T, 1)
                if more:
                    split(T + 1, 0)
                norm(T, 1)

            split(0, 0)
            tiles(act, tile)

        @block.tensor
        def _(pe):
            def three(o, stat, mov, first, last):
                for n, (a, m) in enumerate(((0, 0), (0, 1), (1, 0))):
                    ins = pe.matmul(o, stat[a], mov[m], start=(first and n == 0), stop=(last and n == 2))
                return ins

            def up(T, c, b):
                pe.wait_ge(up_free, 1 + T * NC + max(c - 2, 0))
                for k in range(KT):
                    if c < CI:
                        piece, col = UP_0 + 2 * k + c // 8, c % 8 * P
                    else:
                        piece, col = W1_0 + k // 2, k % 2 * LAT + (c - CI) * P
                    stat = [W[:, piece, a * L + col:a * L + col + P] for a in range(2)]
                    mov = [hid[:, b, :, a, k, :] for a in range(2)]
                    ins = three(slot_of(c), stat, mov, k == 0, k == KT - 1)
                ins.then_inc(up_done, 1)

            def down(T, c):
                pe.wait_ge(h_lo, T * NC + c + 1)
                piece = DN_0 + c if c < CI else FC2_0 + c - CI
                for s in range(2):
                    for k in range(2):
                        stat = [h_hl[:, c % HR, a, s * P:s * P + P] for a in range(2)]
                        mov = [W[:, piece, a * L + k * 512:a * L + k * 512 + 512] for a in range(2)]
                        ins = three(acc[:, s, k, :], stat, mov, c == 0, c == NC - 1)
                    if c == NC - 1 and s == 0:
                        ins.then_inc(acc_done, 1)
                ins.then_inc(down_done, 1)

            def gate_logits(T, b):
                pe.wait_ge(diag_ready, 1 + T)
                for s in range(2):
                    for k in range(KT):
                        for a in ((0, 1) if k == 0 else (1, 0)):
                            w = NE if a else 2 * NE
                            ins = pe.matmul(gate_ps[:, s, 0:w], hid[:, b, s, a, k, :], gate[:, k, 0:w],
                                            start=(k == a == 0), stop=(k == KT - 1 and a == 0), skip_group_check=bool(a))
                ins.then_inc(gate_done, 1)

            start_at_one(pe, down_done)
            pe.wait_ge(consts, 1)
            pe.wait_ge(nu_ready, 1)
            pe.matmul(nu_ps, nu16, id_bf, start=True, stop=True).then_inc(nu_turned, 1)
            pe.wait_ge(nu_copied, 1)
            with pe.Fori(0, TILES // 2) as i:
                for b in range(2):
                    T = 2 * i + b
                    pe.wait_ge(hid_in[b], 32 * i + 32)
                    gate_logits(T, b)
                    for c in range(NC):
                        up(T, c, b)
                        if c == 4:
                            pe.wait_ge(diag_ready, 1 + T + 1)
                            for s in range(2):
                                ins = pe.matmul(route_ps[:, s, :], ones32[:, :], diag[:, s, :], start=True, stop=True)
                            ins.then_inc(route_done, 1)
                        if c == LAG:
                            pe.wait_ge(z_done, 1 + 4 * T)
                        if c >= LAG:
                            down(T, c - LAG)
                    for c in range(NC - LAG, NC):
                        down(T, c)

        @block.vector
        def _(dve):
            chain = Chain(dve, dve_c)
            link = chain.link

            def tt(o, a, b_, op):
                link(dve.tensor_tensor(o, a, b_, op))

            start_at_one(dve, up_free, diag_ready, z_added)
            root, q = tmp[:, 0:1], tmp[:, 1:2]
            tt(tmp[:, 2:3], s_w1, s_gate, ALU.mult)
            tt(tmp[:, 2:3], tmp[:, 2:3], s_fc2, ALU.mult)
            link(dve.reciprocal(q, tmp[:, 2:3]))
            for factor in (s_up, s_down, s_up):
                tt(q, q, factor, ALU.mult)
            link(dve.tensor_scalar(q, q, 2.0 ** -60, 2.0 ** 60, ALU.max, ALU.min))
            link(dve.reciprocal(tmp[:, 2:3], q))
            link(dve.tensor_scalar(tmp[:, 2:3], tmp[:, 2:3], 1.0, None, ALU.min))
            root_power(dve, link, root, tmp[:, 2:3], 2.0 ** -100)
            link(dve.tensor_scalar(root, root, 2.0 ** -8, None, ALU.mult))
            norm_scale(dve, link, k_route, energy[:, :], 0.5, TINY)
            link(dve.tensor_scalar(nu, k_route, root, None, ALU.mult))
            link(dve.tensor_copy(id_bf, id16[:, :]))
            dve.tensor_copy(nu16, nu).then_inc(nu_ready, 1)
            dve.wait_ge(nu_turned, 1)
            dve.tensor_copy(nu_rows, nu_ps).then_inc(nu_copied, 1)
            tt(theta, theta, nu, ALU.mult)
            tt(theta, theta, theta, ALU.mult)
            for factor in (s_up, s_down, s_up):
                link(dve.tensor_scalar(theta, theta, factor, 2.0 ** 62, ALU.mult, ALU.min))
            link(dve.scalar_tensor_tensor(out=theta, in0=theta, scalar=LN_EPS, in1=theta,
                                          op0=ALU.mult, op1=ALU.mult))
            tt(k_route, nu, nu, ALU.mult)
            link(dve.tensor_scalar(k_route, k_route, q, None, ALU.mult))

            def carry_wait():
                dve.tensor_copy(tmp[0:1, 3:4], tmp[0:1, 2:3])

            def route_weights(T):
                dve.wait_ge(gate_done, T + 1)
                link(dve.tensor_copy(g_lo, gate_ps[:, :, NE:2 * NE]))
                tt(logits, gate_ps[:, :, 0:NE], g_lo, ALU.add)
                carry_wait()
                dve.max(top[:, 0, :], logits[:, 0, :])
                link(dve.max(top[:, 1, :], logits[:, 1, :]))
                tt(s_tok[:, :], top[:, :, 0], top[:, :, 1], ALU.add)
                for s in range(2):
                    link(dve.tensor_scalar(diag[:, s, :], id16[:, :], s_tok[:, s:s + 1], k_route[:, bass.ds(2 * T + s, 1)],
                                           ALU.mult, ALU.mult))
                dve.sem_inc(diag_ready, 1)

            def evacuate(T, c):
                n = T * NC + c
                dve.wait_ge(up_done, n + 1)
                if c < CI:
                    dve.scalar_tensor_tensor(out=r_buf[:, c % 2, :], in0=slot_of(c), scalar=0.0, in1=relu_scale[:, :],
                                             op0=ALU.max, op1=ALU.mult).then_inc(up_free, 1)
                else:
                    dve.tensor_tensor(h32[:, c % 2, :], slot_of(c), route[:, :], ALU.mult).then_inc(up_free, 1)

            def layernorm(T, s):
                if s == 0:
                    dve.wait_ge(acc_done, T + 1)
                else:
                    dve.wait_ge(down_done, 1 + (T + 1) * NC)
                for k in range(2):
                    link(dve.bn_stats(stats[:, k, :], acc[:, s, k, :]))
                carry_wait()
                link(dve.bn_aggr(mv[:, :], stats[:, :, :]))
                dve.tensor_tensor(ln[:, 0:1], mv[:, 1:2], theta[:, bass.ds(2 * T + s, 1)], ALU.add).then_inc(root_asked, 1)
                dve.wait_ge(root_done, 2 * T + s + 1)
                link(dve.reciprocal(ln[:, 2:3], ln[:, 1:2]))
                link(dve.scalar_tensor_tensor(out=ln[:, 3:4], in0=ln[:, 0:1], scalar=ln[:, 2:3], in1=ln[:, 2:3],
                                              op0=ALU.mult, op1=ALU.mult))
                link(dve.tensor_scalar(ln[:, 3:4], ln[:, 3:4], -0.5, 1.5, ALU.mult, ALU.add))
                dve.wait_ge(z_done, 1 + 4 * T + 2 * s)
                tt(ln[:, 4:5], ln[:, 2:3], ln[:, 3:4], ALU.mult)
                dve.scalar_tensor_tensor(out=ln[:, 5:6], in0=mv[:, 0:1], scalar=-1.0, in1=ln[:, 4:5],
                                         op0=ALU.mult, op1=ALU.mult).then_inc(norm_ready, 1)

            def add_z(T, s):
                for k in range(2):
                    n = 4 * T + 2 * s + k
                    dve.wait_ge(z_scaled, n + 1)
                    if k == 0:
                        dve.wait_ge(xb_done, 2 * T + s + 1)
                    cols = xr[:, s, k * 512:k * 512 + 512]
                    dve.tensor_tensor(cols, cols, z[:, k, :], ALU.add).then_inc(z_added, 1)

            def first_chunk(T):
                route_weights(T)
                dve.wait_ge(relu_scale_in, 16 * T + 16)
                evacuate(T, 0)

            def tile(T, more):
                for c in range(2, NC):
                    dve.wait_ge(h_lo, T * NC + c - 1)
                    evacuate(T, c)
                    if c == 5:
                        dve.wait_ge(route_done, T + 1)
                        link(dve.tensor_copy(route[:, :], route_ps[:, :, :].rearrange("p s m -> p (s m)")))
                layernorm(T, 0)
                layernorm(T, 1)
                if more:
                    first_chunk(T + 1)
                add_z(T, 0)
                if more:
                    evacuate(T + 1, 1)
                add_z(T, 1)

            first_chunk(0)
            evacuate(0, 1)
            with dve.Fori(0, TILES // 2 - 1) as i:
                chain.loop(i, 2 * (6 + 2 * 7 + 1))
                for b in range(2):
                    tile(2 * i + b, True)
            chain.end_loop(TILES // 2 - 1)
            tile(TILES - 2, True)
            tile(TILES - 1, False)


_INS = ["x", "itok_B_8_3872", "L0_cond_log_dt", "L0_cond_C", "L0_cond_log_A_real", "L0_cond_A_imag", "L0_cond_D",
        "L0_ffn_gate_w", "L0_ffn_up_w", "L0_ffn_down_w", "L0_ffn_fc1_w", "L0_ffn_fc2_w", "L0_ffn_expert_w",
        "L0_ffn_ln_gamma", "L0_ffn_ln_beta"]


def kernel(**inputs):
    import numpy as np
    import concourse.bacc as bacc
    from concourse.bass_utils import run_bass_kernel_spmd

    nc = bacc.Bacc("TRN2", target_bir_lowering=False, num_devices=1)
    arrays, args = {}, []
    for name in _INS:
        a = np.ascontiguousarray(inputs[name])
        arrays[f"in_{name}"] = a
        args.append(nc.dram_tensor(f"in_{name}", a.shape, mybir.dt.from_np(a.dtype), kind="ExternalInput").ap())
    args.append(nc.dram_tensor("out_0", (B, H, L), F32, kind="ExternalOutput").ap())
    build(nc, *args)
    r = run_bass_kernel_spmd(nc, [arrays], core_ids=[0])
    return r.results[0]["out_0"]
```
